# Optimizing a Trainium2 kernel written in Bass

```python
import numpy as np
import jax
import jax.numpy as jnp

def _softmax(x, axis=-1):
    return jax.nn.softmax(x, axis=axis)

def _gelu(x):
    return jax.nn.gelu(x, approximate=True)

def _silu(x):
    return jax.nn.silu(x)

def _sigmoid(x):
    return jax.nn.sigmoid(x)

def _layernorm(x, axis=-1, eps=1e-05):
    m = jnp.mean(x, axis=axis, keepdims=True)
    v = jnp.var(x, axis=axis, keepdims=True)
    return (x - m) / jnp.sqrt(v + eps)

def _scatter_add(tgt, idx, src, axis=0):
    return tgt.at[idx].add(src)

def _segment_sum(src, seg, n):
    return jax.ops.segment_sum(src, seg, n)
kernel_name = 'mk_seq_preln_d1_jaxref_r8_478d4e'

def setup_inputs(seed: int=0):
    np.random.seed(seed)
    _w = jnp.asarray

    def _L0_attn_setup():
        import jax, jax.numpy as jnp
        import numpy as np
        HQ, HK, DH = (32, 8, 64)
        ROPE_BASE = 10000.0

        def _rope_tables(T, dtype):
            pos = jnp.arange(T, dtype=jnp.float32)
            inv_freq = 1.0 / ROPE_BASE ** (jnp.arange(0, DH, 2, dtype=jnp.float32) / DH)
            freqs = pos[:, None] * inv_freq[None, :]
            cos = jnp.concatenate([jnp.cos(freqs), jnp.cos(freqs)], -1).astype(dtype)
            sin = jnp.concatenate([jnp.sin(freqs), jnp.sin(freqs)], -1).astype(dtype)
            return (cos, sin)

        def _rotate_half(t):
            return jnp.concatenate([-t[..., DH // 2:], t[..., :DH // 2]], -1)
        key = jax.random.key(seed)
        k1, k2, k3, k4 = jax.random.split(key, 4)
        B, T, D = (2, 256, 256)
        std = 0.02 / np.sqrt(24)
        kv_std = std / np.sqrt(HQ / HK)
        return {'x': jax.random.normal(k1, (B, T, D), jnp.float32), 'Wq': jax.random.normal(k2, (D, HQ * DH), jnp.float32) * std, 'Wkv': jax.random.normal(k3, (D, 2 * HK * DH), jnp.float32) * kv_std, 'Wo': jax.random.normal(k4, (HQ * DH, D), jnp.float32) * std}
    _L0_attn_in = _L0_attn_setup()

    def _L0_ffn_setup():
        import jax, jax.numpy as jnp
        import numpy as np
        B, S, H = (4, 128, 256)
        E, K, I, SI = (16, 4, 176, 704)

        def _silu_mul(gu, inter):
            return jax.nn.silu(gu[:, :inter]) * gu[:, inter:]
        key = jax.random.key(seed)
        ks = jax.random.split(key, 7)
        s = 0.02
        return {'hidden_states': jax.random.normal(ks[0], (B, S, H), jnp.float32), 'gate_w': jax.random.normal(ks[1], (E, H), jnp.float32) * s, 'expert_gate_up': jax.random.normal(ks[2], (E, 2 * I, H), jnp.float32) * s, 'expert_down': jax.random.normal(ks[3], (E, H, I), jnp.float32) * s, 'shared_gate_up': jax.random.normal(ks[4], (2 * SI, H), jnp.float32) * s, 'shared_down': jax.random.normal(ks[5], (H, SI), jnp.float32) * s, 'shared_gate_vec': jax.random.normal(ks[6], (1, H), jnp.float32) * s}
    _L0_ffn_in = _L0_ffn_setup()
    _d = {'L0_attn_x': _L0_attn_in['x'], 'L0_attn_Wq': _L0_attn_in['Wq'], 'L0_attn_Wkv': _L0_attn_in['Wkv'], 'L0_attn_Wo': _L0_attn_in['Wo'], 'L0_ffn_gate_w': _L0_ffn_in['gate_w'], 'L0_ffn_expert_gate_up': _L0_ffn_in['expert_gate_up'], 'L0_ffn_expert_down': _L0_ffn_in['expert_down'], 'L0_ffn_shared_gate_up': _L0_ffn_in['shared_gate_up'], 'L0_ffn_shared_down': _L0_ffn_in['shared_down'], 'L0_ffn_shared_gate_vec': _L0_ffn_in['shared_gate_vec']}
    _x0 = _d['L0_attn_x']
    _d['L0_attn_x'] = jax.random.normal(jax.random.fold_in(jax.random.key(seed), 1), (16, 256, 256), dtype=_x0.dtype)
    del _x0
    return _d

def reference(L0_attn_x, L0_attn_Wq, L0_attn_Wkv, L0_attn_Wo, L0_ffn_gate_w, L0_ffn_expert_gate_up, L0_ffn_expert_down, L0_ffn_shared_gate_up, L0_ffn_shared_down, L0_ffn_shared_gate_vec):

    def _L0_attn_ref(x, Wq, Wkv, Wo):
        import jax, jax.numpy as jnp
        import numpy as np
        HQ, HK, DH = (32, 8, 64)
        ROPE_BASE = 10000.0

        def _rope_tables(T, dtype):
            pos = jnp.arange(T, dtype=jnp.float32)
            inv_freq = 1.0 / ROPE_BASE ** (jnp.arange(0, DH, 2, dtype=jnp.float32) / DH)
            freqs = pos[:, None] * inv_freq[None, :]
            cos = jnp.concatenate([jnp.cos(freqs), jnp.cos(freqs)], -1).astype(dtype)
            sin = jnp.concatenate([jnp.sin(freqs), jnp.sin(freqs)], -1).astype(dtype)
            return (cos, sin)

        def _rotate_half(t):
            return jnp.concatenate([-t[..., DH // 2:], t[..., :DH // 2]], -1)
        B, T, D = x.shape
        g = HQ // HK
        scale = DH ** (-0.5)
        q = (x @ Wq).reshape(B, T, HQ, DH).transpose(0, 2, 1, 3)
        kv = (x @ Wkv).reshape(B, T, 2, HK, DH)
        k = kv[:, :, 0].transpose(0, 2, 1, 3)
        v = kv[:, :, 1].transpose(0, 2, 1, 3)
        k = jnp.repeat(k, g, axis=1)
        v = jnp.repeat(v, g, axis=1)
        cos, sin = _rope_tables(T, x.dtype)
        q = q * cos + _rotate_half(q) * sin
        k = k * cos + _rotate_half(k) * sin
        scores = jnp.einsum('bhqd,bhkd->bhqk', q, k) * scale
        causal = jnp.triu(jnp.ones((T, T), bool), 1)
        scores = jnp.where(causal, -jnp.inf, scores)
        attn = jax.nn.softmax(scores.astype(jnp.float32), axis=-1).astype(x.dtype)
        out = jnp.einsum('bhqk,bhkd->bhqd', attn, v)
        out = out.transpose(0, 2, 1, 3).reshape(B, T, HQ * DH)
        return out @ Wo

    def _L0_ffn_ref(hidden_states, gate_w, expert_gate_up, expert_down, shared_gate_up, shared_down, shared_gate_vec):
        import jax, jax.numpy as jnp
        import numpy as np
        B, S, H = (4, 128, 256)
        E, K, I, SI = (16, 4, 176, 704)

        def _silu_mul(gu, inter):
            return jax.nn.silu(gu[:, :inter]) * gu[:, inter:]
        orig_shape = hidden_states.shape
        x = hidden_states.reshape(-1, H)
        router_logits = x @ gate_w.T
        routing_probs = jax.nn.softmax(router_logits.astype(jnp.float32), axis=-1)
        topk_w, topk_idx = jax.lax.top_k(routing_probs, K)
        topk_w = topk_w / topk_w.sum(axis=-1, keepdims=True)
        topk_w = topk_w.astype(x.dtype)
        combine = (jax.nn.one_hot(topk_idx, E, dtype=x.dtype) * topk_w[..., None]).sum(1)
        shared = _silu_mul(x @ shared_gate_up.T, SI) @ shared_down.T
        shared = shared * jax.nn.sigmoid(x @ shared_gate_vec.T)

        def step(acc, ew):
            w_gu, w_d, cw = ew
            h = _silu_mul(x @ w_gu.T, I)
            return (acc + h @ w_d.T * cw[:, None], None)
        acc0 = jnp.zeros_like(x)
        sparse, _ = jax.lax.scan(step, acc0, (expert_gate_up, expert_down, combine.T))
        return (shared + sparse).reshape(orig_shape)
    x = L0_attn_x
    x = x + _L0_attn_ref(_layernorm(x, axis=-1), L0_attn_Wq, L0_attn_Wkv, L0_attn_Wo)
    x = x + _L0_ffn_ref(_layernorm(x, axis=-1), L0_ffn_gate_w, L0_ffn_expert_gate_up, L0_ffn_expert_down, L0_ffn_shared_gate_up, L0_ffn_shared_down, L0_ffn_shared_gate_vec)
    return x

_drawn_inputs = setup_inputs


def setup_inputs(seed=0):
    import zlib

    import numpy as np

    out = dict(_drawn_inputs(seed))
    spreads = {}
    factors = {'L0_attn_Wq': 8.0,
     'L0_attn_Wkv': 8.0,
     'L0_attn_Wo': 8.0,
     'L0_ffn_gate_w': 8.0,
     'L0_ffn_expert_gate_up': 7.943,
     'L0_ffn_expert_down': 7.922,
     'L0_ffn_shared_gate_up': 3.994,
     'L0_ffn_shared_down': 3.982,
     'L0_ffn_shared_gate_vec': 8.0}
    for name, (base, spread) in spreads.items():
        noise = np.random.default_rng([zlib.crc32(name.encode()), seed]).standard_normal(out[name].shape)
        drawn = base * np.exp(spread * noise) if base else spread * noise
        out[name] = jnp.asarray(drawn.astype(out[name].dtype))
    for name, factor in factors.items():
        out[name] = (out[name] * factor).astype(out[name].dtype)
    return out
```

```python
import concourse.bass as bass
from concourse import mybir
from contextlib import ExitStack


def attention_block(nc, x, w_q, w_kv, w_o, rope, x1_dram, n_seq):
    fp32, fp16, bf16 = mybir.dt.float32, mybir.dt.float16, mybir.dt.bfloat16
    ALU, ACT, AX = mybir.AluOpType, mybir.ActivationFunctionType, mybir.AxisListType

    P = 128
    SEQ, D = x.shape[1], x.shape[2]
    DH = rope.shape[2]
    HALF = DH // 2
    TT = SEQ // P
    DB = D // P
    HQ = w_q.shape[1] // DH
    HK = w_kv.shape[1] // DH // 2
    G = HQ // HK
    KVS = 2
    QS = KVS * G
    STEPS = HK // KVS
    RH = QS + KVS
    NQ, NKV = QS * DH, 2 * KVS * DH
    UNITS = 6
    KT = STEPS * G

    X_SCALE, W_SCALE, QK_SCALE, O_SCALE = 2.0 ** 5, 2.0 ** 9, 2.0 ** 6, 2.0 ** 6
    ROPE_SCALE = QK_SCALE / (X_SCALE * W_SCALE)
    V_SCALE = O_SCALE / (X_SCALE * W_SCALE)
    SOFTMAX_SCALE = DH ** -0.5 / (QK_SCALE * QK_SCALE)
    OUT_SCALE = 1.0 / (O_SCALE * W_SCALE)
    EPS = 1e-5
    MASKED = -1e30
    assert rope.shape[1] == 2 and ROPE_SCALE == 2.0 ** -8

    ctx = ExitStack()
    with ctx:
        def sb(name, shape, dt):
            return ctx.enter_context(nc.sbuf_tensor(name, shape, dt))

        def pb(name):
            return ctx.enter_context(nc.psum_tensor(name, [P, 512], fp32))

        def sem(name):
            return ctx.enter_context(nc.semaphore(name))

        wq_stage = sb("wq_stage", [P, DB, HQ * DH], fp32)
        wkv_stage = sb("wkv_stage", [P, DB, 2 * HK * DH], fp32)
        wo_stage = sb("wo_stage", [P, KT, D], fp32)
        wq_hi, wq_lo = sb("wq_hi", [P, DB, HQ * DH], fp16), sb("wq_lo", [P, DB, HQ * DH], fp16)
        wkv_hi, wkv_lo = sb("wkv_hi", [P, DB, 2 * HK * DH], fp16), sb("wkv_lo", [P, DB, 2 * HK * DH], fp16)
        wo_hi, wo_lo = sb("wo_hi", [P, KT, D], fp16), sb("wo_lo", [P, KT, D], fp16)
        table = sb("table", [P, TT, 2, DH], fp32)
        ident32 = sb("ident32", [P, P], fp32)
        ident16 = sb("ident16", [P, P], fp16)
        identb = sb("identb", [P, P], bf16)
        causal = sb("causal", [P, 4, P], bf16)
        x_in = sb("x_in", [P, TT, D], fp32)
        x_res = sb("x_res", [P, TT, D], fp32)
        x_out = sb("x_out", [P, TT, D], fp32)
        stats = sb("stats", [P, TT, 6], fp32)
        moments = sb("moments", [P, TT, 2], fp32)
        eps = sb("eps", [P, 1], fp32)
        scale_tile = sb("scale_tile", [P, G], fp32)
        log_var, rough = sb("log_var", [P, TT], fp32), sb("rough", [P, TT], fp32)
        correction, rstd = sb("correction", [P, TT], fp32), sb("rstd", [P, TT], fp32)
        xn = sb("xn", [P, TT, D], fp32)
        xn_hi, xn_lo = sb("xn_hi", [P, TT, D], fp16), sb("xn_lo", [P, TT, D], fp16)
        xn_t = sb("xn_t", [P, TT, 2, DB, P], fp16)
        products = sb("products", [P, TT, 2, RH * DH], fp32)
        rotated = sb("rotated", [P, TT, RH * DH], fp32)
        stacked = sb("stacked", [P, TT, RH + KVS, 2, DH], fp16)
        q_t = sb("q_t", [P, 2, TT, QS, P], fp16)
        k_t = sb("k_t", [P, 2, 2, KVS, TT, P], fp16)
        values = sb("values", [P, 2, TT, KVS * DH], fp32)
        negmax = sb("negmax", [P, 3, G], fp32)
        bias = sb("bias", [P, 3, G], fp32)
        sums = sb("sums", [P, 3, G], fp32)
        inverse = sb("inverse", [P, 3, G], fp32)
        probs = sb("probs", [P, 3, 512], fp32)
        pt0 = sb("pt0", [P, KVS, G, P], fp32)
        pt1 = sb("pt1", [P, KVS, TT, G, P], fp32)
        o_hi, o_lo = sb("o_hi", [P, STEPS, G, SEQ], fp16), sb("o_lo", [P, STEPS, G, SEQ], fp16)

        scores = [pb(f"scores{i}") for i in range(3)]
        proj = ctx.enter_context(nc.psum_tensor("proj", [P, 1024], fp32))
        ring = [pb("ring0"), pb("ring1")]
        heads_out = pb("heads_out")

        s_wq, s_wkv, s_wo, s_table = sem("s_wq"), sem("s_wkv"), sem("s_wo"), sem("s_table")
        s_const = sem("s_const")
        s_w_hi, s_w_lo = sem("s_w_hi"), sem("s_w_lo")
        s_x, s_res, s_stored = sem("s_x"), sem("s_res"), sem("s_stored")
        s_stat, s_moments, s_rstd = sem("s_stat"), sem("s_moments"), sem("s_rstd")
        s_eps, s_rough = sem("s_eps"), sem("s_rough")
        s_passed = sem("s_passed")
        s_xn, s_xn_hi, s_xn_lo = sem("s_xn"), sem("s_xn_hi"), sem("s_xn_lo")
        s_proj, s_mult, s_vals = sem("s_proj"), sem("s_mult"), sem("s_vals")
        s_rot, s_hi, s_lo, s_swap = sem("s_rot"), sem("s_hi"), sem("s_lo"), sem("s_swap")
        s_full = [sem("s_full0"), sem("s_full1")]
        s_free = [sem("s_free0"), sem("s_free1")]
        s_scores, s_max, s_bias = sem("s_scores"), sem("s_max"), sem("s_bias")
        s_exp, s_recip, s_norm = sem("s_exp"), sem("s_recip"), sem("s_norm")
        s_heads, s_o_hi, s_o_lo = sem("s_heads"), sem("s_o_hi"), sem("s_o_lo")
        s_wo_mm, s_x1 = sem("s_wo_mm"), sem("s_x1")

        unit = [(0, 0, 0, G, P), (1, 0, 0, G, P)] + \
               [(j, 1, 2 * h, 2, SEQ) for j in range(KVS) for h in range(2)]

        LN_STEP = STEPS - 2

        def ring_order(last):
            uses = []
            for p in range(STEPS):
                more = not (last and p == STEPS - 1)
                uses += [(p, n) for n in ["P0", "P1"] + (["L0", "L1"] if p == LN_STEP and not last else [])
                         + ["P2"] + (["T0", "P3", "T1", "T2"] if more else ["P3"]) + ["P4", "P5"]]
            return uses

        RING_FIRST = ["L0", "L1", "T0", "T1", "T2"]
        RING_USES, RING_LAST = ring_order(False), ring_order(True)
        PER_BANK = len(RING_USES) // 2
        assert len(RING_USES) % 2 == 0

        def ring_use(b, p, name, back=0):
            if p < 0:
                i = RING_FIRST.index(name)
                return i % 2, i // 2 + 1
            uses = RING_LAST if isinstance(b, int) and b - back == n_seq - 1 else RING_USES
            i = uses.index((p, name))
            before = (len(RING_FIRST) + 1 - i % 2) // 2
            return i % 2, b * PER_BANK + (before + i // 2 + 1 - back * PER_BANK)

        def filled(eng, b, p, name):
            bank, n = ring_use(b, p, name)
            eng.wait_ge(s_full[bank], n)
            return ring[bank], s_free[bank]

        def emptied(eng, b, p, name, back=0):
            bank, n = ring_use(b, p, name, back)
            eng.wait_ge(s_free[bank], n)

        def previous_ring_use(pe, b, p, name):
            bank, n = ring_use(b, p, name)
            if not isinstance(n, int) or n > 1:
                pe.wait_ge(s_free[bank], n - 1)
            return ring[bank], s_full[bank]

        def per_step(b, p, each, n):
            return b * (STEPS * each) + (p * each + n)

        block = ctx.enter_context(nc.Block(name="attention"))

        @block.sync
        def _(sp):
            sp.dma_start(wq_stage[:], w_q.rearrange("(c p) n -> p c n", p=P)).then_inc(s_wq, 16)
            sp.dma_start(x_in[:], x[0].rearrange("(t p) d -> p t d", p=P)).then_inc(s_x, 16)
            sp.dma_start(wkv_stage[:], w_kv.rearrange("(c p) n -> p c n", p=P)).then_inc(s_wkv, 16)
            sp.dma_start(table[:], rope.rearrange("(t p) c d -> p t c d", p=P)).then_inc(s_table, 16)
            wo_rows = w_o.rearrange("(s j g d) n -> j s d g n", j=KVS, g=G, d=DH)
            for j in range(KVS):
                for s in range(STEPS):
                    sp.dma_start(wo_stage[j * DH:(j + 1) * DH, s * G:(s + 1) * G, :],
                                 wo_rows[j, s]).then_inc(s_wo, 16)

            sp.dma_start(x_res[:], x[0].rearrange("(t p) d -> p t d", p=P)).then_inc(s_res, 16)

            def store(b, count):
                sp.wait_ge(s_x1, count)
                sp.dma_start(x1_dram[b].rearrange("(t p) d -> p t d", p=P), x_out[:]).then_inc(s_stored, 16)

            def load_next(b):
                sp.wait_ge(s_xn, b + 1)
                sp.dma_start(x_in[:], x[b + 1].rearrange("(t p) d -> p t d", p=P)).then_inc(s_x, 16)

            def load_residual(b):
                sp.dma_start(x_res[:], x[b].rearrange("(t p) d -> p t d", p=P)).then_inc(s_res, 16)

            if n_seq > 1:
                load_next(0)
            if n_seq > 2:
                with sp.Fori(1, n_seq - 1) as b:
                    load_next(b)
                    store(b - 1, b)
                    load_residual(b)
            if n_seq > 1:
                store(n_seq - 2, n_seq - 1)
                load_residual(n_seq - 1)
            store(n_seq - 1, n_seq)
            sp.wait_ge(s_stored, 16 * n_seq)

        @block.gpsimd
        def _(pool):
            pool.memset(eps[:], EPS).then_inc(s_eps, 1)
            pool.memset(scale_tile[:], SOFTMAX_SCALE).then_inc(s_eps, 1)
            pool.wait_ge(s_eps, 2)
            for m in (ident32, ident16, identb, causal):
                pool.memset(m[:], 0.0).then_inc(s_const, 1)
            pool.wait_ge(s_const, 4)
            for m in (ident32, ident16, identb):
                pool.affine_select(out=m[:], in_=m[:], compare_op=ALU.not_equal, fill=1.0, base=0,
                                   pattern=[[-1, P]], channel_multiplier=1).then_inc(s_const, 1)
            pool.affine_select(out=causal[:], in_=causal[:], compare_op=ALU.is_ge, fill=MASKED, base=0,
                               pattern=[[0, 4], [-1, P]], channel_multiplier=1).then_inc(s_const, 1)

            def rotate(b, p, t):
                pool.wait_ge(s_mult, per_step(b, p, TT, t + 1))
                halves = products[:, t].rearrange("p c (h a d) -> p c h a d", a=2, d=HALF)
                out = rotated[:, t].rearrange("p (h a d) -> p h a d", a=2, d=HALF)
                for a in range(2):
                    pool.tensor_tensor(out[:, :, a], halves[:, 0, :, a], halves[:, 1, :, 1 - a],
                                       ALU.add).then_inc(s_rot, 1)

            def low_parts(b, p, t):
                pool.wait_ge(s_hi, per_step(b, p, TT, t + 1))
                pool.wait_ge(s_rot, per_step(b, p, 2 * TT, 2 * t + 2))
                whole = rotated[:, t].rearrange("p (h d) -> p h d", d=DH)
                pool.tensor_tensor(stacked[:, t, 0:RH, 1], whole, stacked[:, t, 0:RH, 0],
                                   ALU.subtract).then_inc(s_lo, 1)

            def make_bias(b, p, u):
                pool.wait_ge(s_max, per_step(b, p, UNITS, u + 1))
                heads = unit[u][3]
                pool.tensor_tensor(bias[:, u % 3, 0:heads], negmax[:, u % 3, 0:heads], scale_tile[:, 0:heads],
                                   ALU.mult).then_inc(s_bias, 1)

            def normalize(b, p, u):
                pool.wait_ge(s_recip, per_step(b, p, UNITS, u + 1))
                heads, keys = unit[u][3:]
                pr = probs[:, u % 3].rearrange("p (h k) -> p h k", k=keys)
                pool.tensor_tensor(pr, pr, inverse[:, u % 3, 0:heads].unsqueeze(2).broadcast_to(
                    [P, heads, keys]), ALU.mult).then_inc(s_norm, 1)

            def step(b, p, last):
                more = not (last and p + 1 == STEPS)
                normalize(b, p, 0)
                normalize(b, p, 1)
                if more:
                    rotate(b, p + 1, 0)
                make_bias(b, p, 3)
                normalize(b, p, 2)
                make_bias(b, p, 4)
                if more:
                    low_parts(b, p + 1, 0)
                    rotate(b, p + 1, 1)
                normalize(b, p, 3)
                make_bias(b, p, 5)
                if more:
                    low_parts(b, p + 1, 1)
                normalize(b, p, 4)
                if more:
                    make_bias(b, p + 1, 0)
                normalize(b, p, 5)
                if more:
                    make_bias(b, p + 1, 1)
                    make_bias(b, p + 1, 2)

            for t in range(TT):
                rotate(0, 0, t)
                low_parts(0, 0, t)
            for u in range(3):
                make_bias(0, 0, u)
            if n_seq > 1:
                with pool.Fori(0, n_seq - 1) as b:
                    for p in range(STEPS):
                        step(b, p, False)
            for p in range(STEPS):
                step(n_seq - 1, p, True)

        @block.scalar
        def _(act):
            def rough_rstd(b):
                act.wait_ge(s_moments, TT * b + TT)
                act.activation(log_var[:], moments[:, :, 1], ACT.Ln, bias=eps[:]).then_inc(s_rough, 1)
                act.wait_ge(s_rough, 2 * b + 1)
                act.activation(rough[:], log_var[:], ACT.Exp, scale=-0.5).then_inc(s_rough, 1)

            def high_xn(b):
                act.wait_ge(s_xn, b + 1)
                act.activation(xn_hi[:], xn[:], ACT.Copy, scale=X_SCALE).then_inc(s_xn_hi, 1)

            act.preload_act_table_set("natural_log_exp_and_others")
            act.wait_ge(s_eps, 1)
            rough_rstd(0)
            high_xn(0)
            act.wait_ge(s_wq, 16)
            act.activation(wq_hi[:], wq_stage[:], ACT.Copy, scale=W_SCALE).then_inc(s_w_hi, 1)
            act.wait_ge(s_wkv, 16)
            act.activation(wkv_hi[:], wkv_stage[:], ACT.Copy, scale=W_SCALE).then_inc(s_w_hi, 1)
            act.wait_ge(s_wo, 16 * KVS * STEPS)
            act.activation(wo_hi[:], wo_stage[:], ACT.Copy, scale=W_SCALE).then_inc(s_w_hi, 1)

            def copy_values(b, p, t):
                act.wait_ge(s_mult, per_step(b, p, TT, t + 1))
                act.activation(values[:, p % 2, t], proj[:, NQ + KVS * DH:NQ + NKV], ACT.Copy,
                               scale=V_SCALE).then_inc(s_vals, 1)

            def exps(b, p, u):
                act.wait_ge(s_bias, per_step(b, p, UNITS, u + 1))
                heads, keys = unit[u][3:]
                for h in range(heads):
                    last = act.activation(probs[:, u % 3, h * keys:(h + 1) * keys],
                                          scores[u % 3][:, h * keys:(h + 1) * keys], ACT.Exp,
                                          bias=bias[:, u % 3, h:h + 1], scale=SOFTMAX_SCALE,
                                          accum_out=sums[:, u % 3, h:h + 1])
                last.then_inc(s_exp, 1)

            def copy_ln(b, p, t):
                bank, free = filled(act, b, p, f"L{t}")
                act.activation(xn_t[:, t].rearrange("p s c n -> p (s c n)"),
                               bank[:, :].bitcast(fp16)[:, 0:2 * D], ACT.Copy).then_inc(free, 1)

            def copy_p0(b, p, u):
                bank, free = filled(act, b, p, f"P{u}")
                act.activation(pt0[:, u].rearrange("p g n -> p (g n)"), bank[:, :], ACT.Copy).then_inc(free, 1)

            def copy_p1(b, p, u):
                j, _, h, _, _ = unit[u]
                bank, free = filled(act, b, p, f"P{u}")
                act.activation(pt1[:, j, :, h:h + 2, :], bank[:, :].rearrange("p (t g n) -> p t g n", t=TT, g=2),
                               ACT.Copy).then_inc(free, 1)

            def copy_k_t(b, p):
                bank, free = filled(act, b, p, "T2")
                act.activation(k_t[:, (p + 1) % 2].rearrange("p a j t n -> p (a j t n)"),
                               bank[:, :].bitcast(fp16), ACT.Copy).then_inc(free, 1)

            def heads_hi(b, p, t):
                act.wait_ge(s_heads, per_step(b, p, TT, t + 1))
                act.activation(o_hi[:, p, :, t * P:(t + 1) * P],
                               heads_out[:, :].rearrange("p (g n) -> p g n", g=G), ACT.Copy).then_inc(s_o_hi, 1)

            def step(b, p, last):
                more = not (last and p + 1 == STEPS)
                if more:
                    copy_values(b, p + 1, 0)
                exps(b, p, 3)
                if p == 0 and not last:
                    rough_rstd(b + 1)
                copy_p0(b, p, 1)
                if p == 1 and not last:
                    high_xn(b + 1)
                if more:
                    copy_values(b, p + 1, 1)
                exps(b, p, 4)
                heads_hi(b, p, 0)
                if p == LN_STEP and not last:
                    copy_ln(b, p, 0)
                    copy_ln(b, p, 1)
                exps(b, p, 5)
                copy_p1(b, p, 3)
                if more:
                    copy_k_t(b, p)
                    exps(b, p + 1, 0)
                    exps(b, p + 1, 1)
                copy_p1(b, p, 5)
                if more:
                    exps(b, p + 1, 2)
                heads_hi(b, p, 1)

            for t in range(TT):
                copy_ln(0, -1, t)
            for t in range(TT):
                copy_values(0, 0, t)
            copy_k_t(0, -1)
            for u in range(3):
                exps(0, 0, u)
            if n_seq > 1:
                with act.Fori(0, n_seq - 1) as b:
                    for p in range(STEPS):
                        step(b, p, False)
            for p in range(STEPS):
                step(n_seq - 1, p, True)

        @block.vector
        def _(dve):
            def norm_moments(b):
                dve.wait_ge(s_x, 16 * b + 16)
                for t in range(TT):
                    dve.bn_stats(stats[:, t], x_in[:, t]).then_inc(s_stat, 1)
                dve.wait_ge(s_stat, TT * b + TT)
                dve.sem_inc(s_passed, 1)
                for t in range(TT):
                    dve.bn_aggr(moments[:, t], stats[:, t]).then_inc(s_moments, 1)

            def norm_apply(b):
                dve.wait_ge(s_rough, 2 * b + 2)
                dve.tensor_tensor(correction[:], rough[:], rough[:], ALU.mult).then_inc(s_rstd, 1)
                dve.wait_ge(s_rstd, 4 * b + 1)
                dve.scalar_tensor_tensor(correction[:], moments[:, :, 1], EPS, correction[:], ALU.add,
                                         ALU.mult).then_inc(s_rstd, 1)
                dve.wait_ge(s_rstd, 4 * b + 2)
                dve.tensor_scalar(correction[:], correction[:], -0.5, 1.5, ALU.mult, ALU.add).then_inc(s_rstd, 1)
                dve.wait_ge(s_rstd, 4 * b + 3)
                dve.tensor_tensor(rstd[:], rough[:], correction[:], ALU.mult).then_inc(s_rstd, 1)
                dve.wait_ge(s_rstd, 4 * b + 4)
                for t in range(TT):
                    last = dve.tensor_scalar(xn[:, t], x_in[:, t], moments[:, t, 0:1], rstd[:, t:t + 1],
                                             ALU.subtract, ALU.mult)
                last.then_inc(s_xn, 1)

            def low_xn(b):
                dve.wait_ge(s_xn_hi, b + 1)
                dve.scalar_tensor_tensor(xn_lo[:], xn[:], X_SCALE, xn_hi[:], ALU.mult, ALU.subtract).then_inc(s_xn_lo, 1)

            dve.wait_ge(s_table, 16)
            norm_moments(0)
            norm_apply(0)
            low_xn(0)
            dve.wait_ge(s_w_hi, 1)
            dve.scalar_tensor_tensor(wq_lo[:], wq_stage[:], W_SCALE, wq_hi[:], ALU.mult, ALU.subtract).then_inc(s_w_lo, 1)
            dve.wait_ge(s_w_hi, 2)
            dve.scalar_tensor_tensor(wkv_lo[:], wkv_stage[:], W_SCALE, wkv_hi[:], ALU.mult, ALU.subtract).then_inc(s_w_lo, 1)
            dve.wait_ge(s_w_hi, 3)
            dve.scalar_tensor_tensor(wo_lo[:], wo_stage[:], W_SCALE, wo_hi[:], ALU.mult, ALU.subtract).then_inc(s_w_lo, 1)
            dve.wait_ge(s_table, 16)

            def multiply(b, p, t):
                dve.wait_ge(s_proj, per_step(b, p, TT, t + 1))
                heads = proj[:, 0:RH * DH].rearrange("p (h d) -> p h d", d=DH)
                for c in range(2):
                    last = dve.tensor_tensor(products[:, t, c].rearrange("p (h d) -> p h d", d=DH), heads,
                                             table[:, t, c].unsqueeze(1).broadcast_to([P, RH, DH]), ALU.mult)
                last.then_inc(s_mult, 1)

            def high_parts(b, p, t):
                dve.wait_ge(s_rot, per_step(b, p, 2 * TT, 2 * t + 2))
                dve.tensor_copy(stacked[:, t, 0:RH, 0], rotated[:, t].rearrange("p (h d) -> p h d", d=DH))\
                    .then_inc(s_hi, 1)

            def swapped_keys(b, p, t):
                dve.wait_ge(s_lo, per_step(b, p, TT, t + 1))
                for a in range(2):
                    last = dve.tensor_copy(stacked[:, t, RH:RH + KVS, a], stacked[:, t, QS:RH, 1 - a])
                last.then_inc(s_swap, 1)

            def maxima(b, p, u):
                dve.wait_ge(s_scores, per_step(b, p, UNITS, u + 1))
                heads, keys = unit[u][3:]
                dve.tensor_reduce(negmax[:, u % 3, 0:heads], scores[u % 3][:, :].rearrange(
                    "p (h k) -> p h k", k=keys), AX.X, ALU.max, negate=True).then_inc(s_max, 1)

            def recips(b, p, u):
                dve.wait_ge(s_exp, per_step(b, p, UNITS, u + 1))
                heads = unit[u][3]
                dve.reciprocal(inverse[:, u % 3, 0:heads], sums[:, u % 3, 0:heads]).then_inc(s_recip, 1)

            def copy_p0(b, p, u):
                bank, free = filled(dve, b, p, f"P{u}")
                dve.tensor_copy(pt0[:, u].rearrange("p g n -> p (g n)"), bank[:, :]).then_inc(free, 1)

            def copy_p1(b, p, u):
                j, _, h, _, _ = unit[u]
                bank, free = filled(dve, b, p, f"P{u}")
                dve.tensor_copy(pt1[:, j, :, h:h + 2, :], bank[:, :].rearrange("p (t g n) -> p t g n", t=TT, g=2))\
                    .then_inc(free, 1)

            def copy_q_t(b, p, t):
                bank, free = filled(dve, b, p, f"T{t}")
                dve.tensor_copy(q_t[:, (p + 1) % 2, t].rearrange("p h n -> p (h n)"),
                                bank[:, :].bitcast(fp16)).then_inc(free, 1)

            def heads_lo(b, p, t):
                dve.wait_ge(s_o_hi, per_step(b, p, TT, t + 1))
                dve.tensor_tensor(o_lo[:, p, :, t * P:(t + 1) * P],
                                  heads_out[:, :].rearrange("p (g n) -> p g n", g=G),
                                  o_hi[:, p, :, t * P:(t + 1) * P], ALU.subtract).then_inc(s_o_lo, 1)

            def residual(b):
                dve.wait_ge(s_wo_mm, b + 1)
                dve.wait_ge(s_res, 16 * b + 16)
                if not (isinstance(b, int) and b == 0):
                    dve.wait_ge(s_stored, 16 * b)
                dve.scalar_tensor_tensor(x_out[:].rearrange("p t d -> p (t d)"), heads_out[:, :], OUT_SCALE,
                                         x_res[:].rearrange("p t d -> p (t d)"), ALU.mult, ALU.add)\
                    .then_inc(s_x1, 1)

            def step(b, p, last, after):
                more = not (last and p + 1 == STEPS)
                if p == 0 and not last:
                    norm_moments(b + 1)
                recips(b, p, 0)
                recips(b, p, 1)
                if more:
                    multiply(b, p + 1, 0)
                recips(b, p, 2)
                copy_p0(b, p, 0)
                maxima(b, p, 3)
                if more:
                    multiply(b, p + 1, 1)
                    high_parts(b, p + 1, 0)
                maxima(b, p, 4)
                recips(b, p, 3)
                if p == 0 and after:
                    residual(b - 1)
                if more:
                    swapped_keys(b, p + 1, 0)
                    high_parts(b, p + 1, 1)
                heads_lo(b, p, 0)
                if p == 1 and not last:
                    low_xn(b + 1)
                copy_p1(b, p, 2)
                maxima(b, p, 5)
                recips(b, p, 4)
                if more:
                    copy_q_t(b, p, 0)
                    swapped_keys(b, p + 1, 1)
                    copy_q_t(b, p, 1)
                recips(b, p, 5)
                if more:
                    maxima(b, p + 1, 0)
                copy_p1(b, p, 4)
                if more:
                    maxima(b, p + 1, 1)
                    maxima(b, p + 1, 2)
                heads_lo(b, p, 1)
                if p == 0 and not last:
                    norm_apply(b + 1)

            for t in range(TT):
                multiply(0, 0, t)
                high_parts(0, 0, t)
                swapped_keys(0, 0, t)
                copy_q_t(0, -1, t)
            for u in range(3):
                maxima(0, 0, u)
            for p in range(STEPS):
                step(0, p, n_seq == 1, False)
            if n_seq > 2:
                with dve.Fori(1, n_seq - 1) as b:
                    for p in range(STEPS):
                        step(b, p, False, True)
            if n_seq > 1:
                for p in range(STEPS):
                    step(n_seq - 1, p, True, True)
            residual(n_seq - 1)

        @block.tensor
        def _(pe):
            def norm_transposes(b, p, source, t):
                pe.wait_ge(s_xn_lo, source + 1)
                bank, full = previous_ring_use(pe, b, p, f"L{t}")
                out = bank[:, :].bitcast(fp16)
                for s, part in enumerate((xn_hi, xn_lo)):
                    for c in range(DB):
                        i = s * DB + c
                        last = pe.transpose(out[:, i * P:(i + 1) * P], part[:, t, c * P:(c + 1) * P], ident16[:])
                last.then_inc(full, 1)

            def project(b, p, t, before):
                if before:
                    pe.wait_ge(s_mult, per_step(b, p, TT, t))
                    pe.wait_ge(s_vals, per_step(b, p, TT, t))
                if before and p == STEPS:
                    for n in range(TT):
                        emptied(pe, b, LN_STEP, f"L{n}")
                k = p % STEPS
                wq = [w[:, :, k * NQ:(k + 1) * NQ] for w in (wq_hi, wq_lo)]
                wkv = [[w[:, c].rearrange("p (k s n) -> p s k n", k=2, s=STEPS)[:, k] for c in range(DB)]
                       for w in (wkv_hi, wkv_lo)]
                plan = [(s, c, w) for c in range(DB) for s, w in ((0, 0), (0, 1), (1, 0))]
                for i, (s, c, w) in enumerate(plan):
                    lhs = xn_t[:, t, s, c]
                    first, end = i == 0, i == len(plan) - 1
                    pe.matmul(proj[:, 0:NQ], lhs, wq[w][:, c], start=first, stop=end)
                    last = pe.matmul(proj[:, NQ:NQ + NKV].rearrange("p (k n) -> p k n", k=2), lhs, wkv[w][c], start=first, stop=end)
                last.then_inc(s_proj, 1)

            def head_transposes(b, p, n):
                t = min(n, 1)
                if n < 2:
                    pe.wait_ge(s_lo, per_step(b, p + 1, TT, t + 1))
                else:
                    pe.wait_ge(s_swap, per_step(b, p + 1, TT, 2))
                bank, full = previous_ring_use(pe, b, p, f"T{n}")
                out = bank[:, :].bitcast(fp16)
                if n < 2:
                    parts = [stacked[:, n, h] for h in range(QS)]
                else:
                    parts = [stacked[:, t, QS + KVS * a + j] for a in range(2) for j in range(KVS) for t in range(TT)]
                for i, part in enumerate(parts):
                    last = pe.transpose(out[:, i * P:(i + 1) * P], part.rearrange("p s d -> p (s d)"), ident16[:])
                last.then_inc(full, 1)

            def score(b, p, u):
                j, t, h0, heads, keys = unit[u]
                out = scores[u % 3]
                if u == 0:
                    emptied(pe, b, p - 1, "T1")
                    emptied(pe, b, p - 1, "T2")
                if not (isinstance(b, int) and b == 0 and p == 0 and u < 3):
                    pe.wait_ge(s_exp, per_step(b, p, UNITS, u - 2))
                if keys == P:
                    pe.matmul(out[:, :], identb[:], causal[:].rearrange("p h k -> p (h k)"),
                              start=True, stop=False, skip_group_check=True)
                else:
                    pe.matmul(out[:, :].rearrange("p (h t k) -> p h t k", h=2, t=TT)[:, :, 1], identb[:],
                              causal[:, 0:2], start=True, stop=False, skip_group_check=True)
                for i in range(heads):
                    for a in range(2):
                        last = pe.matmul(out[:, i * keys:(i + 1) * keys], q_t[:, p % 2, t, j * G + h0 + i],
                                         k_t[:, p % 2, a, j].rearrange("p t n -> p (t n)")[:, 0:keys],
                                         start=False, stop=i == heads - 1 and a == 1, skip_group_check=True)
                last.then_inc(s_scores, 1)

            def prob_transposes(b, p, u):
                j, t, h0, heads, keys = unit[u]
                pe.wait_ge(s_norm, per_step(b, p, UNITS, u + 1))
                bank, full = previous_ring_use(pe, b, p, f"P{u}")
                for i in range(4):
                    kb, h = divmod(i, heads) if keys > P else (0, i)
                    last = pe.transpose(bank[:, i * P:(i + 1) * P],
                                        probs[:, u % 3, h * keys + kb * P:h * keys + (kb + 1) * P], ident32[:])
                last.then_inc(full, 1)

            def heads_product(b, p, t, free):
                for u in ((0, 1) if t == 0 else (2, 3, 4, 5)):
                    emptied(pe, b, p, f"P{u}")
                pe.wait_ge(s_vals, per_step(b, p, TT, TT))
                free()
                for kb in range(t + 1):
                    for j in range(KVS):
                        rhs = pt0[:, j] if t == 0 else pt1[:, j, kb]
                        last = pe.matmul(heads_out[j * DH:(j + 1) * DH, :], values[:, p % 2, kb, j * DH:(j + 1) * DH],
                                         rhs.rearrange("p g n -> p (g n)"), start=kb == 0, stop=kb == t,
                                         skip_group_check=True)
                last.then_inc(s_heads, 1)

            def out_projection(b):
                pe.wait_ge(s_o_lo, (b + 1) * (STEPS * TT))
                for t in range(TT):
                    n = 0
                    for k in range(KT):
                        for part, w in ((o_hi, wo_hi), (o_hi, wo_lo), (o_lo, wo_hi)):
                            last = pe.matmul(heads_out[:, t * D:(t + 1) * D],
                                             part[:, k // G, k % G, t * P:(t + 1) * P], w[:, k],
                                             start=n == 0, stop=n == 3 * KT - 1)
                            n += 1
                last.then_inc(s_wo_mm, 1)

            def step(b, p, last, after):
                more = not (last and p + 1 == STEPS)
                if more:
                    project(b, p + 1, 0, True)
                prob_transposes(b, p, 0)
                score(b, p, 3)
                if more:
                    project(b, p + 1, 1, True)
                prob_transposes(b, p, 1)
                score(b, p, 4)
                if p == 0 and after:
                    out_projection(b - 1)

                def free0():
                    if p == 0 and after:
                        pe.wait_ge(s_x1, b)
                    elif p:
                        pe.wait_ge(s_o_lo, per_step(b, p, TT, 0))
                heads_product(b, p, 0, free0)
                if p == LN_STEP and not last:
                    for t in range(TT):
                        norm_transposes(b, p, b + 1, t)
                prob_transposes(b, p, 2)
                score(b, p, 5)
                if more:
                    head_transposes(b, p, 0)
                prob_transposes(b, p, 3)
                if more:
                    head_transposes(b, p, 1)
                    head_transposes(b, p, 2)
                    score(b, p + 1, 0)
                prob_transposes(b, p, 4)
                if more:
                    score(b, p + 1, 1)
                prob_transposes(b, p, 5)
                if more:
                    score(b, p + 1, 2)
                heads_product(b, p, 1, lambda: pe.wait_ge(s_o_lo, per_step(b, p, TT, 1)))

            pe.wait_ge(s_const, 8)
            for t in range(TT):
                norm_transposes(0, -1, 0, t)
            for t in range(TT):
                emptied(pe, 0, -1, f"L{t}")
            pe.wait_ge(s_w_lo, 2)
            project(0, 0, 0, False)
            project(0, 0, 1, True)
            for n in range(3):
                head_transposes(0, -1, n)
            for u in range(3):
                score(0, 0, u)
            pe.wait_ge(s_w_lo, 3)
            for p in range(STEPS):
                step(0, p, n_seq == 1, False)
            if n_seq > 2:
                with pe.Fori(1, n_seq - 1) as b:
                    for p in range(STEPS):
                        step(b, p, False, True)
            if n_seq > 1:
                for p in range(STEPS):
                    step(n_seq - 1, p, True, True)
            out_projection(n_seq - 1)


def moe_blocks(nc, x1_dram, gate_w, gate_up, down, shared_gate_up, shared_down, shared_gate, rows_dram,
               hidden_dram, base_dram, out, n_seq):
    fp32, fp16, u32, i32 = mybir.dt.float32, mybir.dt.float16, mybir.dt.uint32, mybir.dt.int32
    ALU, ACT, AX = mybir.AluOpType, mybir.ActivationFunctionType, mybir.AxisListType

    P = 128
    D = gate_w.shape[1]
    DB = D // P
    E = gate_w.shape[0]
    I = down.shape[2]
    SI = shared_down.shape[1]
    TOPK = 4
    HB = 88
    NHB = I // HB
    SB = -(-SI // P)
    GT = 4
    N = GT * P
    TOKENS = n_seq * x1_dram.shape[1]
    GROUPS = TOKENS // N
    TILES = TOKENS // P
    REGION = TOKENS + P
    SLOT_TILES = TOKENS * TOPK // P + E
    U = 4
    SLOT_TILES = -(-SLOT_TILES // U) * U
    SPARE = SLOT_TILES - TOKENS * TOPK // P
    assert NHB * HB == I and GROUPS * N == TOKENS and E % 2 == 0
    assert rows_dram.shape[0] == E * REGION + SPARE * P and hidden_dram.shape[0] == SLOT_TILES * P

    X_SCALE, W_SCALE, H_SCALE = 2.0 ** 5, 2.0 ** 9, 2.0 ** 4
    UP_SCALE = 1.0 / (X_SCALE * W_SCALE)
    DOWN_SCALE = 1.0 / (H_SCALE * W_SCALE)
    EPS = 1e-5
    SPLIT = ((0, 0), (0, 1), (1, 0))

    keep = ExitStack()
    with keep:
        def kept(name, shape, dt):
            return keep.enter_context(nc.sbuf_tensor(name, shape, dt))

        gu_t = [kept(f"gu_t{s}", [P, DB, E * 2 * I], fp16) for s in range(2)]
        dn_t = [kept(f"dn_t{s}", [HB, E, NHB * D], fp16) for s in range(2)]
        sgu_t = [kept(f"sgu_t{s}", [P, DB, 2 * SI], fp16) for s in range(2)]
        sdn_t = [kept(f"sdn_t{s}", [P, SB, D], fp16) for s in range(2)]
        router_t = [kept(f"router_t{s}", [P, DB, E + 1], fp16) for s in range(2)]
        ident32, ident16 = kept("m_ident32", [P, P], fp32), kept("m_ident16", [P, P], fp16)
        places = kept("places", [P, TILES * TOPK], fp32)
        choices = kept("choices", [P, TILES * TOPK], fp32)
        shares = kept("shares", [P, TILES * TOPK], fp32)
        counts = kept("counts", [P, E], fp32)
        chosen = kept("chosen", [P, GT + 1, E], fp16)

        prepare_weights(nc, gate_w, gate_up, down, shared_gate_up, shared_down, shared_gate,
                        gu_t, dn_t, sgu_t, sdn_t, router_t, ident32, ident16, W_SCALE)

        ctx = ExitStack()
        with ctx:
            def sb(name, shape, dt):
                return ctx.enter_context(nc.sbuf_tensor(name, shape, dt))

            def pb(name):
                return ctx.enter_context(nc.psum_tensor(name, [P, 512], fp32))

            def sem(name):
                return ctx.enter_context(nc.semaphore(name))

            strict, ones = sb("strict", [P, P], fp16), sb("ones", [P, P], fp16)
            expert_ids = sb("expert_ids", [P, TOPK, E], fp32)
            regions = sb("regions", [P, E], fp32)
            eps = sb("m_eps", [P, 1], fp32)
            zeros = sb("zeros", [P, 2 * D], fp16)
            x1 = sb("x1", [P, 2, GT, D], fp32)
            stats, moments = sb("m_stats", [P, GT, 6], fp32), sb("m_moments", [P, GT, 2], fp32)
            log_var, rough = sb("m_log_var", [P, GT], fp32), sb("m_rough", [P, GT], fp32)
            correction, rstd = sb("m_correction", [P, GT], fp32), sb("m_rstd", [P, GT], fp32)
            xn = sb("m_xn", [P, GT, D], fp32)
            rows = sb("rows", [P, 2, GT, 2, D], fp16)
            xt = sb("xt", [P, 2, DB, N], fp16)
            logits = sb("logits", [P, GT, E + 1], fp32)
            negmax, sums = sb("m_negmax", [P, GT], fp32), sb("m_sums", [P, GT], fp32)
            probs = sb("m_probs", [P, GT, E], fp32)
            top, index = sb("top", [P, GT, 8], fp32), sb("index", [P, GT, 8], u32)
            indexf = sb("indexf", [P, GT, 8], fp32)
            hot, at = sb("hot", [P, GT, TOPK, E], fp32), sb("at", [P, GT, TOPK, E], fp32)
            chosen_now = sb("chosen_now", [P, GT, E], fp16)
            row_of = sb("row_of", [P, GT, E], fp32)
            share, share_sum = sb("share", [P, GT, TOPK], fp32), sb("share_sum", [P, GT], fp32)
            place = sb("place", [P, GT * TOPK], fp32)
            placeu = sb("placeu", [P, 2, GT * TOPK], u32)
            tail, tailu = sb("tail", [P, E], fp32), sb("tailu", [P, E], u32)
            sigmoid = sb("sigmoid", [P, GT], fp32)
            silu = sb("silu", [P, 2, N], fp32)
            h = sb("h", [P, 2, N], fp32)
            h_hi, h_lo = sb("h_hi", [P, SB, N], fp16), sb("h_lo", [P, SB, N], fp16)
            base = sb("base", [P, GT, D], fp32)

            turned, small = pb("turned"), pb("small")
            gates, ups = [pb("gates0"), pb("gates1")], [pb("ups0"), pb("ups1")]
            downs = [pb("downs0"), pb("downs1")]

            s_const, s_x1, s_stat, s_moments, s_rough = sem("r_const"), [sem("r_x1_0"), sem("r_x1_1")], sem("r_stat"), sem("r_moments"), sem("r_rough")
            s_rstd, s_xn, s_rows_hi, s_rows = sem("r_rstd"), sem("r_xn"), sem("r_rows_hi"), sem("r_rows")
            s_turned, s_xt, s_logits_mm, s_logits = sem("r_turned"), sem("r_xt"), sem("r_logits_mm"), sem("r_logits")
            s_negmax, s_probs, s_dve = sem("r_negmax"), sem("r_probs"), sem("r_dve")
            s_chosen, s_rank, s_place, s_scattered = sem("r_chosen"), sem("r_rank"), sem("r_place"), [sem("r_scattered0"), sem("r_scattered1")]
            s_gu, s_silu, s_h, s_h_hi, s_h_lo = sem("r_gu"), sem("r_silu"), sem("r_h"), sem("r_h_hi"), sem("r_h_lo")
            s_down, s_base, s_stored, s_zero, s_tail = sem("r_down"), sem("r_base"), sem("r_stored"), sem("r_zero"), sem("r_tail")
            s_at, s_kept, s_totals = sem("r_at"), sem("r_kept"), sem("r_totals")
            s_tails = sem("r_tails")
            s_passed, s_pool_passed = sem("r_passed"), sem("r_pool_passed")

            by_group = lambda a, g: a[g * GT:(g + 1) * GT]
            x1_rows = x1_dram.rearrange("b (t p) d -> p (b t) d", p=P)
            base_rows = base_dram.rearrange("b (t p) d -> p (b t) d", p=P)

            def per_group(g, each, n):
                return g * each + n

            ROUTER_STEPS = 14

            def passes(g, half):
                return g // 2 if isinstance(g, int) else (g - half) // 2

            def block_rows(k):
                return min(P, SI - k * P)

            block = ctx.enter_context(nc.Block(name="route"))

            @block.sync
            def _(sp):
                def load(g, half):
                    sp.dma_start(x1[:, half], x1_rows[:, bass.ds(g * GT, GT)]).then_inc(s_x1[half], 16)

                def store(g):
                    sp.wait_ge(s_base, (g + 1) * GT)
                    sp.dma_start(base_rows[:, bass.ds(g * GT, GT)], base[:]).then_inc(s_stored, 16)

                load(0, 0)
                load(1, 1)
                sp.wait_ge(s_const, 1)
                for k in range(SPARE):
                    r = E * REGION + k * P
                    sp.dma_start(rows_dram[r:r + P, :], zeros[:]).then_inc(s_zero, 16)
                if GROUPS > 2:
                    for half in range(2):
                        store(half)
                        load(half + 2, half)
                if GROUPS > 4:
                    with sp.Fori(1, GROUPS // 2 - 1) as gg:
                        for half in range(2):
                            store(gg * 2 + half)
                            load(gg * 2 + (half + 2), half)
                for half in range(2):
                    store(GROUPS - 2 + half)
                sp.wait_ge(s_stored, 16 * GROUPS)
                sp.wait_ge(s_zero, 16 * SPARE)

            @block.gpsimd
            def _(pool):
                pool.memset(zeros[:], 0.0).then_inc(s_const, 1)
                pool.memset(strict[:], 1.0).then_inc(s_const, 1)
                pool.memset(ones[:], 1.0).then_inc(s_const, 1)
                pool.memset(eps[:], EPS).then_inc(s_const, 1)
                pool.memset(chosen[:], 0.0).then_inc(s_const, 1)
                pool.iota(expert_ids[:], pattern=[[0, TOPK], [1, E]], base=0, channel_multiplier=0,
                          allow_small_or_imprecise_dtypes=True).then_inc(s_const, 1)
                pool.iota(regions[:], pattern=[[REGION, E]], base=0, channel_multiplier=0,
                          allow_small_or_imprecise_dtypes=True).then_inc(s_const, 1)
                pool.iota(tail[:], pattern=[[REGION, E]], base=0, channel_multiplier=1,
                          allow_small_or_imprecise_dtypes=True).then_inc(s_const, 1)
                pool.wait_ge(s_const, 8)
                pool.affine_select(out=strict[:], in_=strict[:], compare_op=ALU.is_gt, fill=0.0, base=0,
                                   pattern=[[1, P]], channel_multiplier=-1).then_inc(s_const, 1)

                def scatter(g, half):
                    pool.wait_ge(s_place, g + 1)
                    pool.sem_inc(s_pool_passed, 1)
                    for t in range(GT):
                        for k in range(TOPK):
                            i = t * TOPK + k
                            pool.indirect_dma_start(
                                rows_dram, bass.IndirectOffsetOnAxis(ap=placeu[:, half, i:i + 1], axis=0),
                                rows[:, half, t].rearrange("p s d -> p (s d)"), None).then_inc(s_scattered[half], 16)

                with pool.Fori(0, GROUPS // 2) as gg:
                    for half in range(2):
                        scatter(gg * 2 + half, half)
                pool.wait_ge(s_tail, 2)
                for e in range(E):
                    pool.indirect_dma_start(rows_dram, bass.IndirectOffsetOnAxis(ap=tailu[:, e:e + 1], axis=0),
                                            zeros[:], None).then_inc(s_tails, 16)
                for half in range(2):
                    pool.wait_ge(s_scattered[half], 16 * TILES * TOPK // 2)
                pool.wait_ge(s_tails, 16 * E)

            @block.scalar
            def _(act):
                act.wait_ge(s_const, 9)

                def norm(g):
                    act.wait_ge(s_moments, (g + 1) * GT)
                    act.activation(log_var[:], moments[:, :, 1], ACT.Ln, bias=eps[:]).then_inc(s_rough, 1)
                    act.wait_ge(s_rough, 2 * g + 1)
                    act.activation(rough[:], log_var[:], ACT.Exp, scale=-0.5).then_inc(s_rough, 1)

                def high_rows(g, half):
                    act.wait_ge(s_xn, g + 1)
                    act.activation(rows[:, half, :, 0], xn[:], ACT.Copy, scale=X_SCALE).then_inc(s_rows_hi, 1)

                def router(g):
                    act.wait_ge(s_negmax, g + 1)
                    for t in range(GT):
                        act.activation(probs[:, t], logits[:, t, 0:E], ACT.Exp, bias=negmax[:, t:t + 1],
                                       accum_out=sums[:, t:t + 1])
                    act.activation(sigmoid[:], logits[:, :, E], ACT.Exp, scale=-1.0).then_inc(s_probs, 1)

                def shared(g):
                    for k in range(SB):
                        n = block_rows(k)
                        act.wait_ge(s_gu, per_group(g, SB, k + 1))
                        act.activation(silu[0:n, k % 2], gates[k % 2][0:n, :], ACT.Silu, scale=UP_SCALE).then_inc(s_silu, 1)
                        act.wait_ge(s_h, per_group(g, SB, k + 1))
                        act.activation(h_hi[0:n, k], h[0:n, k % 2], ACT.Copy).then_inc(s_h_hi, 1)

                def group(g, half, last):
                    router(g)
                    if not last:
                        norm(g + 1)
                        high_rows(g + 1, 1 - half)
                    shared(g)

                norm(0)
                high_rows(0, 0)
                if GROUPS > 2:
                    for half in range(2):
                        group(half, half, False)
                if GROUPS > 4:
                    with act.Fori(1, GROUPS // 2 - 1) as gg:
                        for half in range(2):
                            group(gg * 2 + half, half, False)
                for half in range(2):
                    group(GROUPS - 2 + half, half, half == 1)

            @block.vector
            def _(dve):
                dve.wait_ge(s_const, 9)

                def norm(g, half):
                    dve.wait_ge(s_x1[half], passes(g, half) * 16 + 16)
                    for t in range(GT):
                        dve.bn_stats(stats[:, t], x1[:, half, t]).then_inc(s_stat, 1)
                    dve.wait_ge(s_stat, (g + 1) * GT)
                    dve.sem_inc(s_passed, 1)
                    for t in range(GT):
                        dve.bn_aggr(moments[:, t], stats[:, t]).then_inc(s_moments, 1)
                    dve.wait_ge(s_rough, 2 * g + 2)
                    dve.tensor_tensor(correction[:], rough[:], rough[:], ALU.mult).then_inc(s_rstd, 1)
                    dve.wait_ge(s_rstd, 4 * g + 1)
                    dve.scalar_tensor_tensor(correction[:], moments[:, :, 1], EPS, correction[:], ALU.add,
                                             ALU.mult).then_inc(s_rstd, 1)
                    dve.wait_ge(s_rstd, 4 * g + 2)
                    dve.tensor_scalar(correction[:], correction[:], -0.5, 1.5, ALU.mult, ALU.add).then_inc(s_rstd, 1)
                    dve.wait_ge(s_rstd, 4 * g + 3)
                    dve.tensor_tensor(rstd[:], rough[:], correction[:], ALU.mult).then_inc(s_rstd, 1)
                    dve.wait_ge(s_rstd, 4 * g + 4)
                    if not (isinstance(g, int) and g < 2):
                        dve.wait_ge(s_scattered[half], passes(g, half) * (16 * GT * TOPK))
                    for t in range(GT):
                        last = dve.tensor_scalar(xn[:, t], x1[:, half, t], moments[:, t, 0:1], rstd[:, t:t + 1],
                                                 ALU.subtract, ALU.mult)
                    last.then_inc(s_xn, 1)
                    dve.wait_ge(s_rows_hi, g + 1)
                    dve.scalar_tensor_tensor(rows[:, half, :, 1], xn[:], X_SCALE, rows[:, half, :, 0],
                                             ALU.mult, ALU.subtract).then_inc(s_rows, 1)

                def transposed(g):
                    for s in range(2):
                        dve.wait_ge(s_turned, per_group(g, 2, s + 1))
                        dve.tensor_copy(xt[:, s].rearrange("p c n -> p (c n)"), turned[:, :].bitcast(fp16)).then_inc(s_xt, 1)

                def router(g, half):
                    done = [0]

                    def link(ins, apart=False):
                        done[0] += 1
                        ins.then_inc(s_dve, 1)
                        dve.wait_ge(s_dve, g * ROUTER_STEPS + done[0])
                        if apart:
                            dve.sem_inc(s_passed, 1)

                    dve.wait_ge(s_logits_mm, g + 1)
                    link(dve.tensor_scalar(logits[:], small[:, 0:GT * (E + 1)].rearrange("p (t e) -> p t e", t=GT),
                                           UP_SCALE, None, ALU.mult))
                    dve.tensor_reduce(negmax[:], logits[:, :, 0:E], AX.X, ALU.max, negate=True).then_inc(s_negmax, 1)
                    dve.wait_ge(s_probs, g + 1)
                    link(dve.reciprocal(sums[:], sums[:]))
                    link(dve.tensor_tensor(probs[:], probs[:], sums[:].unsqueeze(2).broadcast_to([P, GT, E]), ALU.mult), apart=True)
                    for t in range(GT):
                        ins = dve.max(top[:, t], probs[:, t])
                    link(ins, apart=True)
                    for t in range(GT):
                        ins = dve.max_index(index[:, t], top[:, t], probs[:, t])
                    link(ins)
                    link(dve.tensor_copy(indexf[:], index[:]))
                    for t in range(GT):
                        ins = dve.tensor_tensor(hot[:, t], expert_ids[:], indexf[:, t, 0:TOPK].unsqueeze(2)
                                                .broadcast_to([P, TOPK, E]), ALU.is_equal)
                    link(ins)
                    for t in range(GT):
                        with nc.allow_low_precision(reason="a sum of at most one 1 and zeros"):
                            ins = dve.tensor_reduce(chosen_now[:, t], hot[:, t].rearrange("p k e -> p e k"), AX.X, ALU.add)
                    link(ins)
                    for t in range(GT):
                        ins = dve.tensor_tensor(chosen[:, t + 1], chosen[:, t], chosen_now[:, t], ALU.add)
                        if t < GT - 1:
                            ins.then_inc(s_chosen, 1)
                            dve.wait_ge(s_chosen, g * (GT + 1) + t + 1)
                    ins.then_inc(s_chosen, 1)
                    link(dve.tensor_reduce(share_sum[:], top[:, :, 0:TOPK], AX.X, ALU.add))
                    link(dve.reciprocal(share_sum[:], share_sum[:]))
                    dve.tensor_tensor(shares[:, bass.ds(g * (GT * TOPK), GT * TOPK)].rearrange("p (t k) -> p t k", k=TOPK),
                                      top[:, :, 0:TOPK], share_sum[:].unsqueeze(2).broadcast_to([P, GT, TOPK]), ALU.mult)
                    link(dve.tensor_scalar(sigmoid[:], sigmoid[:], 1.0, None, ALU.add))
                    link(dve.reciprocal(sigmoid[:], sigmoid[:]))
                    link(dve.tensor_scalar(sigmoid[:], sigmoid[:], DOWN_SCALE, None, ALU.mult))
                    assert done[0] == ROUTER_STEPS - 1
                    dve.wait_ge(s_rank, g + 1)
                    dve.tensor_copy(chosen[:, 0], chosen[:, GT]).then_inc(s_chosen, 1)
                    link(dve.tensor_tensor(row_of[:], small[:, 128:128 + GT * E].rearrange("p (t e) -> p t e", t=GT),
                                           regions[:].unsqueeze(1).broadcast_to([P, GT, E]), ALU.add))

                def place_rows(g, half):
                    dve.wait_ge(s_chosen, (g + 1) * (GT + 1))
                    for t in range(GT):
                        ins = dve.tensor_tensor(at[:, t], hot[:, t], row_of[:, t].unsqueeze(1)
                                                .broadcast_to([P, TOPK, E]), ALU.mult)
                    ins.then_inc(s_at, 1)
                    dve.wait_ge(s_at, 2 * g + 1)
                    dve.tensor_reduce(place[:], at[:].rearrange("p t k e -> p (t k) e"), AX.X, ALU.add).then_inc(s_at, 1)
                    dve.wait_ge(s_at, 2 * g + 2)
                    dve.tensor_copy(placeu[:, half], place[:]).then_inc(s_place, 1)
                    dve.tensor_copy(choices[:, bass.ds(g * (GT * TOPK), GT * TOPK)].rearrange("p (t k) -> p t k", k=TOPK),
                                    indexf[:, :, 0:TOPK])
                    dve.tensor_copy(places[:, bass.ds(g * (GT * TOPK), GT * TOPK)], place[:]).then_inc(s_kept, 1)

                def shared(g, half, k):
                    n = block_rows(k)
                    dve.wait_ge(s_silu, per_group(g, SB, k + 1))
                    dve.scalar_tensor_tensor(h[0:n, k % 2], ups[k % 2][0:n, :], UP_SCALE * H_SCALE, silu[0:n, k % 2],
                                             ALU.mult, ALU.mult).then_inc(s_h, 1)
                    dve.wait_ge(s_h_hi, per_group(g, SB, k + 1))
                    dve.tensor_tensor(h_lo[0:n, k], h[0:n, k % 2], h_hi[0:n, k], ALU.subtract).then_inc(s_h_lo, 1)

                def add_base(g, half):
                    if not (isinstance(g, int) and g == 0):
                        dve.wait_ge(s_stored, 16 * g)
                    for t in range(GT):
                        dve.wait_ge(s_down, per_group(g, 2, t // 2 + 1))
                        dve.scalar_tensor_tensor(base[:, t], downs[t // 2][:, (t % 2) * D:(t % 2 + 1) * D],
                                                 sigmoid[:, t:t + 1], x1[:, half, t], ALU.mult, ALU.add).then_inc(s_base, 1)

                def group(g, half, last):
                    router(g, half)
                    place_rows(g, half)
                    if not last:
                        norm(g + 1, 1 - half)
                    for k in range(SB):
                        shared(g, half, k)
                    if not last:
                        transposed(g + 1)
                    add_base(g, half)

                norm(0, 0)
                transposed(0)
                if GROUPS > 2:
                    for half in range(2):
                        group(half, half, False)
                if GROUPS > 4:
                    with dve.Fori(1, GROUPS // 2 - 1) as gg:
                        for half in range(2):
                            group(gg * 2 + half, half, False)
                for half in range(2):
                    group(GROUPS - 2 + half, half, half == 1)
                dve.wait_ge(s_totals, 1)
                dve.tensor_tensor(tail[:], tail[:], small[:, 256:256 + E], ALU.add).then_inc(s_tail, 1)
                dve.wait_ge(s_tail, 1)
                dve.tensor_copy(tailu[:], tail[:]).then_inc(s_tail, 1)
                dve.tensor_copy(counts[:], small[:, 256:256 + E]).then_inc(s_kept, 1)

            @block.tensor
            def _(pe):
                pe.wait_ge(s_const, 9)

                def transposes(g, half):
                    pe.wait_ge(s_rows, g + 1)
                    for s in range(2):
                        if s or not (isinstance(g, int) and g == 0):
                            pe.wait_ge(s_xt, per_group(g, 2, s))
                        bank = turned[:, :].bitcast(fp16)
                        for c in range(DB):
                            for t in range(GT):
                                i = c * GT + t
                                last = pe.transpose(bank[:, i * P:(i + 1) * P],
                                                    rows[:, half, t, s, c * P:(c + 1) * P], ident16[:])
                        last.then_inc(s_turned, 1)

                def route(g):
                    pe.wait_ge(s_xt, per_group(g, 2, 2))
                    if not (isinstance(g, int) and g == 0):
                        pe.wait_ge(s_dve, g * ROUTER_STEPS)
                    for t in range(GT):
                        n = 0
                        for c in range(DB):
                            for a, w in SPLIT:
                                last = pe.matmul(small[:, t * (E + 1):(t + 1) * (E + 1)], xt[:, a, c, t * P:(t + 1) * P],
                                                 router_t[w][:, c], start=n == 0, stop=n == 3 * DB - 1)
                                n += 1
                    last.then_inc(s_logits_mm, 1)

                def ranks(g):
                    pe.wait_ge(s_chosen, g * (GT + 1) + GT)
                    for t in range(GT):
                        out_ = small[:, 128 + t * E:128 + (t + 1) * E]
                        pe.matmul(out_, strict[:], chosen_now[:, t], start=True, stop=False)
                        last = pe.matmul(out_, ones[:], chosen[:, t], start=False, stop=True)
                    last.then_inc(s_rank, 1)

                def shared_up(g, k):
                    n = block_rows(k)
                    if k >= 2 or not (isinstance(g, int) and g == 0):
                        pe.wait_ge(s_h, per_group(g, SB, k - 1))
                    for bank, first in ((gates[k % 2], 0), (ups[k % 2], SI)):
                        i = 0
                        for c in range(DB):
                            for w, a in SPLIT:
                                last = pe.matmul(bank[0:n, :], sgu_t[w][:, c, first + k * P:first + k * P + n],
                                                 xt[:, a, c], start=i == 0, stop=i == 3 * DB - 1)
                                i += 1
                    last.then_inc(s_gu, 1)

                def shared_down(g):
                    pe.wait_ge(s_h_lo, per_group(g, SB, SB))
                    if not (isinstance(g, int) and g == 0):
                        pe.wait_ge(s_base, g * GT)
                    for t in range(GT):
                        i = 0
                        for k in range(SB):
                            n = block_rows(k)
                            for a, w in SPLIT:
                                hh = (h_hi, h_lo)[a]
                                last = pe.matmul(downs[t // 2][:, (t % 2) * D:(t % 2 + 1) * D], hh[0:n, k, t * P:(t + 1) * P],
                                                 sdn_t[w][0:n, k], start=i == 0, stop=i == 3 * SB - 1)
                                i += 1
                        if t % 2:
                            last.then_inc(s_down, 1)

                def group(g, half, last):
                    route(g)
                    shared_up(g, 0)
                    shared_up(g, 1)
                    ranks(g)
                    for k in range(2, SB):
                        shared_up(g, k)
                    if not last:
                        transposes(g + 1, 1 - half)
                    shared_down(g)

                transposes(0, 0)
                if GROUPS > 2:
                    for half in range(2):
                        group(half, half, False)
                if GROUPS > 4:
                    with pe.Fori(1, GROUPS // 2 - 1) as gg:
                        for half in range(2):
                            group(gg * 2 + half, half, False)
                for half in range(2):
                    group(GROUPS - 2 + half, half, half == 1)
                pe.wait_ge(s_chosen, GROUPS * (GT + 1))
                pe.wait_ge(s_dve, GROUPS * ROUTER_STEPS)
                pe.matmul(small[:, 256:256 + E], ones[:], chosen[:, 0], start=True, stop=True).then_inc(s_totals, 1)

        experts_block(nc, rows_dram, hidden_dram, counts, places, choices, gu_t, dn_t, ident16, SLOT_TILES, U, REGION,
                      UP_SCALE, H_SCALE, DOWN_SCALE)
        combine_block(nc, base_dram, hidden_dram, places, shares, out, TILES, TOPK)


def prepare_weights(nc, gate_w, gate_up, down, shared_gate_up, shared_down, shared_gate,
                    gu_t, dn_t, sgu_t, sdn_t, router_t, ident32, ident16, W_SCALE):
    fp32, fp16 = mybir.dt.float32, mybir.dt.float16
    ALU, ACT = mybir.AluOpType, mybir.ActivationFunctionType
    P = 128
    E, D = gate_w.shape
    DB = D // P
    I = down.shape[2]
    SI = shared_down.shape[1]
    HB = dn_t[0].shape[0]
    NHB = I // HB
    FB = 2 * NHB
    BANKS, EACH = 6, 1 + DB

    ctx = ExitStack()
    with ctx:
        def sb(name, shape, dt):
            return ctx.enter_context(nc.sbuf_tensor(name, shape, dt))

        def sem(name):
            return ctx.enter_context(nc.semaphore(name))

        gu = sb("gu", [HB, 2, FB, D], fp32)
        dn = sb("dn", [P, 2, DB, I], fp32)
        sgu = sb("sgu", [HB, 2 * SI // HB, D], fp32)
        sdn = sb("sdn", [P, DB, SI], fp32)
        router = sb("router", [E + 1, D], fp32)
        banks = [ctx.enter_context(nc.psum_tensor(f"w_bank{i}", [P, 512], fp32)) for i in range(BANKS)]
        s_const, s_turned, s_high, s_low = sem("w_const"), sem("w_turned"), sem("w_high"), sem("w_low")
        s_expert, s_rest = [sem("w_expert0"), sem("w_expert1")], sem("w_rest")

        block = ctx.enter_context(nc.Block(name="weights"))

        rest = [("sgu", c, q) for c in range(DB) for q in range(2 * SI // (FB * HB))]
        rest += [("sdn", k, n) for k, n in ((0, 2), (2, 2), (4, 1), (5, 1))] + [("router", 0, 0)]

        def rest_parts(kind, a, n, bank, dst):
            if kind == "sgu":
                return bank[:, 0:FB * HB], dst["sgu"][:, a, n * FB * HB:(n + 1) * FB * HB]
            if kind == "sdn":
                r = min(P, SI - a * P)
                return bank[0:r, 0:n * D], dst["sdn"][0:r, a:a + n].rearrange("p k d -> p (k d)")
            return bank[:, 0:DB * (E + 1)], dst["router"][:].rearrange("p c e -> p (c e)")

        @block.sync
        def _(sp):
            def load(e, half, waits=True):
                if waits:
                    sp.wait_ge(s_turned, e * EACH - EACH)
                sp.dma_start(gu[:, half], gate_up[e].rearrange("(b r) d -> r b d", r=HB)).then_inc(s_expert[half], 16)
                sp.dma_start(dn[:, half], down[e].rearrange("(t p) i -> p t i", p=P)).then_inc(s_expert[half], 16)

            load(0, 0, False)
            load(1, 1, False)
            sp.dma_start(sgu[:], shared_gate_up.rearrange("(b r) d -> r b d", r=HB)).then_inc(s_rest, 16)
            sp.dma_start(sdn[:], shared_down.rearrange("(t p) i -> p t i", p=P)).then_inc(s_rest, 16)
            sp.dma_start(router[0:E, :], gate_w).then_inc(s_rest, 16)
            sp.dma_start(router[E:E + 1, :], shared_gate).then_inc(s_rest, 16)
            with sp.Fori(1, E // 2) as ee:
                for half in range(2):
                    load(ee * 2 + half, half)

        @block.gpsimd
        def _(pool):
            for m in (ident32, ident16):
                pool.memset(m[:], 0.0).then_inc(s_const, 1)
            pool.wait_ge(s_const, 2)
            for m in (ident32, ident16):
                pool.affine_select(out=m[:], in_=m[:], compare_op=ALU.not_equal, fill=1.0, base=0,
                                   pattern=[[-1, P]], channel_multiplier=1).then_inc(s_const, 1)

        @block.tensor
        def _(pe):
            pe.wait_ge(s_const, 4)

            def free(fill):
                if not isinstance(fill, int) or fill >= BANKS:
                    pe.wait_ge(s_low, fill - BANKS + 1)

            def expert(e, half):
                pe.wait_ge(s_expert[half], ((e - half) // 2 if not isinstance(e, int) else e // 2) * 32 + 32)
                for c in range(DB):
                    free(e * EACH + c)
                    for b in range(FB):
                        last = pe.transpose(banks[half * EACH + c][:, b * HB:(b + 1) * HB],
                                            gu[:, half, b, c * P:(c + 1) * P], ident32[0:HB, 0:HB])
                    last.then_inc(s_turned, 1)
                free(e * EACH + DB)
                for b in range(NHB):
                    for t in range(DB):
                        last = pe.transpose(banks[half * EACH + DB][0:HB, b * D + t * P:b * D + (t + 1) * P],
                                            dn[:, half, t, b * HB:(b + 1) * HB], ident32[:])
                last.then_inc(s_turned, 1)

            for half in range(2):
                expert(half, half)
            with pe.Fori(1, E // 2) as ee:
                for half in range(2):
                    expert(ee * 2 + half, half)
            pe.wait_ge(s_rest, 64)
            for i, (kind, a, n) in enumerate(rest):
                fill = E * EACH + i
                free(fill)
                bank = banks[fill % BANKS]
                if kind == "sgu":
                    for b in range(FB):
                        last = pe.transpose(bank[:, b * HB:(b + 1) * HB], sgu[:, n * FB + b, a * P:(a + 1) * P],
                                            ident32[0:HB, 0:HB])
                elif kind == "sdn":
                    for k in range(n):
                        r = min(P, SI - (a + k) * P)
                        for t in range(DB):
                            last = pe.transpose(bank[0:r, k * D + t * P:k * D + (t + 1) * P],
                                                sdn[:, t, (a + k) * P:(a + k) * P + r], ident32[:])
                else:
                    for c in range(DB):
                        last = pe.transpose(bank[:, c * (E + 1):(c + 1) * (E + 1)], router[:, c * P:(c + 1) * P],
                                            ident32[0:E + 1, 0:E + 1])
                last.then_inc(s_turned, 1)

        def split(eng, part, fill, bank, dst):
            if part == 0:
                eng.wait_ge(s_turned, fill + 1)
                eng.activation(dst[0], bank, ACT.Copy, scale=W_SCALE).then_inc(s_high, 1)
            else:
                eng.wait_ge(s_high, fill + 1)
                eng.scalar_tensor_tensor(dst[1], bank, W_SCALE, dst[0], ALU.mult, ALU.subtract).then_inc(s_low, 1)

        def split_all(eng, part):
            def expert(e, half):
                for c in range(DB):
                    split(eng, part, e * EACH + c, banks[half * EACH + c][:, 0:2 * I],
                          [w[:, c, bass.ds(e * (2 * I), 2 * I)] for w in gu_t])
                split(eng, part, e * EACH + DB, banks[half * EACH + DB][0:HB, 0:NHB * D],
                      [w[:, bass.ds(e, 1)].rearrange("p e n -> p (e n)") for w in dn_t])

            with eng.Fori(0, E // 2) as ee:
                for half in range(2):
                    expert(ee * 2 + half, half)
            for i, (kind, a, n) in enumerate(rest):
                fill = E * EACH + i
                dst = [dict(sgu=sgu_t[s], sdn=sdn_t[s], router=router_t[s]) for s in range(2)]
                parts = [rest_parts(kind, a, n, banks[fill % BANKS], d) for d in dst]
                split(eng, part, fill, parts[0][0], [x[1] for x in parts])

        @block.scalar
        def _(act):
            split_all(act, 0)

        @block.vector
        def _(dve):
            split_all(dve, 1)


def experts_block(nc, rows_dram, hidden_dram, counts, places, choices, gu_t, dn_t, ident16, SLOT_TILES, U, REGION,
                  UP_SCALE, H_SCALE, DOWN_SCALE):
    fp32, fp16, i32 = mybir.dt.float32, mybir.dt.float16, mybir.dt.int32
    ALU, ACT, AX = mybir.AluOpType, mybir.ActivationFunctionType, mybir.AxisListType
    P = 128
    DB = gu_t[0].shape[1]
    D = DB * P
    E = counts.shape[1]
    I2 = gu_t[0].shape[2] // E
    HB = dn_t[0].shape[0]
    NHB = I2 // 2 // HB
    MOST = (REGION - P) // P
    PASSES = SLOT_TILES // U
    SPLIT = ((0, 0), (0, 1), (1, 0))

    ctx = ExitStack()
    with ctx:
        def sb(name, shape, dt):
            return ctx.enter_context(nc.sbuf_tensor(name, shape, dt))

        def pb(name):
            return ctx.enter_context(nc.psum_tensor(name, [P, 512], fp32))

        def sem(name):
            return ctx.enter_context(nc.semaphore(name))

        thresholds = sb("thresholds", [P, E, MOST], fp32)
        fuller = sb("fuller", [P, E, MOST], fp32)
        not_after = sb("not_after", [P, E, E], fp32)
        ahead = sb("ahead", [P, E, E], fp32)
        tiles, ends = sb("tiles", [P, E], fp32), sb("ends", [P, E], fp32)
        shift = sb("shift", [P, E], fp32)
        expert_ids = sb("e_expert_ids", [P, E], fp32)
        is_choice = sb("is_choice", [P, places.shape[1], E], fp32)
        moved = sb("moved", [P, places.shape[1]], fp32)
        slot_ids = sb("slot_ids", [1, SLOT_TILES], fp32)
        past = sb("past", [1, SLOT_TILES, E], fp32)
        expert_of, first_of = sb("expert_of", [1, SLOT_TILES], fp32), sb("first_of", [1, SLOT_TILES], fp32)
        experts = sb("experts", [1, SLOT_TILES], i32)
        slot_rows = sb("slot_rows", [1, SLOT_TILES], i32)

        x_in = sb("e_x_in", [P, U, 2 * D], fp16)
        xt = sb("e_xt", [P, 2, 2, DB, P], fp16)
        silu = sb("e_silu", [HB, 2, NHB * P], fp32)
        h = sb("e_h", [HB, 2, NHB * P], fp32)
        h_hi, h_lo = sb("e_h_hi", [HB, U, NHB, P], fp16), sb("e_h_lo", [HB, U, NHB, P], fp16)
        y = sb("e_y", [P, U, D], fp32)
        turned = [pb("e_turned0"), pb("e_turned1")]
        gu, yb = [pb("e_gu0"), pb("e_gu1")], [pb("e_y0"), pb("e_y1")]

        s_const, s_plan, s_planned = sem("e_const"), sem("e_plan"), sem("e_planned")
        s_in, s_out = [sem(f"e_in{u}") for u in range(U)], [sem(f"e_out{u}") for u in range(U)]
        s_turned, s_xt, s_gu, s_silu = sem("e_turned"), sem("e_xt"), sem("e_gu"), sem("e_silu")
        s_h, s_h_hi, s_h_lo, s_down, s_y = sem("e_h"), sem("e_h_hi"), sem("e_h_lo"), sem("e_down"), sem("e_y")

        block = ctx.enter_context(nc.Block(name="experts"))

        @block.gpsimd
        def _(pool):
            iota = dict(channel_multiplier=0, allow_small_or_imprecise_dtypes=True)
            pool.iota(thresholds[:], pattern=[[0, E], [P, MOST]], base=0, **iota).then_inc(s_const, 1)
            pool.iota(expert_ids[:], pattern=[[1, E]], base=0, **iota).then_inc(s_const, 1)
            pool.iota(slot_ids[:], pattern=[[1, SLOT_TILES]], base=0, **iota).then_inc(s_const, 1)
            pool.memset(not_after[:], 1.0).then_inc(s_const, 1)
            pool.wait_ge(s_const, 4)
            pool.affine_select(out=not_after[:], in_=not_after[:], compare_op=ALU.is_ge, fill=0.0, base=0,
                               pattern=[[1, E], [-1, E]], channel_multiplier=0).then_inc(s_const, 1)

        @block.vector
        def _(dve):
            done = [0]

            def link(ins):
                done[0] += 1
                ins.then_inc(s_plan, 1)
                dve.wait_ge(s_plan, done[0])

            dve.wait_ge(s_const, 5)
            link(dve.tensor_tensor(fuller[:], counts[:].unsqueeze(2).broadcast_to([P, E, MOST]), thresholds[:], ALU.is_gt))
            link(dve.tensor_reduce(tiles[:], fuller[:], AX.X, ALU.add))
            link(dve.tensor_tensor(ahead[:], tiles[:].unsqueeze(1).broadcast_to([P, E, E]), not_after[:], ALU.mult))
            link(dve.tensor_reduce(ends[:], ahead[:], AX.X, ALU.add))
            link(dve.tensor_tensor(past[:], ends[0:1].unsqueeze(1).broadcast_to([1, SLOT_TILES, E]),
                                   slot_ids[:].unsqueeze(2).broadcast_to([1, SLOT_TILES, E]), ALU.is_le))
            link(dve.tensor_reduce(expert_of[:], past[:], AX.X, ALU.add))
            link(dve.tensor_tensor(past[:], past[:], tiles[0:1].unsqueeze(1).broadcast_to([1, SLOT_TILES, E]), ALU.mult))
            link(dve.tensor_reduce(first_of[:], past[:], AX.X, ALU.add))
            link(dve.tensor_tensor(first_of[:], slot_ids[:], first_of[:], ALU.subtract))
            link(dve.tensor_scalar(first_of[:], first_of[:], float(P), None, ALU.mult))
            link(dve.scalar_tensor_tensor(first_of[:], expert_of[:], float(REGION), first_of[:], ALU.mult, ALU.add))
            link(dve.tensor_copy(slot_rows[:], first_of[:]))
            link(dve.tensor_scalar(expert_of[:], expert_of[:], float(E - 1), None, ALU.min))
            dve.tensor_copy(experts[:], expert_of[:]).then_inc(s_planned, 1)

            def move_places():
                link(dve.tensor_tensor(shift[:], ends[:], tiles[:], ALU.subtract))
                link(dve.tensor_scalar(shift[:], shift[:], float(P), None, ALU.mult))
                link(dve.scalar_tensor_tensor(shift[:], expert_ids[:], -float(REGION), shift[:], ALU.mult, ALU.add))
                T = places.shape[1]
                link(dve.tensor_tensor(is_choice[:], choices[:].unsqueeze(2).broadcast_to([P, T, E]),
                                       expert_ids[:].unsqueeze(1).broadcast_to([P, T, E]), ALU.is_equal))
                link(dve.tensor_tensor(is_choice[:], is_choice[:], shift[:].unsqueeze(1).broadcast_to([P, T, E]), ALU.mult))
                link(dve.tensor_reduce(moved[:], is_choice[:], AX.X, ALU.add))
                link(dve.tensor_tensor(places[:], places[:], moved[:], ALU.add))

            def copy_xt(n, u):
                dve.wait_ge(s_turned, n + 1)
                dve.tensor_copy(xt[:, u % 2].rearrange("p s c n -> p (s c n)"),
                                turned[u % 2][:, :].bitcast(fp16)[:, 0:2 * D]).then_inc(s_xt, 1)

            def hidden(n, u):
                dve.wait_ge(s_silu, n + 1)
                dve.scalar_tensor_tensor(h[:, u % 2], gu[u % 2][0:HB, NHB * P:2 * NHB * P], UP_SCALE * H_SCALE,
                                         silu[:, u % 2], ALU.mult, ALU.mult).then_inc(s_h, 1)

            def low(n, u):
                dve.wait_ge(s_h_hi, n + 1)
                dve.tensor_tensor(h_lo[:, u].rearrange("p b n -> p (b n)"), h[:, u % 2],
                                  h_hi[:, u].rearrange("p b n -> p (b n)"), ALU.subtract).then_inc(s_h_lo, 1)

            for n in range(3):
                copy_xt(n, n)
            for n in range(2):
                hidden(n, n)
                low(n, n)

            def tile(n, u, i=None):
                if i is None or i + 3 < SLOT_TILES:
                    copy_xt(n + 3, (u + 3) % U)
                if i is None or i + 2 < SLOT_TILES:
                    hidden(n + 2, (u + 2) % U)
                    low(n + 2, (u + 2) % U)

            with dve.Fori(0, PASSES - 1) as q:
                for u in range(U):
                    tile(q * U + u, u)
            for u in range(U):
                tile((PASSES - 1) * U + u, u, (PASSES - 1) * U + u)
            move_places()

        @block.sync
        def _(sp):
            sp.wait_ge(s_planned, 1)

            def rows_at(i):
                return sp.value_load(slot_rows[0:1, i], min_val=0, max_val=rows_dram.shape[0] - P)

            def load(n, u, row):
                if not isinstance(n, int):
                    sp.wait_ge(s_turned, n - (U - 1))
                sp.dma_start(x_in[:, u], rows_dram[bass.ds(row, P), :]).then_inc(s_in[u], 16)

            def store(n, u):
                sp.wait_ge(s_y, n + 1)
                sp.dma_start(hidden_dram[bass.ds(n * P, P), :], y[:, u]).then_inc(s_out[u], 16)

            for u in range(U):
                load(u, u, rows_at(bass.ds(u, 1)))
            with sp.Fori(0, PASSES - 1) as q:
                for u in range(U):
                    load(q * U + (u + U), u, rows_at(bass.ds(q * U + (u + U), 1)))
                    store(q * U + u, u)
            for u in range(U):
                store((PASSES - 1) * U + u, u)
            for u in range(U):
                sp.wait_ge(s_out[u], 16 * PASSES)

        @block.scalar
        def _(act):
            def gate(n, u):
                act.wait_ge(s_gu, n + 1)
                act.activation(silu[:, u % 2], gu[u % 2][0:HB, 0:NHB * P], ACT.Silu, scale=UP_SCALE).then_inc(s_silu, 1)
                act.wait_ge(s_h, n + 1)
                act.activation(h_hi[:, u].rearrange("p b n -> p (b n)"), h[:, u % 2], ACT.Copy).then_inc(s_h_hi, 1)

            for n in range(2):
                gate(n, n)

            def tile(n, u, q, i=None):
                if i is None or i + 2 < SLOT_TILES:
                    gate(n + 2, (u + 2) % U)
                act.wait_ge(s_down, n + 1)
                if not (isinstance(q, int) and q == 0):
                    act.wait_ge(s_out[u], q * 16)
                act.activation(y[:, u], yb[u % 2][:, 0:D], ACT.Copy, scale=DOWN_SCALE).then_inc(s_y, 1)

            for u in range(U):
                tile(u, u, 0)
            with act.Fori(1, PASSES - 1) as q:
                for u in range(U):
                    tile(q * U + u, u, q)
            for u in range(U):
                n = (PASSES - 1) * U + u
                tile(n, u, PASSES - 1, n)

        @block.tensor
        def _(pe):
            pe.wait_ge(s_planned, 1)

            def expert_at(i):
                return pe.value_load(experts[0:1, i], min_val=0, max_val=E - 1)

            def transposes(n, u, p):
                pe.wait_ge(s_in[u], p * 16 + 16)
                if not isinstance(n, int) or n >= 2:
                    pe.wait_ge(s_xt, n - 1)
                for i in range(2 * DB):
                    last = pe.transpose(turned[u % 2][:, :].bitcast(fp16)[:, i * P:(i + 1) * P],
                                        x_in[:, u, i * P:(i + 1) * P], ident16[:])
                last.then_inc(s_turned, 1)

            def up(n, u, e):
                pe.wait_ge(s_xt, n + 1)
                if not isinstance(n, int) or n >= 2:
                    pe.wait_ge(s_h, n - 1)
                for b in range(2 * NHB):
                    k = 0
                    for c in range(DB):
                        for w, a in SPLIT:
                            last = pe.matmul(gu[u % 2][0:HB, b * P:(b + 1) * P],
                                             gu_t[w][:, c, bass.ds(e * I2 + b * HB, HB)], xt[:, u % 2, a, c],
                                             start=k == 0, stop=k == 3 * DB - 1)
                            k += 1
                last.then_inc(s_gu, 1)

            def down(n, u, e):
                pe.wait_ge(s_h_lo, n + 1)
                if not isinstance(n, int) or n >= 2:
                    pe.wait_ge(s_y, n - 1)
                k = 0
                for b in range(NHB):
                    for a, w in SPLIT:
                        last = pe.matmul(yb[u % 2][:, 0:D], (h_hi, h_lo)[a][:, u, b],
                                         dn_t[w][:, bass.ds(e, 1), b * D:(b + 1) * D].rearrange("p e n -> p (e n)"),
                                         start=k == 0, stop=k == 3 * NHB - 1)
                        k += 1
                last.then_inc(s_down, 1)

            def tile(n, u, q, i=None):
                if i is None or i + 3 < SLOT_TILES:
                    transposes(n + 3, (u + 3) % U, q + (u + 3) // U)
                if i is None or i + 2 < SLOT_TILES:
                    up(n + 2, (u + 2) % U, expert_at(bass.ds(n + 2, 1)))
                down(n, u, expert_at(bass.ds(n, 1)))

            for n in range(3):
                transposes(n, n, 0)
                if n < 2:
                    up(n, n, expert_at(bass.ds(n, 1)))
            for u in range(U):
                tile(u, u, 0)
            with pe.Fori(1, PASSES - 1) as q:
                for u in range(U):
                    tile(q * U + u, u, q)
            for u in range(U):
                n = (PASSES - 1) * U + u
                tile(n, u, PASSES - 1, n)


def combine_block(nc, base_dram, hidden_dram, places, shares, out, TILES, TOPK):
    fp32, u32 = mybir.dt.float32, mybir.dt.uint32
    ALU = mybir.AluOpType
    P, GT = 128, 4
    D = out.shape[2]
    GROUPS = TILES // GT
    W = GT * TOPK

    ctx = ExitStack()
    with ctx:
        def sb(name, shape, dt):
            return ctx.enter_context(nc.sbuf_tensor(name, shape, dt))

        def sem(name):
            return ctx.enter_context(nc.semaphore(name))

        place, share = sb("c_place", [P, 2, W], u32), sb("c_share", [P, 2, W], fp32)
        got = sb("c_got", [P, 2, GT, TOPK, D], fp32)
        acc = sb("c_acc", [P, 2, GT, D], fp32)
        s_place, s_share = sem("c_place_s"), sem("c_share_s")
        s_got = [[sem(f"c_got{h}{t}") for t in range(GT)] for h in range(2)]
        s_base, s_sum, s_out = [sem("c_base0"), sem("c_base1")], sem("c_sum"), [sem("c_out0"), sem("c_out1")]
        s_link, s_passed = sem("c_link"), sem("c_passed")

        rows = lambda a: a.rearrange("b (t p) d -> p (b t) d", p=P)
        base_rows, out_rows = rows(base_dram), rows(out)
        block = ctx.enter_context(nc.Block(name="combine"))

        @block.sync
        def _(sp):
            def load(g, half):
                sp.dma_start(acc[:, half], base_rows[:, bass.ds(g * GT, GT)]).then_inc(s_base[half], 16)

            def store(g, half):
                sp.wait_ge(s_sum, (g + 1) * GT)
                sp.dma_start(out_rows[:, bass.ds(g * GT, GT)], acc[:, half]).then_inc(s_out[half], 16)

            for half in range(2):
                load(half, half)
            if GROUPS > 2:
                with sp.Fori(0, GROUPS // 2 - 1) as gg:
                    for half in range(2):
                        store(gg * 2 + half, half)
                        sp.wait_ge(s_out[half], gg * 16 + 16)
                        load(gg * 2 + (half + 2), half)
            for half in range(2):
                store(GROUPS - 2 + half, half)
            for half in range(2):
                sp.wait_ge(s_out[half], 16 * GROUPS // 2)

        def each_group(eng, group):
            for half in range(2):
                group(half, half, 0)
            if GROUPS > 2:
                with eng.Fori(1, GROUPS // 2) as gg:
                    for half in range(2):
                        group(gg * 2 + half, half, gg)

        @block.gpsimd
        def _(pool):
            def group(g, half, gg):
                pool.wait_ge(s_place, g + 1)
                pool.sem_inc(s_passed, 1)
                for t in range(GT):
                    for k in range(TOPK):
                        i = t * TOPK + k
                        pool.indirect_dma_start(got[:, half, t, k], None, hidden_dram,
                                                bass.IndirectOffsetOnAxis(ap=place[:, half, i:i + 1], axis=0))\
                            .then_inc(s_got[half][t], 16)

            each_group(pool, group)

        @block.vector
        def _(dve):
            def places_of(g, half, gg):
                cols = bass.ds(g * W, W)
                dve.tensor_copy(place[:, half], places[:, cols]).then_inc(s_place, 1)
                dve.tensor_copy(share[:, half], shares[:, cols]).then_inc(s_share, 1)

            def group(g, half, gg):
                dve.wait_ge(s_base[half], gg * 16 + 16)
                for k in range(TOPK):
                    for t in range(GT):
                        if k == 0:
                            dve.wait_ge(s_got[half][t], gg * (16 * TOPK) + 16 * TOPK)
                        i = t * TOPK + k
                        ins = dve.scalar_tensor_tensor(acc[:, half, t], got[:, half, t, k], share[:, half, i:i + 1],
                                                       acc[:, half, t], ALU.mult, ALU.add)
                        ins.then_inc(s_sum if k == TOPK - 1 else s_link, 1)
                    if k < TOPK - 1:
                        dve.wait_ge(s_link, g * (GT * (TOPK - 1)) + (k + 1) * GT)

            for half in range(2):
                places_of(half, half, 0)
            dve.wait_ge(s_share, 2)
            for half in range(2):
                group(half, half, 0)
                if GROUPS > 2:
                    dve.wait_ge(s_sum, (half + 1) * GT)
                    places_of(half + 2, half, 1)
                    dve.wait_ge(s_share, half + 3)
            if GROUPS > 4:
                with dve.Fori(1, GROUPS // 2 - 1) as gg:
                    for half in range(2):
                        g = gg * 2 + half
                        group(g, half, gg)
                        dve.wait_ge(s_sum, (g + 1) * GT)
                        places_of(g + 2, half, gg + 1)
                        dve.wait_ge(s_share, g + 3)
            if GROUPS > 2:
                for half in range(2):
                    group(GROUPS - 2 + half, half, GROUPS // 2 - 1)


_INS = ['L0_attn_x', 'L0_attn_Wq', 'L0_attn_Wkv', 'L0_attn_Wo', 'L0_ffn_gate_w', 'L0_ffn_expert_gate_up',
        'L0_ffn_expert_down', 'L0_ffn_shared_gate_up', 'L0_ffn_shared_down', 'L0_ffn_shared_gate_vec']


def layer(nc, x, w_q, w_kv, w_o, gate_w, gate_up, down, shared_gate_up, shared_down, shared_gate, rope, out):
    P = 128
    n_seq, seq, D = x.shape
    E, K, U = gate_w.shape[0], 4, 4
    tokens = n_seq * seq
    region = tokens + P
    slot_tiles = -(-(tokens * K // P + E) // U) * U
    spare = slot_tiles - tokens * K // P
    x1 = nc.dram_tensor("x1_scratch", [n_seq, seq, D], mybir.dt.float32).ap()
    base = nc.dram_tensor("base_scratch", [n_seq, seq, D], mybir.dt.float32).ap()
    rows = nc.dram_tensor("rows_scratch", [E * region + spare * P, 2 * D], mybir.dt.float16).ap()
    hidden = nc.dram_tensor("hidden_scratch", [slot_tiles * P, D], mybir.dt.float32).ap()
    attention_block(nc, x, w_q, w_kv, w_o, rope, x1, n_seq)
    moe_blocks(nc, x1, gate_w, gate_up, down, shared_gate_up, shared_down, shared_gate, rows, hidden, base, out, n_seq)


def _rope_table(seq, width):
    import numpy as np

    one, base = np.float32(1.0), np.float32(10000.0)
    frequencies = one / base ** (np.arange(0, width, 2, dtype=np.float32) / np.float32(width))
    angles = np.arange(seq, dtype=np.float32)[:, None] * frequencies[None, :]
    cos, sin = np.cos(angles), np.sin(angles)
    table = np.stack([np.concatenate([cos, cos], -1), np.concatenate([sin, -sin], -1)], axis=1)
    return (table * np.float32(2.0 ** -8)).astype(np.float32)


def kernel(**inputs):
    import numpy as _np
    import concourse.bacc as _bacc
    from concourse import mybir as _mybir
    from concourse.bass_utils import run_bass_kernel_spmd as _run

    nc = _bacc.Bacc("TRN2", target_bir_lowering=False, num_devices=1)
    arrays, args = {}, []
    for name in _INS:
        a = _np.ascontiguousarray(inputs[name])
        arrays[f"in_{name}_dram"] = a
        args.append(nc.dram_tensor(f"in_{name}_dram", a.shape, _mybir.dt.from_np(a.dtype), kind="ExternalInput").ap())
    shape = tuple(inputs['L0_attn_x'].shape)
    table = _rope_table(shape[1], 64)
    arrays["in_rope_dram"] = table
    args.append(nc.dram_tensor("in_rope_dram", table.shape, _mybir.dt.float32, kind="ExternalInput").ap())
    args.append(nc.dram_tensor("out_0_dram", shape, _mybir.dt.float32, kind="ExternalOutput").ap())
    layer(nc, *args)
    r = _run(nc, [arrays], core_ids=[0])
    return r.results[0]["out_0_dram"]
```

```python
import concourse.bass as bass
from concourse import mybir
from contextlib import ExitStack


def attention_block(nc, x, w_q, w_kv, w_o, rope, x1_dram, x1_moments, n_seq):
    fp32, fp16, bf16 = mybir.dt.float32, mybir.dt.float16, mybir.dt.bfloat16
    ALU, ACT, AX = mybir.AluOpType, mybir.ActivationFunctionType, mybir.AxisListType

    P = 128
    SEQ, D = x.shape[1], x.shape[2]
    DH = rope.shape[2]
    HALF = DH // 2
    TT = SEQ // P
    DB = D // P
    HQ = w_q.shape[1] // DH
    HK = w_kv.shape[1] // DH // 2
    G = HQ // HK
    KVS = 2
    QS = KVS * G
    STEPS = HK // KVS
    RH = QS + KVS
    NQ, NKV = QS * DH, 2 * KVS * DH
    UNITS = 6
    KT = STEPS * G

    X_SCALE, W_SCALE, QK_SCALE, O_SCALE = 2.0 ** 5, 2.0 ** 9, 2.0 ** 6, 2.0 ** 6
    ROPE_SCALE = QK_SCALE / (X_SCALE * W_SCALE)
    V_SCALE = O_SCALE / (X_SCALE * W_SCALE)
    SOFTMAX_SCALE = DH ** -0.5 / (QK_SCALE * QK_SCALE)
    OUT_SCALE = 1.0 / (O_SCALE * W_SCALE)
    EPS = 1e-5
    MASKED = -1e30
    assert rope.shape[1] == 2 and ROPE_SCALE == 2.0 ** -8

    ctx = ExitStack()
    with ctx:
        def sb(name, shape, dt):
            return ctx.enter_context(nc.sbuf_tensor(name, shape, dt))

        def pb(name):
            return ctx.enter_context(nc.psum_tensor(name, [P, 512], fp32))

        def sem(name):
            return ctx.enter_context(nc.semaphore(name))

        wq_stage = sb("wq_stage", [P, DB, HQ * DH], fp32)
        wkv_stage = sb("wkv_stage", [P, DB, 2 * HK * DH], fp32)
        wo_stage = sb("wo_stage", [P, KT, D], fp32)
        wq_hi, wq_lo = sb("wq_hi", [P, DB, HQ * DH], fp16), sb("wq_lo", [P, DB, HQ * DH], fp16)
        wkv_hi, wkv_lo = sb("wkv_hi", [P, DB, 2 * HK * DH], fp16), sb("wkv_lo", [P, DB, 2 * HK * DH], fp16)
        wo_hi, wo_lo = sb("wo_hi", [P, KT, D], fp16), sb("wo_lo", [P, KT, D], fp16)
        table = sb("table", [P, TT, 2, DH], fp32)
        ident32 = sb("ident32", [P, P], fp32)
        ident16 = sb("ident16", [P, P], fp16)
        identb = sb("identb", [P, P], bf16)
        causal = sb("causal", [P, 4, P], bf16)
        x_in = sb("x_in", [P, TT, D], fp32)
        x_res = sb("x_res", [P, TT, D], fp32)
        x_out = sb("x_out", [P, TT, D], fp32)
        x1_stats, x1_pair = sb("x1_stats", [P, TT, 6], fp32), sb("x1_pair", [P, TT, 2], fp32)
        stats = sb("stats", [P, TT, 6], fp32)
        moments = sb("moments", [P, TT, 2], fp32)
        eps = sb("eps", [P, 1], fp32)
        log_var, rough = sb("log_var", [P, TT], fp32), sb("rough", [P, TT], fp32)
        correction, rstd = sb("correction", [P, TT], fp32), sb("rstd", [P, TT], fp32)
        xn = sb("xn", [P, TT, D], fp32)
        xn_hi, xn_lo = sb("xn_hi", [P, TT, D], fp16), sb("xn_lo", [P, TT, D], fp16)
        xn_t = sb("xn_t", [P, TT, 2, DB, P], fp16)
        products = sb("products", [P, TT, 2, RH * DH], fp32)
        rotated = sb("rotated", [P, TT, RH * DH], fp32)
        stacked = sb("stacked", [P, TT, RH + KVS, 2, DH], fp16)
        q_t = sb("q_t", [P, 2, TT, QS, P], fp16)
        k_t = sb("k_t", [P, 2, 2, KVS, TT, P], fp16)
        values = sb("values", [P, STEPS, TT, KVS * DH], fp32)
        negmax = sb("negmax", [P, UNITS, G], fp32)
        bias = sb("bias", [P, UNITS, G], fp32)
        sums = sb("sums", [P, UNITS, G], fp32)
        inverse = sb("inverse", [P, UNITS, G], fp32)
        probs = sb("probs", [P, UNITS, 512], fp32)
        pt0 = sb("pt0", [P, KVS, G, P], fp32)
        pt1 = sb("pt1", [P, KVS, TT, G, P], fp32)
        o_hi, o_lo = sb("o_hi", [P, STEPS, G, SEQ], fp16), sb("o_lo", [P, STEPS, G, SEQ], fp16)

        scores = [pb(f"scores{i}") for i in range(3)]
        proj = ctx.enter_context(nc.psum_tensor("proj", [P, 1024], fp32))
        ring = [pb("ring0"), pb("ring1")]
        heads_out = pb("heads_out")

        s_wq, s_wkv, s_wo, s_table = sem("s_wq"), sem("s_wkv"), sem("s_wo"), sem("s_table")
        s_const = sem("s_const")
        s_w_hi, s_w_lo = sem("s_w_hi"), sem("s_w_lo")
        s_x, s_res, s_stored = sem("s_x"), sem("s_res"), sem("s_stored")
        s_stat, s_moments, s_rstd = sem("s_stat"), sem("s_moments"), sem("s_rstd")
        s_eps, s_rough = sem("s_eps"), sem("s_rough")
        s_x1_stat, s_x1_pair, s_x1_moments = sem("s_x1_stat"), sem("s_x1_pair"), sem("s_x1_moments")
        s_passed = sem("s_passed")
        s_xn, s_xn_hi, s_xn_lo = sem("s_xn"), sem("s_xn_hi"), sem("s_xn_lo")
        s_proj, s_mult, s_vals = sem("s_proj"), sem("s_mult"), sem("s_vals")
        s_rot, s_hi, s_lo, s_swap = sem("s_rot"), sem("s_hi"), sem("s_lo"), sem("s_swap")
        s_full = [sem("s_full0"), sem("s_full1")]
        s_free = [sem("s_free0"), sem("s_free1")]
        s_scores, s_max, s_bias = sem("s_scores"), sem("s_max"), sem("s_bias")
        s_exp, s_recip, s_norm = sem("s_exp"), sem("s_recip"), sem("s_norm")
        s_heads, s_o_hi, s_o_lo = sem("s_heads"), sem("s_o_hi"), sem("s_o_lo")
        s_wo_mm, s_x1 = sem("s_wo_mm"), sem("s_x1")

        unit = [(0, 0, 0, G, P), (1, 0, 0, G, P)] + \
               [(j, 1, 2 * h, 2, SEQ) for j in range(KVS) for h in range(2)]

        LN_STEP = 1

        def ring_order(last):
            uses = []
            for p in range(STEPS):
                more = not (last and p == STEPS - 1)
                names = ["P0"] + (["T0", "T1", "T2"] if more else []) + ["P1", "P2", "P3"] + \
                    (["L0", "L1"] if p == LN_STEP and not last else []) + ["P4", "P5"]
                uses += [(p, n) for n in names]
            return uses

        RING_FIRST = ["L0", "L1", "T0", "T1", "T2"]
        RING_USES, RING_LAST = ring_order(False), ring_order(True)
        PER_BANK = len(RING_USES) // 2
        assert len(RING_USES) % 2 == 0

        def ring_use(b, p, name, back=0):
            if p < 0:
                i = RING_FIRST.index(name)
                return i % 2, i // 2 + 1
            uses = RING_LAST if isinstance(b, int) and b - back == n_seq - 1 else RING_USES
            i = uses.index((p, name))
            before = (len(RING_FIRST) + 1 - i % 2) // 2
            return i % 2, b * PER_BANK + (before + i // 2 + 1 - back * PER_BANK)

        def filled(eng, b, p, name):
            bank, n = ring_use(b, p, name)
            eng.wait_ge(s_full[bank], n)
            return ring[bank], s_free[bank]

        def emptied(eng, b, p, name, back=0):
            bank, n = ring_use(b, p, name, back)
            eng.wait_ge(s_free[bank], n)

        def previous_ring_use(pe, b, p, name):
            bank, n = ring_use(b, p, name)
            if not isinstance(n, int) or n > 1:
                pe.wait_ge(s_free[bank], n - 1)
            return ring[bank], s_full[bank]

        def per_step(b, p, each, n):
            return b * (STEPS * each) + (p * each + n)

        block = ctx.enter_context(nc.Block(name="attention"))

        @block.sync
        def _(sp):
            sp.dma_start(wq_stage[:], w_q.rearrange("(c p) n -> p c n", p=P)).then_inc(s_wq, 16)
            sp.dma_start(x_in[:], x[0].rearrange("(t p) d -> p t d", p=P)).then_inc(s_x, 16)
            sp.dma_start(wkv_stage[:], w_kv.rearrange("(c p) n -> p c n", p=P)).then_inc(s_wkv, 16)
            sp.dma_start(table[:], rope.rearrange("(t p) c d -> p t c d", p=P)).then_inc(s_table, 16)
            wo_rows = w_o.rearrange("(s j g d) n -> j s d g n", j=KVS, g=G, d=DH)
            for j in range(KVS):
                for s in range(STEPS):
                    sp.dma_start(wo_stage[j * DH:(j + 1) * DH, s * G:(s + 1) * G, :],
                                 wo_rows[j, s]).then_inc(s_wo, 16)

            sp.dma_start(x_res[:], x[0].rearrange("(t p) d -> p t d", p=P)).then_inc(s_res, 16)

            def store(b, count):
                sp.wait_ge(s_x1, count)
                sp.dma_start(x1_dram[b].rearrange("(t p) d -> p t d", p=P), x_out[:]).then_inc(s_stored, 16)

            def load_next(b):
                sp.wait_ge(s_xn, b + 1)
                sp.dma_start(x_in[:], x[b + 1].rearrange("(t p) d -> p t d", p=P)).then_inc(s_x, 16)

            def load_residual(b):
                sp.dma_start(x_res[:], x[b].rearrange("(t p) d -> p t d", p=P)).then_inc(s_res, 16)

            if n_seq > 1:
                load_next(0)
            if n_seq > 2:
                with sp.Fori(1, n_seq - 1) as b:
                    load_next(b)
                    store(b - 1, b)
                    load_residual(b)
            if n_seq > 1:
                store(n_seq - 2, n_seq - 1)
                load_residual(n_seq - 1)
            store(n_seq - 1, n_seq)
            sp.wait_ge(s_stored, 16 * n_seq)

        @block.gpsimd
        def _(pool):
            pool.memset(eps[:], EPS).then_inc(s_eps, 1)
            for m in (ident32, ident16, identb, causal):
                pool.memset(m[:], 0.0).then_inc(s_const, 1)
            pool.wait_ge(s_const, 4)
            for m in (ident32, ident16, identb):
                pool.affine_select(out=m[:], in_=m[:], compare_op=ALU.not_equal, fill=1.0, base=0,
                                   pattern=[[-1, P]], channel_multiplier=1).then_inc(s_const, 1)
            pool.affine_select(out=causal[:], in_=causal[:], compare_op=ALU.is_ge, fill=MASKED, base=0,
                               pattern=[[0, 4], [-1, P]], channel_multiplier=1).then_inc(s_const, 1)

            def rotate(b, p, t):
                pool.wait_ge(s_mult, per_step(b, p, TT, t + 1))
                halves = products[:, t].rearrange("p c (h a d) -> p c h a d", a=2, d=HALF)
                out = rotated[:, t].rearrange("p (h a d) -> p h a d", a=2, d=HALF)
                for a in range(2):
                    pool.tensor_tensor(out[:, :, a], halves[:, 0, :, a], halves[:, 1, :, 1 - a],
                                       ALU.add).then_inc(s_rot, 1)

            def low_parts(b, p, t):
                pool.wait_ge(s_hi, per_step(b, p, TT, t + 1))
                pool.wait_ge(s_rot, per_step(b, p, 2 * TT, 2 * t + 2))
                whole = rotated[:, t].rearrange("p (h d) -> p h d", d=DH)
                pool.tensor_tensor(stacked[:, t, 0:RH, 1], whole, stacked[:, t, 0:RH, 0],
                                   ALU.subtract).then_inc(s_lo, 1)

            def normalize(b, p, u):
                pool.wait_ge(s_recip, per_step(b, p, UNITS, u + 1))
                heads, keys = unit[u][3:]
                pr = probs[:, u].rearrange("p (h k) -> p h k", k=keys)
                pool.tensor_tensor(pr, pr, inverse[:, u, 0:heads].unsqueeze(2).broadcast_to(
                    [P, heads, keys]), ALU.mult).then_inc(s_norm, 1)

            def step(b, p, last):
                one, two = not last or p + 1 < STEPS, not last or p + 2 < STEPS
                normalize(b, p, 3)
                if two:
                    rotate(b, p + 2, 0)
                normalize(b, p, 4)
                normalize(b, p, 5)
                if two:
                    low_parts(b, p + 2, 0)
                    rotate(b, p + 2, 1)
                if one:
                    normalize(b, p + 1, 0)
                if two:
                    low_parts(b, p + 2, 1)
                if one:
                    normalize(b, p + 1, 1)
                    normalize(b, p + 1, 2)

            for p in range(2):
                for t in range(TT):
                    rotate(0, p, t)
                    low_parts(0, p, t)
            for u in range(3):
                normalize(0, 0, u)
            if n_seq > 1:
                with pool.Fori(0, n_seq - 1) as b:
                    for p in range(STEPS):
                        step(b, p, False)
            for p in range(STEPS):
                step(n_seq - 1, p, True)

        @block.scalar
        def _(act):
            def rough_rstd(b):
                act.wait_ge(s_moments, TT * b + TT)
                act.activation(log_var[:], moments[:, :, 1], ACT.Ln, bias=eps[:]).then_inc(s_rough, 1)
                act.wait_ge(s_rough, 2 * b + 1)
                act.activation(rough[:], log_var[:], ACT.Exp, scale=-0.5).then_inc(s_rough, 1)

            def high_xn(b):
                act.wait_ge(s_xn, b + 1)
                act.activation(xn_hi[:], xn[:], ACT.Copy, scale=X_SCALE).then_inc(s_xn_hi, 1)

            act.preload_act_table_set("natural_log_exp_and_others")
            act.wait_ge(s_eps, 1)
            rough_rstd(0)
            high_xn(0)
            act.wait_ge(s_wq, 16)
            act.activation(wq_hi[:], wq_stage[:], ACT.Copy, scale=W_SCALE).then_inc(s_w_hi, 1)
            act.wait_ge(s_wkv, 16)
            act.activation(wkv_hi[:], wkv_stage[:], ACT.Copy, scale=W_SCALE).then_inc(s_w_hi, 1)
            act.wait_ge(s_wo, 16 * KVS * STEPS)
            act.activation(wo_hi[:], wo_stage[:], ACT.Copy, scale=W_SCALE).then_inc(s_w_hi, 1)

            def copy_values(b, p, t):
                act.wait_ge(s_mult, per_step(b, p, TT, t + 1))
                act.activation(values[:, p % STEPS, t], proj[:, NQ + KVS * DH:NQ + NKV], ACT.Copy,
                               scale=V_SCALE).then_inc(s_vals, 1)

            def exps(b, p, u):
                heads, keys = unit[u][3:]
                act.wait_ge(s_max, per_step(b, p, UNITS, u + 1))
                act.activation(bias[:, u, 0:heads], negmax[:, u, 0:heads], ACT.Copy, scale=SOFTMAX_SCALE).then_inc(s_bias, 1)
                act.wait_ge(s_bias, per_step(b, p, UNITS, u + 1))
                for h in range(heads):
                    last = act.activation(probs[:, u, h * keys:(h + 1) * keys],
                                          scores[u % 3][:, h * keys:(h + 1) * keys], ACT.Exp,
                                          bias=bias[:, u, h:h + 1], scale=SOFTMAX_SCALE,
                                          accum_out=sums[:, u, h:h + 1])
                last.then_inc(s_exp, 1)

            def copy_ln(b, p, t):
                bank, free = filled(act, b, p, f"L{t}")
                act.activation(xn_t[:, t].rearrange("p s c n -> p (s c n)"),
                               bank[:, :].bitcast(fp16)[:, 0:2 * D], ACT.Copy).then_inc(free, 1)

            def copy_p0(b, p, u):
                bank, free = filled(act, b, p, f"P{u}")
                act.activation(pt0[:, u].rearrange("p g n -> p (g n)"), bank[:, :], ACT.Copy).then_inc(free, 1)

            def copy_p1(b, p, u):
                j, _, h, _, _ = unit[u]
                bank, free = filled(act, b, p, f"P{u}")
                act.activation(pt1[:, j, :, h:h + 2, :], bank[:, :].rearrange("p (t g n) -> p t g n", t=TT, g=2),
                               ACT.Copy).then_inc(free, 1)

            def copy_k_t(b, p):
                bank, free = filled(act, b, p, "T2")
                act.activation(k_t[:, (p + 1) % 2].rearrange("p a j t n -> p (a j t n)"),
                               bank[:, :].bitcast(fp16), ACT.Copy).then_inc(free, 1)

            def heads_hi(b, p, t):
                act.wait_ge(s_heads, per_step(b, p, TT, t + 1))
                act.activation(o_hi[:, p, :, t * P:(t + 1) * P],
                               heads_out[:, :].rearrange("p (g n) -> p g n", g=G), ACT.Copy).then_inc(s_o_hi, 1)

            def step(b, p, last):
                one, two = not last or p + 1 < STEPS, not last or p + 2 < STEPS
                copy_p0(b, p, 0)
                if p == 1 and not last:
                    high_xn(b + 1)
                if one:
                    copy_k_t(b, p)
                if p == 0 and not last:
                    rough_rstd(b + 1)
                if two:
                    copy_values(b, p + 2, 0)
                copy_p0(b, p, 1)
                exps(b, p, 5)
                if one:
                    exps(b, p + 1, 0)
                    exps(b, p + 1, 1)
                heads_hi(b, p, 0)
                copy_p1(b, p, 3)
                if one:
                    exps(b, p + 1, 2)
                if p == LN_STEP and not last:
                    copy_ln(b, p, 0)
                    copy_ln(b, p, 1)
                if two:
                    copy_values(b, p + 2, 1)
                copy_p1(b, p, 5)
                if one:
                    exps(b, p + 1, 3)
                    exps(b, p + 1, 4)
                heads_hi(b, p, 1)

            for t in range(TT):
                copy_ln(0, -1, t)
            for t in range(TT):
                copy_values(0, 0, t)
            for t in range(TT):
                copy_values(0, 1, t)
            copy_k_t(0, -1)
            for u in range(5):
                exps(0, 0, u)
            if n_seq > 1:
                with act.Fori(0, n_seq - 1) as b:
                    for p in range(STEPS):
                        step(b, p, False)
            for p in range(STEPS):
                step(n_seq - 1, p, True)

        @block.vector
        def _(dve):
            def norm_moments(b):
                dve.wait_ge(s_x, 16 * b + 16)
                for t in range(TT):
                    dve.bn_stats(stats[:, t], x_in[:, t]).then_inc(s_stat, 1)
                dve.wait_ge(s_stat, TT * b + TT)
                dve.sem_inc(s_passed, 1)
                for t in range(TT):
                    dve.bn_aggr(moments[:, t], stats[:, t]).then_inc(s_moments, 1)

            def norm_apply(b):
                dve.wait_ge(s_rough, 2 * b + 2)
                dve.tensor_tensor(correction[:], rough[:], rough[:], ALU.mult).then_inc(s_rstd, 1)
                dve.wait_ge(s_rstd, 4 * b + 1)
                dve.scalar_tensor_tensor(correction[:], moments[:, :, 1], EPS, correction[:], ALU.add,
                                         ALU.mult).then_inc(s_rstd, 1)
                dve.wait_ge(s_rstd, 4 * b + 2)
                dve.tensor_scalar(correction[:], correction[:], -0.5, 1.5, ALU.mult, ALU.add).then_inc(s_rstd, 1)
                dve.wait_ge(s_rstd, 4 * b + 3)
                dve.tensor_tensor(rstd[:], rough[:], correction[:], ALU.mult).then_inc(s_rstd, 1)
                dve.wait_ge(s_rstd, 4 * b + 4)
                for t in range(TT):
                    last = dve.tensor_scalar(xn[:, t], x_in[:, t], moments[:, t, 0:1], rstd[:, t:t + 1],
                                             ALU.subtract, ALU.mult)
                last.then_inc(s_xn, 1)

            def low_xn(b):
                dve.wait_ge(s_xn_hi, b + 1)
                dve.scalar_tensor_tensor(xn_lo[:], xn[:], X_SCALE, xn_hi[:], ALU.mult, ALU.subtract).then_inc(s_xn_lo, 1)

            dve.wait_ge(s_table, 16)
            norm_moments(0)
            norm_apply(0)
            low_xn(0)
            dve.wait_ge(s_w_hi, 1)
            dve.scalar_tensor_tensor(wq_lo[:], wq_stage[:], W_SCALE, wq_hi[:], ALU.mult, ALU.subtract).then_inc(s_w_lo, 1)
            dve.wait_ge(s_w_hi, 2)
            dve.scalar_tensor_tensor(wkv_lo[:], wkv_stage[:], W_SCALE, wkv_hi[:], ALU.mult, ALU.subtract).then_inc(s_w_lo, 1)
            dve.wait_ge(s_w_hi, 3)
            dve.scalar_tensor_tensor(wo_lo[:], wo_stage[:], W_SCALE, wo_hi[:], ALU.mult, ALU.subtract).then_inc(s_w_lo, 1)
            dve.wait_ge(s_table, 16)

            def multiply(b, p, t):
                dve.wait_ge(s_proj, per_step(b, p, TT, t + 1))
                heads = proj[:, 0:RH * DH].rearrange("p (h d) -> p h d", d=DH)
                for c in range(2):
                    last = dve.tensor_tensor(products[:, t, c].rearrange("p (h d) -> p h d", d=DH), heads,
                                             table[:, t, c].unsqueeze(1).broadcast_to([P, RH, DH]), ALU.mult)
                last.then_inc(s_mult, 1)

            def high_parts(b, p, t):
                dve.wait_ge(s_rot, per_step(b, p, 2 * TT, 2 * t + 2))
                dve.tensor_copy(stacked[:, t, 0:RH, 0], rotated[:, t].rearrange("p (h d) -> p h d", d=DH))\
                    .then_inc(s_hi, 1)

            def swapped_keys(b, p, t):
                dve.wait_ge(s_lo, per_step(b, p, TT, t + 1))
                for a in range(2):
                    last = dve.tensor_copy(stacked[:, t, RH:RH + KVS, a], stacked[:, t, QS:RH, 1 - a])
                last.then_inc(s_swap, 1)

            def maxima(b, p, u):
                dve.wait_ge(s_scores, per_step(b, p, UNITS, u + 1))
                heads, keys = unit[u][3:]
                dve.tensor_reduce(negmax[:, u, 0:heads], scores[u % 3][:, :].rearrange(
                    "p (h k) -> p h k", k=keys), AX.X, ALU.max, negate=True).then_inc(s_max, 1)

            def recips(b, p, u):
                dve.wait_ge(s_exp, per_step(b, p, UNITS, u + 1))
                heads = unit[u][3]
                dve.reciprocal(inverse[:, u, 0:heads], sums[:, u, 0:heads]).then_inc(s_recip, 1)

            def copy_p0(b, p, u):
                bank, free = filled(dve, b, p, f"P{u}")
                dve.tensor_copy(pt0[:, u].rearrange("p g n -> p (g n)"), bank[:, :]).then_inc(free, 1)

            def copy_p1(b, p, u):
                j, _, h, _, _ = unit[u]
                bank, free = filled(dve, b, p, f"P{u}")
                dve.tensor_copy(pt1[:, j, :, h:h + 2, :], bank[:, :].rearrange("p (t g n) -> p t g n", t=TT, g=2))\
                    .then_inc(free, 1)

            def copy_q_t(b, p, t):
                bank, free = filled(dve, b, p, f"T{t}")
                dve.tensor_copy(q_t[:, (p + 1) % 2, t].rearrange("p h n -> p (h n)"),
                                bank[:, :].bitcast(fp16)).then_inc(free, 1)

            def heads_lo(b, p, t):
                dve.wait_ge(s_o_hi, per_step(b, p, TT, t + 1))
                dve.tensor_tensor(o_lo[:, p, :, t * P:(t + 1) * P],
                                  heads_out[:, :].rearrange("p (g n) -> p g n", g=G),
                                  o_hi[:, p, :, t * P:(t + 1) * P], ALU.subtract).then_inc(s_o_lo, 1)

            def residual(b):
                dve.wait_ge(s_wo_mm, b + 1)
                dve.wait_ge(s_res, 16 * b + 16)
                if not (isinstance(b, int) and b == 0):
                    dve.wait_ge(s_stored, 16 * b)
                dve.scalar_tensor_tensor(x_out[:].rearrange("p t d -> p (t d)"), heads_out[:, :], OUT_SCALE,
                                         x_res[:].rearrange("p t d -> p (t d)"), ALU.mult, ALU.add)\
                    .then_inc(s_x1, 1)

            def result_moments(b):
                dve.wait_ge(s_x1, b + 1)
                for t in range(TT):
                    dve.bn_stats(x1_stats[:, t], x_out[:, t]).then_inc(s_x1_stat, 1)
                dve.wait_ge(s_x1_stat, b * TT + TT)
                dve.sem_inc(s_passed, 1)
                for t in range(TT):
                    last = dve.bn_aggr(x1_pair[:, t], x1_stats[:, t])
                last.then_inc(s_x1_pair, 1)
                dve.wait_ge(s_x1_pair, b + 1)
                dve.tensor_copy(x1_moments[:, bass.ds(b * TT, TT)], x1_pair[:]).then_inc(s_x1_moments, 1)

            def step(b, p, last, after):
                one, two = not last or p + 1 < STEPS, not last or p + 2 < STEPS
                if one:
                    copy_q_t(b, p, 0)
                if p == 0 and not last:
                    norm_moments(b + 1)
                recips(b, p, 3)
                maxima(b, p, 5)
                if one:
                    copy_q_t(b, p, 1)
                if two:
                    multiply(b, p + 2, 0)
                if p == 1 and not last:
                    low_xn(b + 1)
                if p == 1 and after:
                    result_moments(b - 1)
                recips(b, p, 4)
                if one:
                    maxima(b, p + 1, 0)
                if p == 0 and not last:
                    norm_apply(b + 1)
                if two:
                    high_parts(b, p + 2, 0)
                recips(b, p, 5)
                if one:
                    maxima(b, p + 1, 1)
                if two:
                    multiply(b, p + 2, 1)
                if one:
                    maxima(b, p + 1, 2)
                if two:
                    swapped_keys(b, p + 2, 0)
                copy_p1(b, p, 2)
                if p == 0 and after:
                    residual(b - 1)
                if one:
                    recips(b, p + 1, 0)
                    recips(b, p + 1, 1)
                    maxima(b, p + 1, 3)
                if two:
                    high_parts(b, p + 2, 1)
                copy_p1(b, p, 4)
                heads_lo(b, p, 0)
                if one:
                    recips(b, p + 1, 2)
                    maxima(b, p + 1, 4)
                if two:
                    swapped_keys(b, p + 2, 1)
                heads_lo(b, p, 1)

            for p in range(2):
                for t in range(TT):
                    multiply(0, p, t)
                    high_parts(0, p, t)
                    swapped_keys(0, p, t)
                    if p == 0:
                        copy_q_t(0, -1, t)
            for u in range(5):
                maxima(0, 0, u)
                if u < 3:
                    recips(0, 0, u)
            for p in range(STEPS):
                step(0, p, n_seq == 1, False)
            if n_seq > 2:
                with dve.Fori(1, n_seq - 1) as b:
                    for p in range(STEPS):
                        step(b, p, False, True)
            if n_seq > 1:
                for p in range(STEPS):
                    step(n_seq - 1, p, True, True)
            residual(n_seq - 1)
            result_moments(n_seq - 1)

        @block.tensor
        def _(pe):
            def norm_transposes(b, p, source, t):
                pe.wait_ge(s_xn_lo, source + 1)
                bank, full = previous_ring_use(pe, b, p, f"L{t}")
                out = bank[:, :].bitcast(fp16)
                for s, part in enumerate((xn_hi, xn_lo)):
                    for c in range(DB):
                        i = s * DB + c
                        last = pe.transpose(out[:, i * P:(i + 1) * P], part[:, t, c * P:(c + 1) * P], ident16[:])
                last.then_inc(full, 1)

            def project(b, p, t, before):
                if before:
                    pe.wait_ge(s_mult, per_step(b, p, TT, t))
                    pe.wait_ge(s_vals, per_step(b, p, TT, t))
                if before and p == STEPS:
                    for n in range(TT):
                        emptied(pe, b, LN_STEP, f"L{n}")
                k = p % STEPS
                wq = [w[:, :, k * NQ:(k + 1) * NQ] for w in (wq_hi, wq_lo)]
                wkv = [[w[:, c].rearrange("p (k s n) -> p s k n", k=2, s=STEPS)[:, k] for c in range(DB)]
                       for w in (wkv_hi, wkv_lo)]
                plan = [(s, c, w) for c in range(DB) for s, w in ((0, 0), (0, 1), (1, 0))]
                for i, (s, c, w) in enumerate(plan):
                    lhs = xn_t[:, t, s, c]
                    first, end = i == 0, i == len(plan) - 1
                    pe.matmul(proj[:, 0:NQ], lhs, wq[w][:, c], start=first, stop=end)
                    last = pe.matmul(proj[:, NQ:NQ + NKV].rearrange("p (k n) -> p k n", k=2), lhs, wkv[w][c], start=first, stop=end)
                last.then_inc(s_proj, 1)

            def head_transposes(b, p, n):
                t = min(n, 1)
                if n < 2:
                    pe.wait_ge(s_lo, per_step(b, p + 1, TT, t + 1))
                else:
                    pe.wait_ge(s_swap, per_step(b, p + 1, TT, 2))
                bank, full = previous_ring_use(pe, b, p, f"T{n}")
                out = bank[:, :].bitcast(fp16)
                if n < 2:
                    parts = [stacked[:, n, h] for h in range(QS)]
                else:
                    parts = [stacked[:, t, QS + KVS * a + j] for a in range(2) for j in range(KVS) for t in range(TT)]
                for i, part in enumerate(parts):
                    last = pe.transpose(out[:, i * P:(i + 1) * P], part.rearrange("p s d -> p (s d)"), ident16[:])
                last.then_inc(full, 1)

            def score(b, p, u):
                j, t, h0, heads, keys = unit[u]
                out = scores[u % 3]
                if u == 0:
                    emptied(pe, b, p - 1, "T0")
                    emptied(pe, b, p - 1, "T1")
                    emptied(pe, b, p - 1, "T2")
                if not (isinstance(b, int) and b == 0 and p == 0 and u < 3):
                    pe.wait_ge(s_exp, per_step(b, p, UNITS, u - 2))
                if keys == P:
                    pe.matmul(out[:, :], identb[:], causal[:].rearrange("p h k -> p (h k)"),
                              start=True, stop=False, skip_group_check=True)
                else:
                    pe.matmul(out[:, :].rearrange("p (h t k) -> p h t k", h=2, t=TT)[:, :, 1], identb[:],
                              causal[:, 0:2], start=True, stop=False, skip_group_check=True)
                for i in range(heads):
                    for a in range(2):
                        last = pe.matmul(out[:, i * keys:(i + 1) * keys], q_t[:, p % 2, t, j * G + h0 + i],
                                         k_t[:, p % 2, a, j].rearrange("p t n -> p (t n)")[:, 0:keys],
                                         start=False, stop=i == heads - 1 and a == 1, skip_group_check=True)
                last.then_inc(s_scores, 1)

            def prob_transposes(b, p, u):
                j, t, h0, heads, keys = unit[u]
                pe.wait_ge(s_norm, per_step(b, p, UNITS, u + 1))
                bank, full = previous_ring_use(pe, b, p, f"P{u}")
                for i in range(4):
                    kb, h = divmod(i, heads) if keys > P else (0, i)
                    last = pe.transpose(bank[:, i * P:(i + 1) * P],
                                        probs[:, u, h * keys + kb * P:h * keys + (kb + 1) * P], ident32[:])
                last.then_inc(full, 1)

            def heads_product(b, p, t, free):
                for u in ((0, 1) if t == 0 else (2, 3, 4, 5)):
                    emptied(pe, b, p, f"P{u}")
                pe.wait_ge(s_vals, per_step(b, p, TT, TT))
                free()
                for kb in range(t + 1):
                    for j in range(KVS):
                        rhs = pt0[:, j] if t == 0 else pt1[:, j, kb]
                        last = pe.matmul(heads_out[j * DH:(j + 1) * DH, :], values[:, p % STEPS, kb, j * DH:(j + 1) * DH],
                                         rhs.rearrange("p g n -> p (g n)"), start=kb == 0, stop=kb == t,
                                         skip_group_check=True)
                last.then_inc(s_heads, 1)

            def out_projection(b, part):
                t, second = divmod(part, 2)
                if part == 0:
                    pe.wait_ge(s_o_lo, (b + 1) * (STEPS * TT))
                blocks = range(second * KT // 2, (second + 1) * KT // 2)
                for k in blocks:
                    for n, (o, w) in enumerate(((o_hi, wo_hi), (o_hi, wo_lo), (o_lo, wo_hi))):
                        last = pe.matmul(heads_out[:, t * D:(t + 1) * D],
                                         o[:, k // G, k % G, t * P:(t + 1) * P], w[:, k],
                                         start=k == 0 and n == 0, stop=k == KT - 1 and n == 2)
                if part == 3:
                    last.then_inc(s_wo_mm, 1)

            def step(b, p, last, after):
                one, two = not last or p + 1 < STEPS, not last or p + 2 < STEPS
                quarter = (lambda n: out_projection(b - 1, n)) if p == 0 and after else (lambda n: None)

                def out_bank_read():
                    if p == 0 and after:
                        pe.wait_ge(s_x1, b)
                    elif p:
                        pe.wait_ge(s_o_lo, per_step(b, p, TT, 0))

                prob_transposes(b, p, 0)
                if one:
                    head_transposes(b, p, 0)
                score(b, p, 5)
                if one:
                    head_transposes(b, p, 1)
                quarter(0)
                if one:
                    head_transposes(b, p, 2)
                if two:
                    project(b, p + 2, 0, True)
                quarter(1)
                prob_transposes(b, p, 1)
                if one:
                    score(b, p + 1, 0)
                    score(b, p + 1, 1)
                quarter(2)
                prob_transposes(b, p, 2)
                if two:
                    project(b, p + 2, 1, True)
                if one:
                    score(b, p + 1, 2)
                quarter(3)
                heads_product(b, p, 0, out_bank_read)
                prob_transposes(b, p, 3)
                if p == LN_STEP and not last:
                    norm_transposes(b, p, b + 1, 0)
                if one:
                    score(b, p + 1, 3)
                if p == LN_STEP and not last:
                    norm_transposes(b, p, b + 1, 1)
                if one:
                    score(b, p + 1, 4)
                prob_transposes(b, p, 4)
                prob_transposes(b, p, 5)
                heads_product(b, p, 1, lambda: pe.wait_ge(s_o_lo, per_step(b, p, TT, 1)))

            pe.wait_ge(s_const, 8)
            for t in range(TT):
                norm_transposes(0, -1, 0, t)
            for t in range(TT):
                emptied(pe, 0, -1, f"L{t}")
            pe.wait_ge(s_w_lo, 2)
            for t in range(TT):
                project(0, 0, t, t > 0)
            for n in range(3):
                head_transposes(0, -1, n)
            for t in range(TT):
                project(0, 1, t, True)
            for u in range(5):
                score(0, 0, u)
            pe.wait_ge(s_w_lo, 3)
            for p in range(STEPS):
                step(0, p, n_seq == 1, False)
            if n_seq > 2:
                with pe.Fori(1, n_seq - 1) as b:
                    for p in range(STEPS):
                        step(b, p, False, True)
            if n_seq > 1:
                for p in range(STEPS):
                    step(n_seq - 1, p, True, True)
            for n in range(4):
                out_projection(n_seq - 1, n)


def moe_blocks(nc, x1_dram, moments, gate_w, gate_up, down, shared_gate_up, shared_down, shared_gate, rows_dram,
               hidden_dram, base_dram, out, n_seq):
    fp32, fp16, u32, i32 = mybir.dt.float32, mybir.dt.float16, mybir.dt.uint32, mybir.dt.int32
    ALU, ACT, AX = mybir.AluOpType, mybir.ActivationFunctionType, mybir.AxisListType

    P = 128
    D = gate_w.shape[1]
    DB = D // P
    E = gate_w.shape[0]
    I = down.shape[2]
    SI = shared_down.shape[1]
    TOPK = 4
    HB = 88
    NHB = I // HB
    SB = -(-SI // P)
    GT = 4
    N = GT * P
    TOKENS = n_seq * x1_dram.shape[1]
    GROUPS = TOKENS // N
    TILES = TOKENS // P
    REGION = TOKENS + P
    SLOT_TILES = TOKENS * TOPK // P + E
    U = 4
    SLOT_TILES = -(-SLOT_TILES // U) * U
    SPARE = SLOT_TILES - TOKENS * TOPK // P
    assert NHB * HB == I and GROUPS * N == TOKENS and E % 2 == 0
    assert rows_dram.shape[0] == E * REGION + SPARE * P and hidden_dram.shape[0] == SLOT_TILES * P

    X_SCALE, W_SCALE, H_SCALE = 2.0 ** 5, 2.0 ** 9, 2.0 ** 4
    UP_SCALE = 1.0 / (X_SCALE * W_SCALE)
    DOWN_SCALE = 1.0 / (H_SCALE * W_SCALE)
    EPS = 1e-5
    SPLIT = ((0, 0), (0, 1), (1, 0))

    keep = ExitStack()
    with keep:
        def kept(name, shape, dt):
            return keep.enter_context(nc.sbuf_tensor(name, shape, dt))

        gu_t = [kept(f"gu_t{s}", [P, DB, E * 2 * I], fp16) for s in range(2)]
        dn_t = [kept(f"dn_t{s}", [HB, E, NHB * D], fp16) for s in range(2)]
        sgu_t = [kept(f"sgu_t{s}", [P, DB, 2 * SI], fp16) for s in range(2)]
        sdn_t = [kept(f"sdn_t{s}", [P, SB, D], fp16) for s in range(2)]
        router_t = [kept(f"router_t{s}", [P, DB, E + 1], fp16) for s in range(2)]
        ident32, ident16 = kept("m_ident32", [P, P], fp32), kept("m_ident16", [P, P], fp16)
        places = kept("places", [P, TILES * TOPK], fp32)
        choices = kept("choices", [P, TILES * TOPK], fp32)
        shares = kept("shares", [P, TILES * TOPK], fp32)
        counts = kept("counts", [P, E], fp32)
        chosen = kept("chosen", [P, GT + 1, E], fp16)

        prepare_weights(nc, gate_w, gate_up, down, shared_gate_up, shared_down, shared_gate,
                        gu_t, dn_t, sgu_t, sdn_t, router_t, ident32, ident16, W_SCALE)

        ctx = ExitStack()
        with ctx:
            def sb(name, shape, dt):
                return ctx.enter_context(nc.sbuf_tensor(name, shape, dt))

            def pb(name):
                return ctx.enter_context(nc.psum_tensor(name, [P, 512], fp32))

            def sem(name):
                return ctx.enter_context(nc.semaphore(name))

            strict, ones = sb("strict", [P, P], fp16), sb("ones", [P, P], fp16)
            expert_ids = sb("expert_ids", [P, TOPK, E], fp32)
            regions = sb("regions", [P, E], fp32)
            eps = sb("m_eps", [P, 1], fp32)
            zeros = sb("zeros", [P, 2 * D], fp16)
            x1 = sb("x1", [P, 2, GT, D], fp32)
            log_var, rough = sb("m_log_var", [P, TILES], fp32), sb("m_rough", [P, TILES], fp32)
            correction, rstd = sb("m_correction", [P, TILES], fp32), sb("m_rstd", [P, TILES], fp32)
            xn = sb("m_xn", [P, GT, D], fp32)
            rows = sb("rows", [P, 2, GT, 2, D], fp16)
            xt = sb("xt", [P, 2, 2, DB, N], fp16)
            logits = sb("logits", [P, GT, E + 1], fp32)
            negmax, sums = sb("m_negmax", [P, GT], fp32), sb("m_sums", [P, GT], fp32)
            probs = sb("m_probs", [P, GT, E], fp32)
            top, index = sb("top", [P, GT, 8], fp32), sb("index", [P, GT, 8], u32)
            indexf = sb("indexf", [P, GT, 8], fp32)
            hot, at = sb("hot", [P, GT, TOPK, E], fp32), sb("at", [P, GT, TOPK, E], fp32)
            chosen_now = sb("chosen_now", [P, GT, E], fp16)
            row_of = sb("row_of", [P, GT, E], fp32)
            share, share_sum = sb("share", [P, GT, TOPK], fp32), sb("share_sum", [P, GT], fp32)
            place = sb("place", [P, GT * TOPK], fp32)
            placeu = sb("placeu", [P, 2, GT * TOPK], u32)
            tail, tailu = sb("tail", [P, E], fp32), sb("tailu", [P, E], u32)
            sigmoid = sb("sigmoid", [P, 2, GT], fp32)
            silu = sb("silu", [P, 2, N], fp32)
            h = sb("h", [P, 2, N], fp32)
            h_hi, h_lo = sb("h_hi", [P, SB, N], fp16), sb("h_lo", [P, SB, N], fp16)
            base = sb("base", [P, GT, D], fp32)

            turned, small = pb("turned"), pb("small")
            gates, ups = [pb("gates0"), pb("gates1")], [pb("ups0"), pb("ups1")]
            downs = [pb("downs0"), pb("downs1")]

            s_residual = sem("r_residual")
            s_const, s_x1, s_rough = sem("r_const"), [sem("r_x1_0"), sem("r_x1_1")], sem("r_rough")
            s_rstd, s_xn, s_rows_hi, s_rows = sem("r_rstd"), sem("r_xn"), sem("r_rows_hi"), sem("r_rows")
            s_turned, s_xt, s_logits_mm, s_logits = sem("r_turned"), sem("r_xt"), sem("r_logits_mm"), sem("r_logits")
            s_negmax, s_probs, s_dve = sem("r_negmax"), sem("r_probs"), sem("r_dve")
            s_chosen, s_rank, s_place, s_scattered = sem("r_chosen"), sem("r_rank"), sem("r_place"), [sem("r_scattered0"), sem("r_scattered1")]
            s_gu, s_silu, s_h, s_h_hi, s_h_lo = sem("r_gu"), sem("r_silu"), sem("r_h"), sem("r_h_hi"), sem("r_h_lo")
            s_down, s_base, s_stored, s_zero, s_tail = sem("r_down"), sem("r_base"), sem("r_stored"), sem("r_zero"), sem("r_tail")
            s_at, s_kept, s_totals = sem("r_at"), sem("r_kept"), sem("r_totals")
            s_tails = sem("r_tails")
            s_passed, s_pool_passed = sem("r_passed"), sem("r_pool_passed")

            by_group = lambda a, g: a[g * GT:(g + 1) * GT]
            x1_rows = x1_dram.rearrange("b (t p) d -> p (b t) d", p=P)
            base_rows = base_dram.rearrange("b (t p) d -> p (b t) d", p=P)

            def per_group(g, each, n):
                return g * each + n

            ROUTER_STEPS = 14

            def passes(g, half):
                return g // 2 if isinstance(g, int) else (g - half) // 2

            def block_rows(k):
                return min(P, SI - k * P)

            block = ctx.enter_context(nc.Block(name="route"))

            @block.sync
            def _(sp):
                def load(g, half):
                    sp.dma_start(x1[:, half], x1_rows[:, bass.ds(g * GT, GT)]).then_inc(s_x1[half], 16)

                def load_residual(g):
                    sp.dma_start(base[:], x1_rows[:, bass.ds(g * GT, GT)]).then_inc(s_residual, 16)

                def store(g):
                    sp.wait_ge(s_base, (g + 1) * GT)
                    sp.dma_start(base_rows[:, bass.ds(g * GT, GT)], base[:]).then_inc(s_stored, 16)

                def group(g, half, more):
                    store(g)
                    sp.wait_ge(s_stored, g * 16 + 16)
                    load_residual(g + 1)
                    if more:
                        sp.wait_ge(s_xn, g + 2)
                        load(g + 3, 1 - half)

                load(0, 0)
                load(1, 1)
                load_residual(0)
                sp.wait_ge(s_const, 1)
                for k in range(SPARE):
                    r = E * REGION + k * P
                    sp.dma_start(rows_dram[r:r + P, :], zeros[:]).then_inc(s_zero, 16)
                if GROUPS > 2:
                    sp.wait_ge(s_xn, 1)
                    load(2, 0)
                if GROUPS > 4:
                    with sp.Fori(0, GROUPS // 2 - 2) as gg:
                        for half in range(2):
                            group(gg * 2 + half, half, True)
                for g in range(max(GROUPS - 4, 0), GROUPS - 1):
                    group(g, g % 2, g + 3 < GROUPS)
                store(GROUPS - 1)
                sp.wait_ge(s_stored, 16 * GROUPS)
                sp.wait_ge(s_zero, 16 * SPARE)

            @block.gpsimd
            def _(pool):
                pool.memset(zeros[:], 0.0).then_inc(s_const, 1)
                pool.memset(strict[:], 1.0).then_inc(s_const, 1)
                pool.memset(ones[:], 1.0).then_inc(s_const, 1)
                pool.memset(eps[:], EPS).then_inc(s_const, 1)
                pool.memset(chosen[:], 0.0).then_inc(s_const, 1)
                pool.iota(expert_ids[:], pattern=[[0, TOPK], [1, E]], base=0, channel_multiplier=0,
                          allow_small_or_imprecise_dtypes=True).then_inc(s_const, 1)
                pool.iota(regions[:], pattern=[[REGION, E]], base=0, channel_multiplier=0,
                          allow_small_or_imprecise_dtypes=True).then_inc(s_const, 1)
                pool.iota(tail[:], pattern=[[REGION, E]], base=0, channel_multiplier=1,
                          allow_small_or_imprecise_dtypes=True).then_inc(s_const, 1)
                pool.wait_ge(s_const, 8)
                pool.affine_select(out=strict[:], in_=strict[:], compare_op=ALU.is_gt, fill=0.0, base=0,
                                   pattern=[[1, P]], channel_multiplier=-1).then_inc(s_const, 1)

                def scatter(g, half):
                    pool.wait_ge(s_place, g + 1)
                    pool.sem_inc(s_pool_passed, 1)
                    for t in range(GT):
                        for k in range(TOPK):
                            i = t * TOPK + k
                            pool.indirect_dma_start(
                                rows_dram, bass.IndirectOffsetOnAxis(ap=placeu[:, half, i:i + 1], axis=0),
                                rows[:, half, t].rearrange("p s d -> p (s d)"), None).then_inc(s_scattered[half], 16)

                with pool.Fori(0, GROUPS // 2) as gg:
                    for half in range(2):
                        scatter(gg * 2 + half, half)
                pool.wait_ge(s_tail, 2)
                for e in range(E):
                    pool.indirect_dma_start(rows_dram, bass.IndirectOffsetOnAxis(ap=tailu[:, e:e + 1], axis=0),
                                            zeros[:], None).then_inc(s_tails, 16)
                for half in range(2):
                    pool.wait_ge(s_scattered[half], 16 * TILES * TOPK // 2)
                pool.wait_ge(s_tails, 16 * E)

            @block.scalar
            def _(act):
                act.wait_ge(s_const, 9)

                def high_rows(g, half):
                    act.wait_ge(s_xn, g + 1)
                    if not (isinstance(g, int) and g < 2):
                        act.wait_ge(s_scattered[half], passes(g, half) * (16 * GT * TOPK))
                    act.activation(rows[:, half, :, 0], xn[:], ACT.Copy, scale=X_SCALE).then_inc(s_rows_hi, 1)

                def router(g, half):
                    act.wait_ge(s_negmax, g + 1)
                    for t in range(GT):
                        act.activation(probs[:, t], logits[:, t, 0:E], ACT.Exp, bias=negmax[:, t:t + 1],
                                       accum_out=sums[:, t:t + 1])
                    act.activation(sigmoid[:, half], logits[:, :, E], ACT.Exp, scale=-1.0).then_inc(s_probs, 1)

                def shared(g, k):
                    n = block_rows(k)
                    act.wait_ge(s_gu, per_group(g, SB, k + 1))
                    act.activation(silu[0:n, k % 2], gates[k % 2][0:n, :], ACT.Silu, scale=UP_SCALE).then_inc(s_silu, 1)
                    act.wait_ge(s_h, per_group(g, SB, k + 1))
                    act.activation(h_hi[0:n, k], h[0:n, k % 2], ACT.Copy).then_inc(s_h_hi, 1)

                def group(g, half, last):
                    for k in range(SB):
                        shared(g, k)
                        if k == 0 and not last:
                            high_rows(g + 1, 1 - half)
                    if not last:
                        router(g + 1, 1 - half)

                act.activation(log_var[:], moments[:, :, 1], ACT.Ln, bias=eps[:]).then_inc(s_rough, 1)
                act.wait_ge(s_rough, 1)
                act.activation(rough[:], log_var[:], ACT.Exp, scale=-0.5).then_inc(s_rough, 1)
                high_rows(0, 0)
                router(0, 0)
                if GROUPS > 2:
                    for half in range(2):
                        group(half, half, False)
                if GROUPS > 4:
                    with act.Fori(1, GROUPS // 2 - 1) as gg:
                        for half in range(2):
                            group(gg * 2 + half, half, False)
                for half in range(2):
                    group(GROUPS - 2 + half, half, half == 1)

            @block.vector
            def _(dve):
                dve.wait_ge(s_const, 9)

                def all_rstd():
                    dve.wait_ge(s_rough, 2)
                    dve.tensor_tensor(correction[:], rough[:], rough[:], ALU.mult).then_inc(s_rstd, 1)
                    dve.wait_ge(s_rstd, 1)
                    dve.scalar_tensor_tensor(correction[:], moments[:, :, 1], EPS, correction[:], ALU.add,
                                             ALU.mult).then_inc(s_rstd, 1)
                    dve.wait_ge(s_rstd, 2)
                    dve.tensor_scalar(correction[:], correction[:], -0.5, 1.5, ALU.mult, ALU.add).then_inc(s_rstd, 1)
                    dve.wait_ge(s_rstd, 3)
                    dve.tensor_tensor(rstd[:], rough[:], correction[:], ALU.mult).then_inc(s_rstd, 1)
                    dve.wait_ge(s_rstd, 4)

                def norm(g, half):
                    dve.wait_ge(s_x1[half], passes(g, half) * 16 + 16)
                    for t in range(GT):
                        i = bass.ds(g * GT + t, 1)
                        last = dve.tensor_scalar(xn[:, t], x1[:, half, t],
                                                 moments[:, i, 0:1].rearrange("p a b -> p (a b)"), rstd[:, i],
                                                 ALU.subtract, ALU.mult)
                    last.then_inc(s_xn, 1)

                def low_rows(g, half):
                    dve.wait_ge(s_rows_hi, g + 1)
                    dve.scalar_tensor_tensor(rows[:, half, :, 1], xn[:], X_SCALE, rows[:, half, :, 0],
                                             ALU.mult, ALU.subtract).then_inc(s_rows, 1)

                def transposed(g, half, s):
                    dve.wait_ge(s_turned, per_group(g, 2, s + 1))
                    dve.tensor_copy(xt[:, half, s].rearrange("p c n -> p (c n)"), turned[:, :].bitcast(fp16)).then_inc(s_xt, 1)

                def router(g, half, part):
                    done = [(0, 1, 6, ROUTER_STEPS - 1)[part]]

                    def link(ins, apart=False):
                        done[0] += 1
                        ins.then_inc(s_dve, 1)
                        dve.wait_ge(s_dve, g * ROUTER_STEPS + done[0])
                        if apart:
                            dve.sem_inc(s_passed, 1)

                    if part == 0:
                        dve.wait_ge(s_logits_mm, g + 1)
                        link(dve.tensor_scalar(logits[:], small[:, 0:GT * (E + 1)].rearrange("p (t e) -> p t e", t=GT),
                                               UP_SCALE, None, ALU.mult))
                        dve.tensor_reduce(negmax[:], logits[:, :, 0:E], AX.X, ALU.max, negate=True).then_inc(s_negmax, 1)
                    if part == 1:
                        dve.wait_ge(s_probs, g + 1)
                        link(dve.reciprocal(sums[:], sums[:]))
                        link(dve.tensor_tensor(probs[:], probs[:], sums[:].unsqueeze(2).broadcast_to([P, GT, E]), ALU.mult), apart=True)
                        for t in range(GT):
                            ins = dve.max(top[:, t], probs[:, t])
                        link(ins, apart=True)
                        for t in range(GT):
                            ins = dve.max_index(index[:, t], top[:, t], probs[:, t])
                        link(ins)
                        link(dve.tensor_copy(indexf[:], index[:]))
                    if part == 2:
                        for t in range(GT):
                            ins = dve.tensor_tensor(hot[:, t], expert_ids[:], indexf[:, t, 0:TOPK].unsqueeze(2)
                                                    .broadcast_to([P, TOPK, E]), ALU.is_equal)
                        link(ins)
                        for t in range(GT):
                            with nc.allow_low_precision(reason="a sum of at most one 1 and zeros"):
                                ins = dve.tensor_reduce(chosen_now[:, t], hot[:, t].rearrange("p k e -> p e k"), AX.X, ALU.add)
                        link(ins)
                        for t in range(GT):
                            ins = dve.tensor_tensor(chosen[:, t + 1], chosen[:, t], chosen_now[:, t], ALU.add)
                            if t < GT - 1:
                                ins.then_inc(s_chosen, 1)
                                dve.wait_ge(s_chosen, g * (GT + 1) + t + 1)
                        ins.then_inc(s_chosen, 1)
                        link(dve.tensor_reduce(share_sum[:], top[:, :, 0:TOPK], AX.X, ALU.add))
                        link(dve.reciprocal(share_sum[:], share_sum[:]))
                        dve.tensor_tensor(shares[:, bass.ds(g * (GT * TOPK), GT * TOPK)].rearrange("p (t k) -> p t k", k=TOPK),
                                          top[:, :, 0:TOPK], share_sum[:].unsqueeze(2).broadcast_to([P, GT, TOPK]), ALU.mult)
                        link(dve.tensor_scalar(sigmoid[:, half], sigmoid[:, half], 1.0, None, ALU.add))
                        link(dve.reciprocal(sigmoid[:, half], sigmoid[:, half]))
                        link(dve.tensor_scalar(sigmoid[:, half], sigmoid[:, half], DOWN_SCALE, None, ALU.mult))
                        assert done[0] == ROUTER_STEPS - 1
                    if part == 3:
                        dve.wait_ge(s_rank, g + 1)
                        dve.tensor_copy(chosen[:, 0], chosen[:, GT]).then_inc(s_chosen, 1)
                        link(dve.tensor_tensor(row_of[:], small[:, 128:128 + GT * E].rearrange("p (t e) -> p t e", t=GT),
                                               regions[:].unsqueeze(1).broadcast_to([P, GT, E]), ALU.add))

                def place_rows(g, half):
                    dve.wait_ge(s_chosen, (g + 1) * (GT + 1))
                    for t in range(GT):
                        ins = dve.tensor_tensor(at[:, t], hot[:, t], row_of[:, t].unsqueeze(1)
                                                .broadcast_to([P, TOPK, E]), ALU.mult)
                    ins.then_inc(s_at, 1)
                    dve.wait_ge(s_at, 2 * g + 1)
                    dve.tensor_reduce(place[:], at[:].rearrange("p t k e -> p (t k) e"), AX.X, ALU.add).then_inc(s_at, 1)
                    dve.wait_ge(s_at, 2 * g + 2)
                    dve.tensor_copy(placeu[:, half], place[:]).then_inc(s_place, 1)
                    dve.tensor_copy(choices[:, bass.ds(g * (GT * TOPK), GT * TOPK)].rearrange("p (t k) -> p t k", k=TOPK),
                                    indexf[:, :, 0:TOPK])
                    dve.tensor_copy(places[:, bass.ds(g * (GT * TOPK), GT * TOPK)], place[:]).then_inc(s_kept, 1)

                def shared(g, half, k):
                    n = block_rows(k)
                    dve.wait_ge(s_silu, per_group(g, SB, k + 1))
                    dve.scalar_tensor_tensor(h[0:n, k % 2], ups[k % 2][0:n, :], UP_SCALE * H_SCALE, silu[0:n, k % 2],
                                             ALU.mult, ALU.mult).then_inc(s_h, 1)
                    dve.wait_ge(s_h_hi, per_group(g, SB, k + 1))
                    dve.tensor_tensor(h_lo[0:n, k], h[0:n, k % 2], h_hi[0:n, k], ALU.subtract).then_inc(s_h_lo, 1)

                def add_base(g, half):
                    dve.wait_ge(s_residual, g * 16 + 16)
                    dve.wait_ge(s_down, g + 1)
                    for t in range(GT):
                        dve.scalar_tensor_tensor(base[:, t], downs[t // 2][:, (t % 2) * D:(t % 2 + 1) * D],
                                                 sigmoid[:, half, t:t + 1], base[:, t], ALU.mult, ALU.add).then_inc(s_base, 1)

                def group(g, half, last):
                    router(g, half, 1)
                    for k in range(SB):
                        shared(g, half, k)
                        if k == 0:
                            if not last:
                                norm(g + 1, 1 - half)
                            router(g, half, 2)
                        if k == 1:
                            router(g, half, 3)
                            place_rows(g, half)
                            if not last:
                                low_rows(g + 1, 1 - half)
                        if k in (3, 4) and not last:
                            transposed(g + 1, 1 - half, k - 3)
                    if not last:
                        router(g + 1, 1 - half, 0)
                    add_base(g, half)

                all_rstd()
                norm(0, 0)
                low_rows(0, 0)
                for s in range(2):
                    transposed(0, 0, s)
                router(0, 0, 0)
                if GROUPS > 2:
                    for half in range(2):
                        group(half, half, False)
                if GROUPS > 4:
                    with dve.Fori(1, GROUPS // 2 - 1) as gg:
                        for half in range(2):
                            group(gg * 2 + half, half, False)
                for half in range(2):
                    group(GROUPS - 2 + half, half, half == 1)
                dve.wait_ge(s_totals, 1)
                dve.tensor_tensor(tail[:], tail[:], small[:, 256:256 + E], ALU.add).then_inc(s_tail, 1)
                dve.wait_ge(s_tail, 1)
                dve.tensor_copy(tailu[:], tail[:]).then_inc(s_tail, 1)
                dve.tensor_copy(counts[:], small[:, 256:256 + E]).then_inc(s_kept, 1)

            @block.tensor
            def _(pe):
                pe.wait_ge(s_const, 9)

                def transposes(g, half, s):
                    if s == 0:
                        pe.wait_ge(s_rows, g + 1)
                    if s or not (isinstance(g, int) and g == 0):
                        pe.wait_ge(s_xt, per_group(g, 2, s))
                    bank = turned[:, :].bitcast(fp16)
                    for c in range(DB):
                        for t in range(GT):
                            i = c * GT + t
                            last = pe.transpose(bank[:, i * P:(i + 1) * P],
                                                rows[:, half, t, s, c * P:(c + 1) * P], ident16[:])
                    last.then_inc(s_turned, 1)

                def route(g, half):
                    pe.wait_ge(s_xt, per_group(g, 2, 2))
                    if not (isinstance(g, int) and g == 0):
                        pe.wait_ge(s_dve, g * ROUTER_STEPS)
                    for t in range(GT):
                        n = 0
                        for c in range(DB):
                            for a, w in SPLIT:
                                last = pe.matmul(small[:, t * (E + 1):(t + 1) * (E + 1)], xt[:, half, a, c, t * P:(t + 1) * P],
                                                 router_t[w][:, c], start=n == 0, stop=n == 3 * DB - 1)
                                n += 1
                    last.then_inc(s_logits_mm, 1)

                def ranks(g):
                    pe.wait_ge(s_chosen, g * (GT + 1) + GT)
                    for t in range(GT):
                        out_ = small[:, 128 + t * E:128 + (t + 1) * E]
                        pe.matmul(out_, strict[:], chosen_now[:, t], start=True, stop=False)
                        last = pe.matmul(out_, ones[:], chosen[:, t], start=False, stop=True)
                    last.then_inc(s_rank, 1)

                def shared_up(g, half, k):
                    n = block_rows(k)
                    if k >= 2 or not (isinstance(g, int) and g == 0):
                        pe.wait_ge(s_h, per_group(g, SB, k - 1))
                    for bank, first in ((gates[k % 2], 0), (ups[k % 2], SI)):
                        i = 0
                        for c in range(DB):
                            for w, a in SPLIT:
                                last = pe.matmul(bank[0:n, :], sgu_t[w][:, c, first + k * P:first + k * P + n],
                                                 xt[:, half, a, c], start=i == 0, stop=i == 3 * DB - 1)
                                i += 1
                    last.then_inc(s_gu, 1)

                def shared_down(g, k):
                    n = block_rows(k)
                    pe.wait_ge(s_h_lo, per_group(g, SB, k + 1))
                    if k == 0 and not (isinstance(g, int) and g == 0):
                        pe.wait_ge(s_base, g * GT)
                    for t in range(GT):
                        for i, (a, w) in enumerate(SPLIT):
                            hh = (h_hi, h_lo)[a]
                            last = pe.matmul(downs[t // 2][:, (t % 2) * D:(t % 2 + 1) * D], hh[0:n, k, t * P:(t + 1) * P],
                                             sdn_t[w][0:n, k], start=k == 0 and i == 0 and t % 2 == 0, stop=k == SB - 1 and i == 2,
                                             skip_group_check=True)
                    if k == SB - 1:
                        last.then_inc(s_down, 1)

                def group(g, half, last):
                    for k in range(SB):
                        shared_up(g, half, k)
                        if k == 2:
                            ranks(g)
                        if k in (3, 4) and not last:
                            transposes(g + 1, 1 - half, k - 3)
                        if k == 5 and not last:
                            route(g + 1, 1 - half)
                        if k >= 2:
                            shared_down(g, k - 2)
                    for k in (SB - 2, SB - 1):
                        shared_down(g, k)

                for s in range(2):
                    transposes(0, 0, s)
                route(0, 0)
                if GROUPS > 2:
                    for half in range(2):
                        group(half, half, False)
                if GROUPS > 4:
                    with pe.Fori(1, GROUPS // 2 - 1) as gg:
                        for half in range(2):
                            group(gg * 2 + half, half, False)
                for half in range(2):
                    group(GROUPS - 2 + half, half, half == 1)
                pe.wait_ge(s_chosen, GROUPS * (GT + 1))
                pe.wait_ge(s_dve, GROUPS * ROUTER_STEPS)
                pe.matmul(small[:, 256:256 + E], ones[:], chosen[:, 0], start=True, stop=True).then_inc(s_totals, 1)

        experts_block(nc, rows_dram, hidden_dram, counts, places, choices, gu_t, dn_t, ident16, SLOT_TILES, U, REGION,
                      UP_SCALE, H_SCALE, DOWN_SCALE)
        combine_block(nc, base_dram, hidden_dram, places, shares, out, TILES, TOPK)


def prepare_weights(nc, gate_w, gate_up, down, shared_gate_up, shared_down, shared_gate,
                    gu_t, dn_t, sgu_t, sdn_t, router_t, ident32, ident16, W_SCALE):
    fp32, fp16 = mybir.dt.float32, mybir.dt.float16
    ALU, ACT = mybir.AluOpType, mybir.ActivationFunctionType
    P = 128
    E, D = gate_w.shape
    DB = D // P
    I = down.shape[2]
    SI = shared_down.shape[1]
    HB = dn_t[0].shape[0]
    NHB = I // HB
    FB = 2 * NHB
    BANKS, EACH = 6, 1 + DB

    ctx = ExitStack()
    with ctx:
        def sb(name, shape, dt):
            return ctx.enter_context(nc.sbuf_tensor(name, shape, dt))

        def sem(name):
            return ctx.enter_context(nc.semaphore(name))

        gu = sb("gu", [HB, 2, FB, D], fp32)
        dn = sb("dn", [P, 2, DB, I], fp32)
        sgu = sb("sgu", [HB, 2 * SI // HB, D], fp32)
        sdn = sb("sdn", [P, DB, SI], fp32)
        router = sb("router", [E + 1, D], fp32)
        banks = [ctx.enter_context(nc.psum_tensor(f"w_bank{i}", [P, 512], fp32)) for i in range(BANKS)]
        s_const, s_turned, s_high, s_low = sem("w_const"), sem("w_turned"), sem("w_high"), sem("w_low")
        s_expert, s_rest = [sem("w_expert0"), sem("w_expert1")], sem("w_rest")

        block = ctx.enter_context(nc.Block(name="weights"))

        rest = [("sgu", c, q) for c in range(DB) for q in range(2 * SI // (FB * HB))]
        rest += [("sdn", k, n) for k, n in ((0, 2), (2, 2), (4, 1), (5, 1))] + [("router", 0, 0)]

        def rest_parts(kind, a, n, bank, dst):
            if kind == "sgu":
                return bank[:, 0:FB * HB], dst["sgu"][:, a, n * FB * HB:(n + 1) * FB * HB]
            if kind == "sdn":
                r = min(P, SI - a * P)
                return bank[0:r, 0:n * D], dst["sdn"][0:r, a:a + n].rearrange("p k d -> p (k d)")
            return bank[:, 0:DB * (E + 1)], dst["router"][:].rearrange("p c e -> p (c e)")

        @block.sync
        def _(sp):
            def load(e, half, waits=True):
                if waits:
                    sp.wait_ge(s_turned, e * EACH - EACH)
                sp.dma_start(gu[:, half], gate_up[e].rearrange("(b r) d -> r b d", r=HB)).then_inc(s_expert[half], 16)
                sp.dma_start(dn[:, half], down[e].rearrange("(t p) i -> p t i", p=P)).then_inc(s_expert[half], 16)

            load(0, 0, False)
            load(1, 1, False)
            sp.dma_start(sgu[:], shared_gate_up.rearrange("(b r) d -> r b d", r=HB)).then_inc(s_rest, 16)
            sp.dma_start(sdn[:], shared_down.rearrange("(t p) i -> p t i", p=P)).then_inc(s_rest, 16)
            sp.dma_start(router[0:E, :], gate_w).then_inc(s_rest, 16)
            sp.dma_start(router[E:E + 1, :], shared_gate).then_inc(s_rest, 16)
            with sp.Fori(1, E // 2) as ee:
                for half in range(2):
                    load(ee * 2 + half, half)

        @block.gpsimd
        def _(pool):
            for m in (ident32, ident16):
                pool.memset(m[:], 0.0).then_inc(s_const, 1)
            pool.wait_ge(s_const, 2)
            for m in (ident32, ident16):
                pool.affine_select(out=m[:], in_=m[:], compare_op=ALU.not_equal, fill=1.0, base=0,
                                   pattern=[[-1, P]], channel_multiplier=1).then_inc(s_const, 1)

        @block.tensor
        def _(pe):
            pe.wait_ge(s_const, 4)

            def free(fill):
                if not isinstance(fill, int) or fill >= BANKS:
                    pe.wait_ge(s_low, fill - BANKS + 1)

            def expert(e, half):
                pe.wait_ge(s_expert[half], ((e - half) // 2 if not isinstance(e, int) else e // 2) * 32 + 32)
                for c in range(DB):
                    free(e * EACH + c)
                    for b in range(FB):
                        last = pe.transpose(banks[half * EACH + c][:, b * HB:(b + 1) * HB],
                                            gu[:, half, b, c * P:(c + 1) * P], ident32[0:HB, 0:HB])
                    last.then_inc(s_turned, 1)
                free(e * EACH + DB)
                for b in range(NHB):
                    for t in range(DB):
                        last = pe.transpose(banks[half * EACH + DB][0:HB, b * D + t * P:b * D + (t + 1) * P],
                                            dn[:, half, t, b * HB:(b + 1) * HB], ident32[:])
                last.then_inc(s_turned, 1)

            for half in range(2):
                expert(half, half)
            with pe.Fori(1, E // 2) as ee:
                for half in range(2):
                    expert(ee * 2 + half, half)
            pe.wait_ge(s_rest, 64)
            for i, (kind, a, n) in enumerate(rest):
                fill = E * EACH + i
                free(fill)
                bank = banks[fill % BANKS]
                if kind == "sgu":
                    for b in range(FB):
                        last = pe.transpose(bank[:, b * HB:(b + 1) * HB], sgu[:, n * FB + b, a * P:(a + 1) * P],
                                            ident32[0:HB, 0:HB])
                elif kind == "sdn":
                    for k in range(n):
                        r = min(P, SI - (a + k) * P)
                        for t in range(DB):
                            last = pe.transpose(bank[0:r, k * D + t * P:k * D + (t + 1) * P],
                                                sdn[:, t, (a + k) * P:(a + k) * P + r], ident32[:])
                else:
                    for c in range(DB):
                        last = pe.transpose(bank[:, c * (E + 1):(c + 1) * (E + 1)], router[:, c * P:(c + 1) * P],
                                            ident32[0:E + 1, 0:E + 1])
                last.then_inc(s_turned, 1)

        def split(eng, part, fill, bank, dst):
            if part == 0:
                eng.wait_ge(s_turned, fill + 1)
                eng.activation(dst[0], bank, ACT.Copy, scale=W_SCALE).then_inc(s_high, 1)
            else:
                eng.wait_ge(s_high, fill + 1)
                eng.scalar_tensor_tensor(dst[1], bank, W_SCALE, dst[0], ALU.mult, ALU.subtract).then_inc(s_low, 1)

        def split_all(eng, part):
            def expert(e, half):
                for c in range(DB):
                    split(eng, part, e * EACH + c, banks[half * EACH + c][:, 0:2 * I],
                          [w[:, c, bass.ds(e * (2 * I), 2 * I)] for w in gu_t])
                split(eng, part, e * EACH + DB, banks[half * EACH + DB][0:HB, 0:NHB * D],
                      [w[:, bass.ds(e, 1)].rearrange("p e n -> p (e n)") for w in dn_t])

            with eng.Fori(0, E // 2) as ee:
                for half in range(2):
                    expert(ee * 2 + half, half)
            for i, (kind, a, n) in enumerate(rest):
                fill = E * EACH + i
                dst = [dict(sgu=sgu_t[s], sdn=sdn_t[s], router=router_t[s]) for s in range(2)]
                parts = [rest_parts(kind, a, n, banks[fill % BANKS], d) for d in dst]
                split(eng, part, fill, parts[0][0], [x[1] for x in parts])

        @block.scalar
        def _(act):
            split_all(act, 0)

        @block.vector
        def _(dve):
            split_all(dve, 1)


def experts_block(nc, rows_dram, hidden_dram, counts, places, choices, gu_t, dn_t, ident16, SLOT_TILES, U, REGION,
                  UP_SCALE, H_SCALE, DOWN_SCALE):
    fp32, fp16, i32 = mybir.dt.float32, mybir.dt.float16, mybir.dt.int32
    ALU, ACT, AX = mybir.AluOpType, mybir.ActivationFunctionType, mybir.AxisListType
    P = 128
    DB = gu_t[0].shape[1]
    D = DB * P
    E = counts.shape[1]
    I2 = gu_t[0].shape[2] // E
    HB = dn_t[0].shape[0]
    I = I2 // 2
    NHB = I // HB
    MOST = (REGION - P) // P
    PASSES = SLOT_TILES // U
    SPLIT = ((0, 0), (0, 1), (1, 0))

    ctx = ExitStack()
    with ctx:
        def sb(name, shape, dt):
            return ctx.enter_context(nc.sbuf_tensor(name, shape, dt))

        def pb(name):
            return ctx.enter_context(nc.psum_tensor(name, [P, 512], fp32))

        def sem(name):
            return ctx.enter_context(nc.semaphore(name))

        thresholds = sb("thresholds", [P, E, MOST], fp32)
        fuller = sb("fuller", [P, E, MOST], fp32)
        not_after = sb("not_after", [P, E, E], fp32)
        ahead = sb("ahead", [P, E, E], fp32)
        tiles, ends = sb("tiles", [P, E], fp32), sb("ends", [P, E], fp32)
        shift = sb("shift", [P, E], fp32)
        expert_ids = sb("e_expert_ids", [P, E], fp32)
        is_choice = sb("is_choice", [P, places.shape[1], E], fp32)
        moved = sb("moved", [P, places.shape[1]], fp32)
        slot_ids = sb("slot_ids", [1, SLOT_TILES], fp32)
        past = sb("past", [1, SLOT_TILES, E], fp32)
        expert_of, first_of = sb("expert_of", [1, SLOT_TILES], fp32), sb("first_of", [1, SLOT_TILES], fp32)
        experts = sb("experts", [1, SLOT_TILES], i32)
        slot_rows = sb("slot_rows", [1, SLOT_TILES], i32)

        x_in = sb("e_x_in", [P, U, 2 * D], fp16)
        xt = sb("e_xt", [P, 2, 2, DB, P], fp16)
        silu, h = sb("e_silu", [P, 2, I], fp32), sb("e_h", [P, 2, I], fp32)
        h_parts = sb("e_h_parts", [P, 2, 2, I], fp16)
        ht = sb("e_ht", [HB, 2, 2, NHB, P], fp16)
        y = sb("e_y", [P, U, D], fp32)
        turned, h_turned = [pb("e_turned0"), pb("e_turned1")], [pb("e_h_turned0"), pb("e_h_turned1")]
        gu, yb = [pb("e_gu0"), pb("e_gu1")], [pb("e_y0"), pb("e_y1")]

        s_const, s_plan, s_planned = sem("e_const"), sem("e_plan"), sem("e_planned")
        s_in, s_out = [sem(f"e_in{u}") for u in range(U)], [sem(f"e_out{u}") for u in range(U)]
        s_turned, s_xt, s_gu, s_silu = sem("e_turned"), sem("e_xt"), sem("e_gu"), sem("e_silu")
        s_h, s_h_hi, s_h_lo, s_down, s_y = sem("e_h"), sem("e_h_hi"), sem("e_h_lo"), sem("e_down"), sem("e_y")
        s_h_turned, s_ht = sem("e_h_turned_s"), sem("e_ht_s")

        block = ctx.enter_context(nc.Block(name="experts"))

        @block.gpsimd
        def _(pool):
            iota = dict(channel_multiplier=0, allow_small_or_imprecise_dtypes=True)
            pool.iota(thresholds[:], pattern=[[0, E], [P, MOST]], base=0, **iota).then_inc(s_const, 1)
            pool.iota(expert_ids[:], pattern=[[1, E]], base=0, **iota).then_inc(s_const, 1)
            pool.iota(slot_ids[:], pattern=[[1, SLOT_TILES]], base=0, **iota).then_inc(s_const, 1)
            pool.memset(not_after[:], 1.0).then_inc(s_const, 1)
            pool.wait_ge(s_const, 4)
            pool.affine_select(out=not_after[:], in_=not_after[:], compare_op=ALU.is_ge, fill=0.0, base=0,
                               pattern=[[1, E], [-1, E]], channel_multiplier=0).then_inc(s_const, 1)

        @block.vector
        def _(dve):
            done = [0]

            def link(ins):
                done[0] += 1
                ins.then_inc(s_plan, 1)
                dve.wait_ge(s_plan, done[0])

            dve.wait_ge(s_const, 5)
            link(dve.tensor_tensor(fuller[:], counts[:].unsqueeze(2).broadcast_to([P, E, MOST]), thresholds[:], ALU.is_gt))
            link(dve.tensor_reduce(tiles[:], fuller[:], AX.X, ALU.add))
            link(dve.tensor_tensor(ahead[:], tiles[:].unsqueeze(1).broadcast_to([P, E, E]), not_after[:], ALU.mult))
            link(dve.tensor_reduce(ends[:], ahead[:], AX.X, ALU.add))
            link(dve.tensor_tensor(past[:], ends[0:1].unsqueeze(1).broadcast_to([1, SLOT_TILES, E]),
                                   slot_ids[:].unsqueeze(2).broadcast_to([1, SLOT_TILES, E]), ALU.is_le))
            link(dve.tensor_reduce(expert_of[:], past[:], AX.X, ALU.add))
            link(dve.tensor_tensor(past[:], past[:], tiles[0:1].unsqueeze(1).broadcast_to([1, SLOT_TILES, E]), ALU.mult))
            link(dve.tensor_reduce(first_of[:], past[:], AX.X, ALU.add))
            link(dve.tensor_tensor(first_of[:], slot_ids[:], first_of[:], ALU.subtract))
            link(dve.tensor_scalar(first_of[:], first_of[:], float(P), None, ALU.mult))
            link(dve.scalar_tensor_tensor(first_of[:], expert_of[:], float(REGION), first_of[:], ALU.mult, ALU.add))
            link(dve.tensor_copy(slot_rows[:], first_of[:]))
            link(dve.tensor_scalar(expert_of[:], expert_of[:], float(E - 1), None, ALU.min))
            dve.tensor_copy(experts[:], expert_of[:]).then_inc(s_planned, 1)

            def move_places():
                link(dve.tensor_tensor(shift[:], ends[:], tiles[:], ALU.subtract))
                link(dve.tensor_scalar(shift[:], shift[:], float(P), None, ALU.mult))
                link(dve.scalar_tensor_tensor(shift[:], expert_ids[:], -float(REGION), shift[:], ALU.mult, ALU.add))
                T = places.shape[1]
                link(dve.tensor_tensor(is_choice[:], choices[:].unsqueeze(2).broadcast_to([P, T, E]),
                                       expert_ids[:].unsqueeze(1).broadcast_to([P, T, E]), ALU.is_equal))
                link(dve.tensor_tensor(is_choice[:], is_choice[:], shift[:].unsqueeze(1).broadcast_to([P, T, E]), ALU.mult))
                link(dve.tensor_reduce(moved[:], is_choice[:], AX.X, ALU.add))
                link(dve.tensor_tensor(places[:], places[:], moved[:], ALU.add))

            def copy_xt(n, u):
                dve.wait_ge(s_turned, n + 1)
                dve.tensor_copy(xt[:, u % 2].rearrange("p s c n -> p (s c n)"),
                                turned[u % 2][:, :].bitcast(fp16)[:, 0:2 * D]).then_inc(s_xt, 1)

            def hidden(n, u):
                dve.wait_ge(s_silu, n + 1)
                dve.scalar_tensor_tensor(h[:, u % 2], gu[u % 2][:, I:2 * I], UP_SCALE * H_SCALE,
                                         silu[:, u % 2], ALU.mult, ALU.mult).then_inc(s_h, 1)
                dve.wait_ge(s_h_hi, n + 1)
                dve.tensor_tensor(h_parts[:, u % 2, 1], h[:, u % 2], h_parts[:, u % 2, 0],
                                  ALU.subtract).then_inc(s_h_lo, 1)

            def copy_ht(n, u):
                dve.wait_ge(s_h_turned, n + 1)
                dve.tensor_copy(ht[:, u % 2].rearrange("p s b n -> p (s b n)"),
                                h_turned[u % 2][0:HB, :].bitcast(fp16)[:, 0:2 * NHB * P]).then_inc(s_ht, 1)

            for n in range(3):
                copy_xt(n, n)
            hidden(0, 0)
            copy_ht(0, 0)
            hidden(1, 1)

            def tile(n, u, i=None):
                if i is None or i + 3 < SLOT_TILES:
                    copy_xt(n + 3, (u + 3) % U)
                if i is None or i + 1 < SLOT_TILES:
                    copy_ht(n + 1, (u + 1) % U)
                if i is None or i + 2 < SLOT_TILES:
                    hidden(n + 2, (u + 2) % U)

            with dve.Fori(0, PASSES - 1) as q:
                for u in range(U):
                    tile(q * U + u, u)
            for u in range(U):
                tile((PASSES - 1) * U + u, u, (PASSES - 1) * U + u)
            move_places()

        @block.sync
        def _(sp):
            sp.wait_ge(s_planned, 1)

            def rows_at(i):
                return sp.value_load(slot_rows[0:1, i], min_val=0, max_val=rows_dram.shape[0] - P)

            def load_next(n, u):
                row = rows_at(bass.ds(n + U, 1))
                sp.wait_ge(s_turned, n + 1)
                load(n + U, u, row)

            def load(n, u, row):
                sp.dma_start(x_in[:, u], rows_dram[bass.ds(row, P), :]).then_inc(s_in[u], 16)

            def store(n, u):
                sp.wait_ge(s_y, n + 1)
                sp.dma_start(hidden_dram[bass.ds(n * P, P), :], y[:, u]).then_inc(s_out[u], 16)

            for u in range(U):
                load(u, u, rows_at(bass.ds(u, 1)))
            for u in range(U):
                load_next(u, u)
                if u >= 2:
                    store(u - 2, u - 2)
            with sp.Fori(1, PASSES - 1) as q:
                for u in range(U):
                    load_next(q * U + u, u)
                    store(q * U + (u - 2), (u - 2) % U)
            for n in range((PASSES - 1) * U - 2, SLOT_TILES):
                store(n, n % U)
            for u in range(U):
                sp.wait_ge(s_out[u], 16 * PASSES)

        @block.scalar
        def _(act):
            def gate(n, u):
                act.wait_ge(s_gu, n + 1)
                act.activation(silu[:, u % 2], gu[u % 2][:, 0:I], ACT.Silu, scale=UP_SCALE).then_inc(s_silu, 1)
                act.wait_ge(s_h, n + 1)
                act.activation(h_parts[:, u % 2, 0], h[:, u % 2], ACT.Copy).then_inc(s_h_hi, 1)

            for n in range(2):
                gate(n, n)

            def tile(n, u, q, i=None):
                if i is None or i + 2 < SLOT_TILES:
                    gate(n + 2, (u + 2) % U)
                act.wait_ge(s_down, n + 1)
                if not (isinstance(q, int) and q == 0):
                    act.wait_ge(s_out[u], q * 16)
                act.activation(y[:, u], yb[u % 2][:, 0:D], ACT.Copy, scale=DOWN_SCALE).then_inc(s_y, 1)

            for u in range(U):
                tile(u, u, 0)
            with act.Fori(1, PASSES - 1) as q:
                for u in range(U):
                    tile(q * U + u, u, q)
            for u in range(U):
                n = (PASSES - 1) * U + u
                tile(n, u, PASSES - 1, n)

        @block.tensor
        def _(pe):
            pe.wait_ge(s_planned, 1)

            def experts_at(n, count):
                return nc.values_load_multi_w_load_instructions(
                    experts[0:1, bass.ds(n, count)], [pe.engine], min_val=0, max_val=E - 1,
                    skip_runtime_bounds_check_because="the plan bounds it by E - 1")[1]

            def transposes(n, u, p):
                pe.wait_ge(s_in[u], p * 16 + 16)
                if not isinstance(n, int) or n >= 2:
                    pe.wait_ge(s_xt, n - 1)
                for i in range(2 * DB):
                    last = pe.transpose(turned[u % 2][:, :].bitcast(fp16)[:, i * P:(i + 1) * P],
                                        x_in[:, u, i * P:(i + 1) * P], ident16[:])
                last.then_inc(s_turned, 1)

            def up(n, u, e):
                pe.wait_ge(s_xt, n + 1)
                if not isinstance(n, int) or n >= 2:
                    pe.wait_ge(s_h, n - 1)
                k = 0
                for c in range(DB):
                    for a, w in SPLIT:
                        last = pe.matmul(gu[u % 2][:, 0:I2], xt[:, u % 2, a, c], gu_t[w][:, c, bass.ds(e * I2, I2)],
                                         start=k == 0, stop=k == 3 * DB - 1)
                        k += 1
                last.then_inc(s_gu, 1)

            def h_transposes(n, u):
                pe.wait_ge(s_h_lo, n + 1)
                if not isinstance(n, int) or n >= 2:
                    pe.wait_ge(s_ht, n - 1)
                for a in range(2):
                    for b in range(NHB):
                        i = a * NHB + b
                        last = pe.transpose(h_turned[u % 2][0:HB, :].bitcast(fp16)[:, i * P:(i + 1) * P],
                                            h_parts[:, u % 2, a, b * HB:(b + 1) * HB], ident16[:])
                last.then_inc(s_h_turned, 1)

            def down(n, u, e):
                pe.wait_ge(s_ht, n + 1)
                if not isinstance(n, int) or n >= 2:
                    pe.wait_ge(s_y, n - 1)
                k = 0
                for b in range(NHB):
                    for a, w in SPLIT:
                        last = pe.matmul(yb[u % 2][:, 0:D], ht[:, u % 2, a, b],
                                         dn_t[w][:, bass.ds(e, 1), b * D:(b + 1) * D].rearrange("p e n -> p (e n)"),
                                         start=k == 0, stop=k == 3 * NHB - 1)
                        k += 1
                last.then_inc(s_down, 1)

            def tile(n, u, q, es, i=None):
                if i is None or i + 3 < SLOT_TILES:
                    transposes(n + 3, (u + 3) % U, q + (u + 3) // U)
                if i is None or i + 2 < SLOT_TILES:
                    up(n + 2, (u + 2) % U, es[u + 2])
                if i is None or i + 1 < SLOT_TILES:
                    h_transposes(n + 1, (u + 1) % U)
                down(n, u, es[u])

            es = experts_at(0, U + 2)
            for n in range(3):
                transposes(n, n, 0)
                if n < 2:
                    up(n, n, es[n])
            h_transposes(0, 0)
            for u in range(U):
                tile(u, u, 0, es)
            with pe.Fori(1, PASSES - 1) as q:
                es = experts_at(q * U, U + 2)
                for u in range(U):
                    tile(q * U + u, u, q, es)
            es = experts_at((PASSES - 1) * U, U)
            for u in range(U):
                n = (PASSES - 1) * U + u
                tile(n, u, PASSES - 1, es, n)


def combine_block(nc, base_dram, hidden_dram, places, shares, out, TILES, TOPK):
    fp32, u32 = mybir.dt.float32, mybir.dt.uint32
    ALU = mybir.AluOpType
    P, GT = 128, 4
    D = out.shape[2]
    GROUPS = TILES // GT
    W = GT * TOPK

    ctx = ExitStack()
    with ctx:
        def sb(name, shape, dt):
            return ctx.enter_context(nc.sbuf_tensor(name, shape, dt))

        def sem(name):
            return ctx.enter_context(nc.semaphore(name))

        place, share = sb("c_place", [P, 2, W], u32), sb("c_share", [P, 2, W], fp32)
        got = sb("c_got", [P, 2, GT, TOPK, D], fp32)
        acc = sb("c_acc", [P, 2, GT, D], fp32)
        s_place, s_share = sem("c_place_s"), sem("c_share_s")
        s_got = [[sem(f"c_got{h}{t}") for t in range(GT)] for h in range(2)]
        s_base, s_sum, s_out = [sem("c_base0"), sem("c_base1")], sem("c_sum"), [sem("c_out0"), sem("c_out1")]
        s_link, s_passed = sem("c_link"), sem("c_passed")

        rows = lambda a: a.rearrange("b (t p) d -> p (b t) d", p=P)
        base_rows, out_rows = rows(base_dram), rows(out)
        block = ctx.enter_context(nc.Block(name="combine"))

        @block.sync
        def _(sp):
            def load(g, half):
                sp.dma_start(acc[:, half], base_rows[:, bass.ds(g * GT, GT)]).then_inc(s_base[half], 16)

            def store(g, half):
                sp.wait_ge(s_sum, (g + 1) * GT)
                sp.dma_start(out_rows[:, bass.ds(g * GT, GT)], acc[:, half]).then_inc(s_out[half], 16)

            for half in range(2):
                load(half, half)
            if GROUPS > 2:
                with sp.Fori(0, GROUPS // 2 - 1) as gg:
                    for half in range(2):
                        store(gg * 2 + half, half)
                        sp.wait_ge(s_out[half], gg * 16 + 16)
                        load(gg * 2 + (half + 2), half)
            for half in range(2):
                store(GROUPS - 2 + half, half)
            for half in range(2):
                sp.wait_ge(s_out[half], 16 * GROUPS // 2)

        def each_group(eng, group):
            for half in range(2):
                group(half, half, 0)
            if GROUPS > 2:
                with eng.Fori(1, GROUPS // 2) as gg:
                    for half in range(2):
                        group(gg * 2 + half, half, gg)

        @block.gpsimd
        def _(pool):
            def group(g, half, gg):
                pool.wait_ge(s_place, g + 1)
                pool.sem_inc(s_passed, 1)
                for t in range(GT):
                    for k in range(TOPK):
                        i = t * TOPK + k
                        pool.indirect_dma_start(got[:, half, t, k], None, hidden_dram,
                                                bass.IndirectOffsetOnAxis(ap=place[:, half, i:i + 1], axis=0))\
                            .then_inc(s_got[half][t], 16)

            each_group(pool, group)

        @block.vector
        def _(dve):
            def places_of(g, half, gg):
                cols = bass.ds(g * W, W)
                dve.tensor_copy(place[:, half], places[:, cols]).then_inc(s_place, 1)
                dve.tensor_copy(share[:, half], shares[:, cols]).then_inc(s_share, 1)

            def group(g, half, gg):
                dve.wait_ge(s_base[half], gg * 16 + 16)
                for k in range(TOPK):
                    for t in range(GT):
                        if k == 0:
                            dve.wait_ge(s_got[half][t], gg * (16 * TOPK) + 16 * TOPK)
                        i = t * TOPK + k
                        ins = dve.scalar_tensor_tensor(acc[:, half, t], got[:, half, t, k], share[:, half, i:i + 1],
                                                       acc[:, half, t], ALU.mult, ALU.add)
                        ins.then_inc(s_sum if k == TOPK - 1 else s_link, 1)
                    if k < TOPK - 1:
                        dve.wait_ge(s_link, g * (GT * (TOPK - 1)) + (k + 1) * GT)

            for half in range(2):
                places_of(half, half, 0)
            dve.wait_ge(s_share, 2)
            for half in range(2):
                group(half, half, 0)
                if GROUPS > 2:
                    dve.wait_ge(s_sum, (half + 1) * GT)
                    places_of(half + 2, half, 1)
                    dve.wait_ge(s_share, half + 3)
            if GROUPS > 4:
                with dve.Fori(1, GROUPS // 2 - 1) as gg:
                    for half in range(2):
                        g = gg * 2 + half
                        group(g, half, gg)
                        dve.wait_ge(s_sum, (g + 1) * GT)
                        places_of(g + 2, half, gg + 1)
                        dve.wait_ge(s_share, g + 3)
            if GROUPS > 2:
                for half in range(2):
                    group(GROUPS - 2 + half, half, GROUPS // 2 - 1)


_INS = ['L0_attn_x', 'L0_attn_Wq', 'L0_attn_Wkv', 'L0_attn_Wo', 'L0_ffn_gate_w', 'L0_ffn_expert_gate_up',
        'L0_ffn_expert_down', 'L0_ffn_shared_gate_up', 'L0_ffn_shared_down', 'L0_ffn_shared_gate_vec']


def layer(nc, x, w_q, w_kv, w_o, gate_w, gate_up, down, shared_gate_up, shared_down, shared_gate, rope, out):
    P = 128
    n_seq, seq, D = x.shape
    E, K, U = gate_w.shape[0], 4, 4
    tokens = n_seq * seq
    region = tokens + P
    slot_tiles = -(-(tokens * K // P + E) // U) * U
    spare = slot_tiles - tokens * K // P
    x1 = nc.dram_tensor("x1_scratch", [n_seq, seq, D], mybir.dt.float32).ap()
    base = nc.dram_tensor("base_scratch", [n_seq, seq, D], mybir.dt.float32).ap()
    rows = nc.dram_tensor("rows_scratch", [E * region + spare * P, 2 * D], mybir.dt.float16).ap()
    hidden = nc.dram_tensor("hidden_scratch", [slot_tiles * P, D], mybir.dt.float32).ap()
    with nc.sbuf_tensor("x1_moments", [P, tokens // P, 2], mybir.dt.float32) as moments:
        attention_block(nc, x, w_q, w_kv, w_o, rope, x1, moments, n_seq)
        moe_blocks(nc, x1, moments, gate_w, gate_up, down, shared_gate_up, shared_down, shared_gate, rows, hidden, base,
                   out, n_seq)


def _rope_table(seq, width):
    import numpy as np

    one, base = np.float32(1.0), np.float32(10000.0)
    frequencies = one / base ** (np.arange(0, width, 2, dtype=np.float32) / np.float32(width))
    angles = np.arange(seq, dtype=np.float32)[:, None] * frequencies[None, :]
    cos, sin = np.cos(angles), np.sin(angles)
    table = np.stack([np.concatenate([cos, cos], -1), np.concatenate([sin, -sin], -1)], axis=1)
    return (table * np.float32(2.0 ** -8)).astype(np.float32)


def kernel(**inputs):
    import numpy as _np
    import concourse.bacc as _bacc
    from concourse import mybir as _mybir
    from concourse.bass_utils import run_bass_kernel_spmd as _run

    nc = _bacc.Bacc("TRN2", target_bir_lowering=False, num_devices=1)
    arrays, args = {}, []
    for name in _INS:
        a = _np.ascontiguousarray(inputs[name])
        arrays[f"in_{name}_dram"] = a
        args.append(nc.dram_tensor(f"in_{name}_dram", a.shape, _mybir.dt.from_np(a.dtype), kind="ExternalInput").ap())
    shape = tuple(inputs['L0_attn_x'].shape)
    table = _rope_table(shape[1], 64)
    arrays["in_rope_dram"] = table
    args.append(nc.dram_tensor("in_rope_dram", table.shape, _mybir.dt.float32, kind="ExternalInput").ap())
    args.append(nc.dram_tensor("out_0_dram", shape, _mybir.dt.float32, kind="ExternalOutput").ap())
    layer(nc, *args)
    r = _run(nc, [arrays], core_ids=[0])
    return r.results[0]["out_0_dram"]
```

```python
import concourse.bass as bass
from concourse import mybir
from contextlib import ExitStack


def attention_block(nc, x, w_q, w_kv, w_o, rope, x1_dram, x1_moments, n_seq):
    fp32, fp16, bf16 = mybir.dt.float32, mybir.dt.float16, mybir.dt.bfloat16
    ALU, ACT, AX = mybir.AluOpType, mybir.ActivationFunctionType, mybir.AxisListType

    P = 128
    SEQ, D = x.shape[1], x.shape[2]
    DH = rope.shape[2]
    HALF = DH // 2
    TT = SEQ // P
    DB = D // P
    HQ = w_q.shape[1] // DH
    HK = w_kv.shape[1] // DH // 2
    G = HQ // HK
    KVS = 2
    QS = KVS * G
    STEPS = HK // KVS
    RH = QS + KVS
    NQ, NKV = QS * DH, 2 * KVS * DH
    UNITS = 6
    KT = STEPS * G

    X_SCALE, W_SCALE, QK_SCALE, O_SCALE = 2.0 ** 5, 2.0 ** 9, 2.0 ** 6, 2.0 ** 6
    ROPE_SCALE = QK_SCALE / (X_SCALE * W_SCALE)
    V_SCALE = O_SCALE / (X_SCALE * W_SCALE)
    SOFTMAX_SCALE = DH ** -0.5 / (QK_SCALE * QK_SCALE)
    OUT_SCALE = 1.0 / (O_SCALE * W_SCALE)
    EPS = 1e-5
    MASKED = -1e30
    assert rope.shape[1] == 2 and ROPE_SCALE == 2.0 ** -8

    ctx = ExitStack()
    with ctx:
        def sb(name, shape, dt):
            return ctx.enter_context(nc.sbuf_tensor(name, shape, dt))

        def pb(name):
            return ctx.enter_context(nc.psum_tensor(name, [P, 512], fp32))

        def sem(name):
            return ctx.enter_context(nc.semaphore(name))

        wq_stage = sb("wq_stage", [P, DB, HQ * DH], fp32)
        wkv_stage = sb("wkv_stage", [P, DB, 2 * HK * DH], fp32)
        wo_stage = sb("wo_stage", [P, KT, D], fp32)
        wq_hi, wq_lo = sb("wq_hi", [P, DB, HQ * DH], fp16), sb("wq_lo", [P, DB, HQ * DH], fp16)
        wkv_hi, wkv_lo = sb("wkv_hi", [P, DB, 2 * HK * DH], fp16), sb("wkv_lo", [P, DB, 2 * HK * DH], fp16)
        wo_hi, wo_lo = sb("wo_hi", [P, KT, D], fp16), sb("wo_lo", [P, KT, D], fp16)
        table = sb("table", [P, TT, 2, DH], fp32)
        ident32 = sb("ident32", [P, P], fp32)
        ident16 = sb("ident16", [P, P], fp16)
        identb = sb("identb", [P, P], bf16)
        causal = sb("causal", [P, 4, P], bf16)
        x_in = sb("x_in", [P, TT, D], fp32)
        x_res = sb("x_res", [P, TT, D], fp32)
        x_out = sb("x_out", [P, TT, D], fp32)
        x1_stats, x1_pair = sb("x1_stats", [P, TT, 6], fp32), sb("x1_pair", [P, TT, 2], fp32)
        stats = sb("stats", [P, TT, 6], fp32)
        moments = sb("moments", [P, TT, 2], fp32)
        eps = sb("eps", [P, 1], fp32)
        log_var, rough = sb("log_var", [P, TT], fp32), sb("rough", [P, TT], fp32)
        correction, rstd = sb("correction", [P, TT], fp32), sb("rstd", [P, TT], fp32)
        xn = sb("xn", [P, TT, D], fp32)
        xn_hi, xn_lo = sb("xn_hi", [P, TT, D], fp16), sb("xn_lo", [P, TT, D], fp16)
        xn_t = sb("xn_t", [P, TT, 2, DB, P], fp16)
        products = sb("products", [P, TT, 2, RH * DH], fp32)
        rotated = sb("rotated", [P, TT, RH * DH], fp32)
        stacked = sb("stacked", [P, TT, RH + KVS, 2, DH], fp16)
        q_t = sb("q_t", [P, 2, TT, QS, P], fp16)
        k_t = sb("k_t", [P, 2, 2, KVS, TT, P], fp16)
        values = sb("values", [P, STEPS, TT, KVS * DH], fp32)
        negmax = sb("negmax", [P, UNITS, G], fp32)
        bias = sb("bias", [P, UNITS, G], fp32)
        sums = sb("sums", [P, UNITS, G], fp32)
        inverse = sb("inverse", [P, UNITS, G], fp32)
        probs = sb("probs", [P, UNITS, 512], fp32)
        pt0 = sb("pt0", [P, KVS, G, P], fp32)
        pt1 = sb("pt1", [P, KVS, TT, G, P], fp32)
        o_hi, o_lo = sb("o_hi", [P, STEPS, G, SEQ], fp16), sb("o_lo", [P, STEPS, G, SEQ], fp16)

        scores = [pb(f"scores{i}") for i in range(3)]
        proj = ctx.enter_context(nc.psum_tensor("proj", [P, 1024], fp32))
        ring = [pb("ring0"), pb("ring1")]
        heads_out = pb("heads_out")

        s_wq, s_wkv, s_wo, s_table = [sem(f"s_wq{k}") for k in range(STEPS)], sem("s_wkv"), sem("s_wo"), sem("s_table")
        s_const = sem("s_const")
        s_w_hi, s_w_lo = sem("s_w_hi"), sem("s_w_lo")
        s_x, s_res, s_stored = sem("s_x"), sem("s_res"), sem("s_stored")
        s_stat, s_moments, s_rstd = sem("s_stat"), sem("s_moments"), sem("s_rstd")
        s_eps, s_rough = sem("s_eps"), sem("s_rough")
        s_x1_stat, s_x1_pair = sem("s_x1_stat"), sem("s_x1_pair")
        s_passed = sem("s_passed")
        s_xn, s_xn_hi, s_xn_lo = sem("s_xn"), sem("s_xn_hi"), sem("s_xn_lo")
        s_proj, s_mult, s_vals = sem("s_proj"), sem("s_mult"), sem("s_vals")
        s_rot, s_hi, s_lo, s_swap = sem("s_rot"), sem("s_hi"), sem("s_lo"), sem("s_swap")
        s_full = [sem("s_full0"), sem("s_full1")]
        s_free = [sem("s_free0"), sem("s_free1")]
        s_scores, s_max, s_bias = sem("s_scores"), sem("s_max"), sem("s_bias")
        s_exp, s_recip, s_norm = sem("s_exp"), sem("s_recip"), sem("s_norm")
        s_heads, s_o_hi, s_o_lo = sem("s_heads"), sem("s_o_hi"), sem("s_o_lo")
        s_wo_mm, s_sum = sem("s_wo_mm"), sem("s_sum")

        unit = [(0, 0, 0, G, P), (1, 0, 0, G, P)] + \
               [(j, 1, 2 * h, 2, SEQ) for j in range(KVS) for h in range(2)]

        LN_STEP = 1

        def ring_order(last):
            uses = []
            for p in range(STEPS):
                more = not (last and p == STEPS - 1)
                names = (["T0"] if more else []) + ["P0"] + (["T1", "T2"] if more else []) + \
                    ["P1", "P2", "P3"] + (["L0"] if p == LN_STEP and not last else []) + ["P4", "P5"] + \
                    (["L1"] if p == LN_STEP and not last else [])
                uses += [(p, n) for n in names]
            return uses

        RING_FIRST = ["L0", "L1", "T0", "T1", "T2"]
        RING_USES, RING_LAST = ring_order(False), ring_order(True)
        PER_BANK = len(RING_USES) // 2
        assert len(RING_USES) % 2 == 0

        def ring_use(b, p, name):
            if p < 0:
                i = RING_FIRST.index(name)
                return i % 2, i // 2 + 1
            uses = RING_LAST if isinstance(b, int) and b == n_seq - 1 else RING_USES
            i = uses.index((p, name))
            before = (len(RING_FIRST) + 1 - i % 2) // 2
            return i % 2, b * PER_BANK + (before + i // 2 + 1)

        def filled(eng, b, p, name):
            bank, n = ring_use(b, p, name)
            eng.wait_ge(s_full[bank], n)
            return ring[bank], s_free[bank]

        def emptied(eng, b, p, names):
            last = {}
            for name in names:
                bank, n = ring_use(b, p, name)
                last[bank] = n
            for bank, n in last.items():
                eng.wait_ge(s_free[bank], n)

        def previous_ring_use(pe, b, p, name):
            bank, n = ring_use(b, p, name)
            if not isinstance(n, int) or n > 1:
                pe.wait_ge(s_free[bank], n - 1)
            return ring[bank], s_full[bank]

        def per_step(b, p, each, n):
            return b * (STEPS * each) + (p * each + n)

        block = ctx.enter_context(nc.Block(name="attention"))

        @block.sync
        def _(sp):
            def load_queries(k):
                part = bass.ds(k * NQ, NQ)
                sp.dma_start(wq_stage[:, :, part], w_q.rearrange("(c p) n -> p c n", p=P)[:, :, part])\
                    .then_inc(s_wq[k], 16)

            sp.dma_start(x_in[:], x[0].rearrange("(t p) d -> p t d", p=P)).then_inc(s_x, 16)
            load_queries(0)
            sp.dma_start(wkv_stage[:], w_kv.rearrange("(c p) n -> p c n", p=P)).then_inc(s_wkv, 16)
            sp.dma_start(table[:], rope.rearrange("(t p) c d -> p t c d", p=P)).then_inc(s_table, 16)
            for k in range(1, STEPS):
                load_queries(k)
            wo_rows = w_o.rearrange("(s j g d) n -> j s d g n", j=KVS, g=G, d=DH)
            for j in range(KVS):
                for s in range(STEPS):
                    sp.dma_start(wo_stage[j * DH:(j + 1) * DH, s * G:(s + 1) * G, :],
                                 wo_rows[j, s]).then_inc(s_wo, 16)

            sp.dma_start(x_res[:], x[0].rearrange("(t p) d -> p t d", p=P)).then_inc(s_res, 16)

            def load_next(b):
                sp.wait_ge(s_xn, b + 1)
                sp.dma_start(x_in[:], x[b + 1].rearrange("(t p) d -> p t d", p=P)).then_inc(s_x, 16)

            def load_residual(b):
                sp.wait_ge(s_sum, per_step(b - 1, 0, 1, 1))
                sp.dma_start(x_res[:], x[b].rearrange("(t p) d -> p t d", p=P)).then_inc(s_res, 16)

            def store(b):
                sp.wait_ge(s_sum, per_step(b, 0, 1, STEPS))
                sp.dma_start(x1_dram[b].rearrange("(t p) d -> p t d", p=P), x_out[:]).then_inc(s_stored, 16)

            if n_seq > 1:
                load_next(0)
                load_residual(1)
            if n_seq > 2:
                with sp.Fori(1, n_seq - 1) as b:
                    load_next(b)
                    store(b - 1)
                    load_residual(b + 1)
            if n_seq > 1:
                store(n_seq - 2)
            store(n_seq - 1)
            sp.wait_ge(s_stored, 16 * n_seq)

        @block.gpsimd
        def _(pool):
            pool.memset(eps[:], EPS).then_inc(s_eps, 1)
            for m in (ident32, ident16, identb, causal):
                pool.memset(m[:], 0.0).then_inc(s_const, 1)
            pool.wait_ge(s_const, 4)
            for m in (ident32, ident16, identb):
                pool.affine_select(out=m[:], in_=m[:], compare_op=ALU.not_equal, fill=1.0, base=0,
                                   pattern=[[-1, P]], channel_multiplier=1).then_inc(s_const, 1)
            pool.affine_select(out=causal[:], in_=causal[:], compare_op=ALU.is_ge, fill=MASKED, base=0,
                               pattern=[[0, 4], [-1, P]], channel_multiplier=1).then_inc(s_const, 1)

            def rotate(b, p, t):
                pool.wait_ge(s_mult, per_step(b, p, TT, t + 1))
                halves = products[:, t].rearrange("p c (h a d) -> p c h a d", a=2, d=HALF)
                out = rotated[:, t].rearrange("p (h a d) -> p h a d", a=2, d=HALF)
                for a in range(2):
                    pool.tensor_tensor(out[:, :, a], halves[:, 0, :, a], halves[:, 1, :, 1 - a],
                                       ALU.add).then_inc(s_rot, 1)

            def low_parts(b, p, t):
                pool.wait_ge(s_hi, per_step(b, p, TT, t + 1))
                pool.wait_ge(s_rot, per_step(b, p, 2 * TT, 2 * t + 2))
                whole = rotated[:, t].rearrange("p (h d) -> p h d", d=DH)
                pool.tensor_tensor(stacked[:, t, 0:RH, 1], whole, stacked[:, t, 0:RH, 0],
                                   ALU.subtract).then_inc(s_lo, 1)

            def normalize(b, p, u):
                pool.wait_ge(s_recip, per_step(b, p, UNITS, u + 1))
                heads, keys = unit[u][3:]
                pr = probs[:, u].rearrange("p (h k) -> p h k", k=keys)
                pool.tensor_tensor(pr, pr, inverse[:, u, 0:heads].unsqueeze(2).broadcast_to(
                    [P, heads, keys]), ALU.mult).then_inc(s_norm, 1)

            def step(b, p, last):
                one, two = not last or p + 1 < STEPS, not last or p + 2 < STEPS
                if two:
                    rotate(b, p + 2, 0)
                normalize(b, p, 3)
                normalize(b, p, 4)
                normalize(b, p, 5)
                if two:
                    low_parts(b, p + 2, 0)
                if one:
                    normalize(b, p + 1, 0)
                if two:
                    rotate(b, p + 2, 1)
                    low_parts(b, p + 2, 1)
                if one:
                    normalize(b, p + 1, 1)
                    normalize(b, p + 1, 2)

            for p in range(2):
                for t in range(TT):
                    rotate(0, p, t)
                    low_parts(0, p, t)
            for u in range(3):
                normalize(0, 0, u)
            if n_seq > 1:
                with pool.Fori(0, n_seq - 1) as b:
                    for p in range(STEPS):
                        step(b, p, False)
            for p in range(STEPS):
                step(n_seq - 1, p, True)

        @block.scalar
        def _(act):
            def rough_rstd(b):
                act.wait_ge(s_moments, TT * b + TT)
                act.activation(log_var[:], moments[:, :, 1], ACT.Ln, bias=eps[:]).then_inc(s_rough, 1)
                act.wait_ge(s_rough, 2 * b + 1)
                act.activation(rough[:], log_var[:], ACT.Exp, scale=-0.5).then_inc(s_rough, 1)

            def high_xn(b):
                act.wait_ge(s_xn, b + 1)
                act.activation(xn_hi[:], xn[:], ACT.Copy, scale=X_SCALE).then_inc(s_xn_hi, 1)

            act.preload_act_table_set("natural_log_exp_and_others")
            act.wait_ge(s_eps, 1)
            rough_rstd(0)
            high_xn(0)

            def high_queries(k):
                act.wait_ge(s_wq[k], 16)
                part = bass.ds(k * NQ, NQ)
                act.activation(wq_hi[:, :, part], wq_stage[:, :, part], ACT.Copy, scale=W_SCALE).then_inc(s_w_hi, 1)

            def high_out(k):
                act.activation(wo_hi[:, k * G:(k + 1) * G], wo_stage[:, k * G:(k + 1) * G], ACT.Copy,
                               scale=W_SCALE).then_inc(s_w_hi, 1)

            high_queries(0)
            act.wait_ge(s_wkv, 16)
            act.activation(wkv_hi[:], wkv_stage[:], ACT.Copy, scale=W_SCALE).then_inc(s_w_hi, 1)

            def copy_values(b, p, t):
                act.wait_ge(s_mult, per_step(b, p, TT, t + 1))
                act.activation(values[:, p % STEPS, t], proj[:, NQ + KVS * DH:NQ + NKV], ACT.Copy,
                               scale=V_SCALE).then_inc(s_vals, 1)

            def exps(b, p, u):
                heads, keys = unit[u][3:]
                act.wait_ge(s_max, per_step(b, p, UNITS, u + 1))
                act.activation(bias[:, u, 0:heads], negmax[:, u, 0:heads], ACT.Copy, scale=SOFTMAX_SCALE).then_inc(s_bias, 1)
                act.wait_ge(s_bias, per_step(b, p, UNITS, u + 1))
                for h in range(heads):
                    last = act.activation(probs[:, u, h * keys:(h + 1) * keys],
                                          scores[u % 3][:, h * keys:(h + 1) * keys], ACT.Exp,
                                          bias=bias[:, u, h:h + 1], scale=SOFTMAX_SCALE,
                                          accum_out=sums[:, u, h:h + 1])
                last.then_inc(s_exp, 1)

            def copy_ln(b, p, t):
                bank, free = filled(act, b, p, f"L{t}")
                act.activation(xn_t[:, t].rearrange("p s c n -> p (s c n)"),
                               bank[:, :].bitcast(fp16)[:, 0:2 * D], ACT.Copy).then_inc(free, 1)

            def copy_p0(b, p, u):
                bank, free = filled(act, b, p, f"P{u}")
                act.activation(pt0[:, u].rearrange("p g n -> p (g n)"), bank[:, :], ACT.Copy).then_inc(free, 1)

            def copy_p1(b, p, u):
                j, _, h, _, _ = unit[u]
                bank, free = filled(act, b, p, f"P{u}")
                act.activation(pt1[:, j, :, h:h + 2, :], bank[:, :].rearrange("p (t g n) -> p t g n", t=TT, g=2),
                               ACT.Copy).then_inc(free, 1)

            def copy_k_t(b, p):
                bank, free = filled(act, b, p, "T2")
                act.activation(k_t[:, (p + 1) % 2].rearrange("p a j t n -> p (a j t n)"),
                               bank[:, :].bitcast(fp16), ACT.Copy).then_inc(free, 1)

            def heads_hi(b, p, t):
                act.wait_ge(s_heads, per_step(b, p, TT, t + 1))
                act.activation(o_hi[:, p, :, t * P:(t + 1) * P],
                               heads_out[:, :].rearrange("p (g n) -> p g n", g=G), ACT.Copy).then_inc(s_o_hi, 1)

            def step(b, p, last):
                one, two = not last or p + 1 < STEPS, not last or p + 2 < STEPS
                copy_p0(b, p, 0)
                if one:
                    copy_k_t(b, p)
                if p == 1 and not last:
                    high_xn(b + 1)
                if two:
                    copy_values(b, p + 2, 0)
                if p == 0 and not last:
                    rough_rstd(b + 1)
                exps(b, p, 5)
                if one:
                    exps(b, p + 1, 0)
                    exps(b, p + 1, 1)
                copy_p1(b, p, 2)
                copy_p1(b, p, 3)
                if p == LN_STEP and not last:
                    copy_ln(b, p, 0)
                if two:
                    copy_values(b, p + 2, 1)
                heads_hi(b, p, 0)
                copy_p1(b, p, 4)
                copy_p1(b, p, 5)
                if p == LN_STEP and not last:
                    copy_ln(b, p, 1)
                if one:
                    exps(b, p + 1, 2)
                    exps(b, p + 1, 3)
                heads_hi(b, p, 1)
                if one:
                    exps(b, p + 1, 4)

            for t in range(TT):
                copy_ln(0, -1, t)
            for k in range(1, STEPS):
                high_queries(k)
            for t in range(TT):
                copy_values(0, 0, t)
            act.wait_ge(s_wo, 16 * KVS * STEPS)
            for k in range(STEPS):
                high_out(k)
            copy_values(0, 1, 0)
            copy_k_t(0, -1)
            copy_values(0, 1, 1)
            for u in range(5):
                exps(0, 0, u)
            if n_seq > 1:
                with act.Fori(0, n_seq - 1) as b:
                    for p in range(STEPS):
                        step(b, p, False)
            for p in range(STEPS):
                step(n_seq - 1, p, True)

        @block.vector
        def _(dve):
            def norm_moments(b):
                dve.wait_ge(s_x, 16 * b + 16)
                for t in range(TT):
                    dve.bn_stats(stats[:, t], x_in[:, t]).then_inc(s_stat, 1)
                dve.wait_ge(s_stat, TT * b + TT)
                dve.sem_inc(s_passed, 1)
                for t in range(TT):
                    dve.bn_aggr(moments[:, t], stats[:, t]).then_inc(s_moments, 1)

            def norm_apply(b):
                dve.wait_ge(s_rough, 2 * b + 2)
                dve.tensor_tensor(correction[:], rough[:], rough[:], ALU.mult).then_inc(s_rstd, 1)
                dve.wait_ge(s_rstd, 4 * b + 1)
                dve.scalar_tensor_tensor(correction[:], moments[:, :, 1], EPS, correction[:], ALU.add,
                                         ALU.mult).then_inc(s_rstd, 1)
                dve.wait_ge(s_rstd, 4 * b + 2)
                dve.tensor_scalar(correction[:], correction[:], -0.5, 1.5, ALU.mult, ALU.add).then_inc(s_rstd, 1)
                dve.wait_ge(s_rstd, 4 * b + 3)
                dve.tensor_tensor(rstd[:], rough[:], correction[:], ALU.mult).then_inc(s_rstd, 1)
                dve.wait_ge(s_rstd, 4 * b + 4)
                for t in range(TT):
                    last = dve.tensor_scalar(xn[:, t], x_in[:, t], moments[:, t, 0:1], rstd[:, t:t + 1],
                                             ALU.subtract, ALU.mult)
                last.then_inc(s_xn, 1)

            def low_xn(b):
                dve.wait_ge(s_xn_hi, b + 1)
                dve.scalar_tensor_tensor(xn_lo[:], xn[:], X_SCALE, xn_hi[:], ALU.mult, ALU.subtract).then_inc(s_xn_lo, 1)

            def low_queries(k, done):
                dve.wait_ge(s_w_hi, done)
                part = bass.ds(k * NQ, NQ)
                dve.scalar_tensor_tensor(wq_lo[:, :, part], wq_stage[:, :, part], W_SCALE, wq_hi[:, :, part],
                                         ALU.mult, ALU.subtract).then_inc(s_w_lo, 1)

            def low_out(k):
                dve.wait_ge(s_w_hi, STEPS + k + 2)
                part = slice(k * G, (k + 1) * G)
                dve.scalar_tensor_tensor(wo_lo[:, part], wo_stage[:, part], W_SCALE, wo_hi[:, part],
                                         ALU.mult, ALU.subtract).then_inc(s_w_lo, 1)

            norm_moments(0)
            norm_apply(0)
            low_xn(0)
            low_queries(0, 1)
            dve.wait_ge(s_w_hi, 2)
            dve.scalar_tensor_tensor(wkv_lo[:], wkv_stage[:], W_SCALE, wkv_hi[:], ALU.mult, ALU.subtract).then_inc(s_w_lo, 1)
            low_queries(1, 3)
            dve.wait_ge(s_table, 16)

            def multiply(b, p, t):
                dve.wait_ge(s_proj, per_step(b, p, TT, t + 1))
                heads = proj[:, 0:RH * DH].rearrange("p (h d) -> p h d", d=DH)
                for c in range(2):
                    last = dve.tensor_tensor(products[:, t, c].rearrange("p (h d) -> p h d", d=DH), heads,
                                             table[:, t, c].unsqueeze(1).broadcast_to([P, RH, DH]), ALU.mult)
                last.then_inc(s_mult, 1)

            def high_parts(b, p, t):
                dve.wait_ge(s_rot, per_step(b, p, 2 * TT, 2 * t + 2))
                dve.tensor_copy(stacked[:, t, 0:RH, 0], rotated[:, t].rearrange("p (h d) -> p h d", d=DH))\
                    .then_inc(s_hi, 1)

            def swapped_keys(b, p, t):
                dve.wait_ge(s_lo, per_step(b, p, TT, t + 1))
                for a in range(2):
                    last = dve.tensor_copy(stacked[:, t, RH:RH + KVS, a], stacked[:, t, QS:RH, 1 - a])
                last.then_inc(s_swap, 1)

            def maxima(b, p, u):
                dve.wait_ge(s_scores, per_step(b, p, UNITS, u + 1))
                heads, keys = unit[u][3:]
                dve.tensor_reduce(negmax[:, u, 0:heads], scores[u % 3][:, :].rearrange(
                    "p (h k) -> p h k", k=keys), AX.X, ALU.max, negate=True).then_inc(s_max, 1)

            def recips(b, p, u):
                dve.wait_ge(s_exp, per_step(b, p, UNITS, u + 1))
                heads = unit[u][3]
                dve.reciprocal(inverse[:, u, 0:heads], sums[:, u, 0:heads]).then_inc(s_recip, 1)

            def copy_p0(b, p, u):
                bank, free = filled(dve, b, p, f"P{u}")
                dve.tensor_copy(pt0[:, u].rearrange("p g n -> p (g n)"), bank[:, :]).then_inc(free, 1)

            def copy_p1(b, p, u):
                j, _, h, _, _ = unit[u]
                bank, free = filled(dve, b, p, f"P{u}")
                dve.tensor_copy(pt1[:, j, :, h:h + 2, :], bank[:, :].rearrange("p (t g n) -> p t g n", t=TT, g=2))\
                    .then_inc(free, 1)

            def copy_q_t(b, p, t):
                bank, free = filled(dve, b, p, f"T{t}")
                dve.tensor_copy(q_t[:, (p + 1) % 2, t].rearrange("p h n -> p (h n)"),
                                bank[:, :].bitcast(fp16)).then_inc(free, 1)

            def heads_lo(b, p, t):
                dve.wait_ge(s_o_hi, per_step(b, p, TT, t + 1))
                dve.tensor_tensor(o_lo[:, p, :, t * P:(t + 1) * P],
                                  heads_out[:, :].rearrange("p (g n) -> p g n", g=G),
                                  o_hi[:, p, :, t * P:(t + 1) * P], ALU.subtract).then_inc(s_o_lo, 1)

            def add_heads(b, k):
                dve.wait_ge(s_wo_mm, per_step(b, k, 1, 1))
                if k == 0:
                    dve.wait_ge(s_res, 16 * b + 16)
                    if not (isinstance(b, int) and b == 0):
                        dve.wait_ge(s_stored, 16 * b)
                else:
                    dve.wait_ge(s_sum, per_step(b, k, 1, 0))
                dve.scalar_tensor_tensor(x_out[:].rearrange("p t d -> p (t d)"), heads_out[:, :], OUT_SCALE,
                                         (x_out if k else x_res)[:].rearrange("p t d -> p (t d)"), ALU.mult, ALU.add)\
                    .then_inc(s_sum, 1)

            def add_last_heads(b, p, after):
                if p:
                    add_heads(b, p - 1)
                elif after:
                    add_heads(b - 1, STEPS - 1)

            def result_moments(b):
                dve.wait_ge(s_sum, per_step(b, 0, 1, STEPS))
                for t in range(TT):
                    dve.bn_stats(x1_stats[:, t], x_out[:, t]).then_inc(s_x1_stat, 1)
                dve.wait_ge(s_x1_stat, b * TT + TT)
                dve.sem_inc(s_passed, 1)
                for t in range(TT):
                    last = dve.bn_aggr(x1_pair[:, t], x1_stats[:, t])
                last.then_inc(s_x1_pair, 1)
                dve.wait_ge(s_x1_pair, b + 1)
                dve.tensor_copy(x1_moments[:, bass.ds(b * TT, TT)], x1_pair[:])

            def step(b, p, last, after):
                one, two = not last or p + 1 < STEPS, not last or p + 2 < STEPS
                if one:
                    copy_q_t(b, p, 0)
                if p == 0 and not last:
                    norm_moments(b + 1)
                if two:
                    multiply(b, p + 2, 0)
                maxima(b, p, 5)
                if one:
                    copy_q_t(b, p, 1)
                recips(b, p, 3)
                recips(b, p, 4)
                if p == 0 and not last:
                    norm_apply(b + 1)
                if one:
                    maxima(b, p + 1, 0)
                if p == 1 and not last:
                    low_xn(b + 1)
                if one:
                    maxima(b, p + 1, 1)
                recips(b, p, 5)
                copy_p0(b, p, 1)
                if two:
                    high_parts(b, p + 2, 0)
                add_last_heads(b, p, after)
                if one:
                    recips(b, p + 1, 0)
                if two:
                    multiply(b, p + 2, 1)
                if one:
                    maxima(b, p + 1, 2)
                if p == 0 and after:
                    result_moments(b - 1)
                heads_lo(b, p, 0)
                if one:
                    maxima(b, p + 1, 3)
                if two:
                    high_parts(b, p + 2, 1)
                    swapped_keys(b, p + 2, 0)
                if one:
                    maxima(b, p + 1, 4)
                heads_lo(b, p, 1)
                if two:
                    swapped_keys(b, p + 2, 1)
                if one:
                    recips(b, p + 1, 1)
                    recips(b, p + 1, 2)

            multiply(0, 0, 0)
            low_queries(2, 4)
            high_parts(0, 0, 0)
            multiply(0, 0, 1)
            swapped_keys(0, 0, 0)
            low_queries(3, 5)
            high_parts(0, 0, 1)
            copy_q_t(0, -1, 0)
            multiply(0, 1, 0)
            swapped_keys(0, 0, 1)
            copy_q_t(0, -1, 1)
            low_out(0)
            filled(dve, 0, -1, "T2")
            high_parts(0, 1, 0)
            low_out(1)
            multiply(0, 1, 1)
            swapped_keys(0, 1, 0)
            low_out(2)
            high_parts(0, 1, 1)
            low_out(3)
            swapped_keys(0, 1, 1)
            for u in range(5):
                maxima(0, 0, u)
                if u < 3:
                    recips(0, 0, u)
            for p in range(STEPS):
                step(0, p, n_seq == 1, False)
            if n_seq > 2:
                with dve.Fori(1, n_seq - 1) as b:
                    for p in range(STEPS):
                        step(b, p, False, True)
            if n_seq > 1:
                for p in range(STEPS):
                    step(n_seq - 1, p, True, True)
            add_heads(n_seq - 1, STEPS - 1)
            result_moments(n_seq - 1)

        @block.tensor
        def _(pe):
            def norm_transposes(b, p, source, t):
                pe.wait_ge(s_xn_lo, source + 1)
                bank, full = previous_ring_use(pe, b, p, f"L{t}")
                out = bank[:, :].bitcast(fp16)
                for s, part in enumerate((xn_hi, xn_lo)):
                    for c in range(DB):
                        i = s * DB + c
                        last = pe.transpose(out[:, i * P:(i + 1) * P], part[:, t, c * P:(c + 1) * P], ident16[:])
                last.then_inc(full, 1)

            def project(b, p, t, before):
                if before:
                    pe.wait_ge(s_mult, per_step(b, p, TT, t))
                    pe.wait_ge(s_vals, per_step(b, p, TT, t))
                if before and p == STEPS:
                    emptied(pe, b, LN_STEP, ("L0", "L1"))
                k = p % STEPS
                wq = [w[:, :, k * NQ:(k + 1) * NQ] for w in (wq_hi, wq_lo)]
                wkv = [[w[:, c].rearrange("p (k s n) -> p s k n", k=2, s=STEPS)[:, k] for c in range(DB)]
                       for w in (wkv_hi, wkv_lo)]
                plan = [(s, c, w) for c in range(DB) for s, w in ((0, 0), (0, 1), (1, 0))]
                for i, (s, c, w) in enumerate(plan):
                    lhs = xn_t[:, t, s, c]
                    first, end = i == 0, i == len(plan) - 1
                    pe.matmul(proj[:, 0:NQ], lhs, wq[w][:, c], start=first, stop=end)
                    last = pe.matmul(proj[:, NQ:NQ + NKV].rearrange("p (k n) -> p k n", k=2), lhs, wkv[w][c], start=first, stop=end)
                last.then_inc(s_proj, 1)

            def head_transposes(b, p, n):
                t = min(n, 1)
                if n < 2:
                    pe.wait_ge(s_lo, per_step(b, p + 1, TT, t + 1))
                else:
                    pe.wait_ge(s_swap, per_step(b, p + 1, TT, 2))
                bank, full = previous_ring_use(pe, b, p, f"T{n}")
                out = bank[:, :].bitcast(fp16)
                if n < 2:
                    parts = [stacked[:, n, h] for h in range(QS)]
                else:
                    parts = [stacked[:, t, QS + KVS * a + j] for a in range(2) for j in range(KVS) for t in range(TT)]
                for i, part in enumerate(parts):
                    last = pe.transpose(out[:, i * P:(i + 1) * P], part.rearrange("p s d -> p (s d)"), ident16[:])
                last.then_inc(full, 1)

            def score(b, p, u):
                j, t, h0, heads, keys = unit[u]
                out = scores[u % 3]
                if u == 0:
                    emptied(pe, b, p - 1, ("T0", "T1", "T2"))
                if not (isinstance(b, int) and b == 0 and p == 0 and u < 3):
                    pe.wait_ge(s_exp, per_step(b, p, UNITS, u - 2))
                if keys == P:
                    pe.matmul(out[:, :], identb[:], causal[:].rearrange("p h k -> p (h k)"),
                              start=True, stop=False, skip_group_check=True)
                else:
                    pe.matmul(out[:, :].rearrange("p (h t k) -> p h t k", h=2, t=TT)[:, :, 1], identb[:],
                              causal[:, 0:2], start=True, stop=False, skip_group_check=True)
                for i in range(heads):
                    for a in range(2):
                        last = pe.matmul(out[:, i * keys:(i + 1) * keys], q_t[:, p % 2, t, j * G + h0 + i],
                                         k_t[:, p % 2, a, j].rearrange("p t n -> p (t n)")[:, 0:keys],
                                         start=False, stop=i == heads - 1 and a == 1, skip_group_check=True)
                last.then_inc(s_scores, 1)

            def prob_transposes(b, p, u):
                j, t, h0, heads, keys = unit[u]
                pe.wait_ge(s_norm, per_step(b, p, UNITS, u + 1))
                bank, full = previous_ring_use(pe, b, p, f"P{u}")
                for i in range(4):
                    kb, h = divmod(i, heads) if keys > P else (0, i)
                    last = pe.transpose(bank[:, i * P:(i + 1) * P],
                                        probs[:, u, h * keys + kb * P:h * keys + (kb + 1) * P], ident32[:])
                last.then_inc(full, 1)

            def heads_product(b, p, t, free):
                emptied(pe, b, p, [f"P{u}" for u in ((0, 1) if t == 0 else (2, 3, 4, 5))])
                pe.wait_ge(s_vals, per_step(b, p, TT, TT))
                free()
                for kb in range(t + 1):
                    for j in range(KVS):
                        rhs = pt0[:, j] if t == 0 else pt1[:, j, kb]
                        last = pe.matmul(heads_out[j * DH:(j + 1) * DH, :], values[:, p % STEPS, kb, j * DH:(j + 1) * DH],
                                         rhs.rearrange("p g n -> p (g n)"), start=kb == 0, stop=kb == t,
                                         skip_group_check=True)
                last.then_inc(s_heads, 1)

            def out_projection(b, k, t):
                if t == 0:
                    pe.wait_ge(s_o_lo, per_step(b, k, TT, TT))
                for g in range(G):
                    for n, (o, w) in enumerate(((o_hi, wo_hi), (o_hi, wo_lo), (o_lo, wo_hi))):
                        last = pe.matmul(heads_out[:, t * D:(t + 1) * D], o[:, k, g, t * P:(t + 1) * P],
                                         w[:, k * G + g], start=g == 0 and n == 0, stop=g == G - 1 and n == 2)
                if t == TT - 1:
                    last.then_inc(s_wo_mm, 1)

            def step(b, p, last, after):
                one, two = not last or p + 1 < STEPS, not last or p + 2 < STEPS

                def out_part(t):
                    if p:
                        out_projection(b, p - 1, t)
                    elif after:
                        out_projection(b - 1, STEPS - 1, t)

                def out_bank_read():
                    if p or after:
                        pe.wait_ge(s_sum, per_step(b, p, 1, 0))

                if one:
                    head_transposes(b, p, 0)
                prob_transposes(b, p, 0)
                if two:
                    project(b, p + 2, 0, True)
                score(b, p, 5)
                if one:
                    head_transposes(b, p, 1)
                    head_transposes(b, p, 2)
                out_part(0)
                out_part(1)
                if one:
                    score(b, p + 1, 0)
                prob_transposes(b, p, 1)
                if one:
                    score(b, p + 1, 1)
                if two:
                    project(b, p + 2, 1, True)
                prob_transposes(b, p, 2)
                prob_transposes(b, p, 3)
                if one:
                    score(b, p + 1, 2)
                if p == LN_STEP and not last:
                    norm_transposes(b, p, b + 1, 0)
                heads_product(b, p, 0, out_bank_read)
                prob_transposes(b, p, 4)
                prob_transposes(b, p, 5)
                if one:
                    score(b, p + 1, 3)
                if p == LN_STEP and not last:
                    norm_transposes(b, p, b + 1, 1)
                if one:
                    score(b, p + 1, 4)
                heads_product(b, p, 1, lambda: pe.wait_ge(s_o_lo, per_step(b, p, TT, 1)))

            pe.wait_ge(s_const, 8)
            for t in range(TT):
                norm_transposes(0, -1, 0, t)
            emptied(pe, 0, -1, ("L0", "L1"))
            pe.wait_ge(s_w_lo, 2)
            for t in range(TT):
                project(0, 0, t, t > 0)
            head_transposes(0, -1, 0)
            pe.wait_ge(s_w_lo, 3)
            project(0, 1, 0, True)
            for n in range(1, 3):
                head_transposes(0, -1, n)
            project(0, 1, 1, True)
            for u in range(5):
                score(0, 0, u)
            pe.wait_ge(s_w_lo, 2 * STEPS + 1)
            for p in range(STEPS):
                step(0, p, n_seq == 1, False)
            if n_seq > 2:
                with pe.Fori(1, n_seq - 1) as b:
                    for p in range(STEPS):
                        step(b, p, False, True)
            if n_seq > 1:
                for p in range(STEPS):
                    step(n_seq - 1, p, True, True)
            for t in range(TT):
                out_projection(n_seq - 1, STEPS - 1, t)


def moe_blocks(nc, x1_dram, moments, gate_w, gate_up, down, shared_gate_up, shared_down, shared_gate, rows_dram,
               hidden_dram, base_dram, out, n_seq):
    fp32, fp16, u32, i32 = mybir.dt.float32, mybir.dt.float16, mybir.dt.uint32, mybir.dt.int32
    ALU, ACT, AX = mybir.AluOpType, mybir.ActivationFunctionType, mybir.AxisListType

    P = 128
    D = gate_w.shape[1]
    DB = D // P
    E = gate_w.shape[0]
    I = down.shape[2]
    SI = shared_down.shape[1]
    TOPK = 4
    HB = 88
    NHB = I // HB
    SB = -(-SI // P)
    GT = 4
    N = GT * P
    TOKENS = n_seq * x1_dram.shape[1]
    GROUPS = TOKENS // N
    TILES = TOKENS // P
    WAVES = 2
    WAVE_TILES = TILES // WAVES
    REGION = WAVE_TILES * P + P
    SLOT_TILES = WAVE_TILES * TOPK + E
    U = 4
    SLOT_TILES = -(-SLOT_TILES // U) * U
    SPARE = SLOT_TILES - WAVE_TILES * TOPK
    assert NHB * HB == I and GROUPS * N == TOKENS and E % 2 == 0 and GROUPS % (2 * WAVES) == 0
    assert rows_dram[0].shape[0] == E * REGION + SPARE * P and hidden_dram[0].shape[0] == SLOT_TILES * P

    X_SCALE, W_SCALE, H_SCALE = 2.0 ** 5, 2.0 ** 9, 2.0 ** 4
    UP_SCALE = 1.0 / (X_SCALE * W_SCALE)
    DOWN_SCALE = 1.0 / (H_SCALE * W_SCALE)
    EPS = 1e-5
    SPLIT = ((0, 0), (0, 1), (1, 0))

    keep = ExitStack()
    with keep:
        def kept(name, shape, dt):
            return keep.enter_context(nc.sbuf_tensor(name, shape, dt))

        gu_t = [kept(f"gu_t{s}", [P, DB, E * 2 * I], fp16) for s in range(2)]
        dn_t = [kept(f"dn_t{s}", [HB, E, NHB * D], fp16) for s in range(2)]
        sgu_t = [kept(f"sgu_t{s}", [P, DB, 2 * SI], fp16) for s in range(2)]
        sdn_t = [kept(f"sdn_t{s}", [P, SB, D], fp16) for s in range(2)]
        router_t = [kept(f"router_t{s}", [P, DB, E + 1], fp16) for s in range(2)]
        ident32, ident16 = kept("m_ident32", [P, P], fp32), kept("m_ident16", [P, P], fp16)
        places = kept("places", [P, TILES * TOPK], fp32)
        choices = kept("choices", [P, TILES * TOPK], fp32)
        shares = kept("shares", [P, TILES * TOPK], fp32)
        counts = [kept(f"counts{w}", [P, E], fp32) for w in range(WAVES)]
        chosen = kept("chosen", [P, GT + 1, E], fp16)

        prepare_weights(nc, gate_w, gate_up, down, shared_gate_up, shared_down, shared_gate,
                        gu_t, dn_t, sgu_t, sdn_t, router_t, ident32, ident16, W_SCALE)

        ctx = ExitStack()
        with ctx:
            def sb(name, shape, dt):
                return ctx.enter_context(nc.sbuf_tensor(name, shape, dt))

            def pb(name):
                return ctx.enter_context(nc.psum_tensor(name, [P, 512], fp32))

            def sem(name):
                return ctx.enter_context(nc.semaphore(name))

            strict, ones = sb("strict", [P, P], fp16), sb("ones", [P, P], fp16)
            expert_ids = sb("expert_ids", [P, TOPK, E], fp32)
            regions = sb("regions", [P, E], fp32)
            eps = sb("m_eps", [P, 1], fp32)
            zeros = sb("zeros", [P, 2 * D], fp16)
            x1 = sb("x1", [P, 2, GT, D], fp32)
            log_var, rough = sb("m_log_var", [P, TILES], fp32), sb("m_rough", [P, TILES], fp32)
            correction, rstd = sb("m_correction", [P, TILES], fp32), sb("m_rstd", [P, TILES], fp32)
            xn = sb("m_xn", [P, GT, D], fp32)
            rows = sb("rows", [P, 2, GT, 2, D], fp16)
            xt = sb("xt", [P, 2, 2, DB, N], fp16)
            logits = sb("logits", [P, GT, E + 1], fp32)
            negmax, sums = sb("m_negmax", [P, GT], fp32), sb("m_sums", [P, GT], fp32)
            probs = sb("m_probs", [P, GT, E], fp32)
            top, index = sb("top", [P, GT, 8], fp32), sb("index", [P, GT, 8], u32)
            indexf = sb("indexf", [P, GT, 8], fp32)
            hot, at = sb("hot", [P, GT, TOPK, E], fp32), sb("at", [P, GT, TOPK, E], fp32)
            chosen_now = sb("chosen_now", [P, GT, E], fp16)
            row_of = sb("row_of", [P, GT, E], fp32)
            share, share_sum = sb("share", [P, GT, TOPK], fp32), sb("share_sum", [P, GT], fp32)
            place = sb("place", [P, GT * TOPK], fp32)
            placeu = sb("placeu", [P, 2, GT * TOPK], u32)
            tail, tail_rows = sb("tail", [1, WAVES, E], fp32), sb("tail_rows", [1, WAVES, E], i32)
            sigmoid = sb("sigmoid", [P, 2, GT], fp32)
            silu = sb("silu", [P, 2, N], fp32)
            h = sb("h", [P, 2, N], fp32)
            h_hi, h_lo = sb("h_hi", [P, SB, N], fp16), sb("h_lo", [P, SB, N], fp16)
            base = sb("base", [P, GT, D], fp32)

            turned, small = pb("turned"), pb("small")
            gates, ups = [pb("gates0"), pb("gates1")], [pb("ups0"), pb("ups1")]
            downs = [pb("downs0"), pb("downs1")]

            s_residual = sem("r_residual")
            s_const, s_x1, s_rough = sem("r_const"), [sem("r_x1_0"), sem("r_x1_1")], sem("r_rough")
            s_rstd, s_xn, s_rows_hi, s_rows = sem("r_rstd"), sem("r_xn"), sem("r_rows_hi"), sem("r_rows")
            s_turned, s_xt, s_logits_mm, s_logits = sem("r_turned"), sem("r_xt"), sem("r_logits_mm"), sem("r_logits")
            s_negmax, s_probs, s_dve = sem("r_negmax"), sem("r_probs"), sem("r_dve")
            s_chosen, s_rank, s_place, s_scattered = sem("r_chosen"), sem("r_rank"), sem("r_place"), [sem("r_scattered0"), sem("r_scattered1")]
            s_gu, s_silu, s_h, s_h_hi, s_h_lo = sem("r_gu"), sem("r_silu"), sem("r_h"), sem("r_h_hi"), sem("r_h_lo")
            s_down, s_base, s_stored, s_zero, s_tail = sem("r_down"), sem("r_base"), sem("r_stored"), sem("r_zero"), sem("r_tail")
            s_at = sem("r_at")
            s_passed, s_pool_passed = sem("r_passed"), sem("r_pool_passed")

            by_group = lambda a, g: a[g * GT:(g + 1) * GT]
            x1_rows = x1_dram.rearrange("b (t p) d -> p (b t) d", p=P)
            base_rows = base_dram.rearrange("b (t p) d -> p (b t) d", p=P)

            def per_group(g, each, n):
                return g * each + n

            ROUTER_STEPS = 14

            def passes(g, half):
                return g // 2 if isinstance(g, int) else (g - half) // 2

            def block_rows(k):
                return min(P, SI - k * P)

            def zeros_behind(eng, wave, experts):
                eng.wait_ge(s_tail, 2 * (wave + 1))
                for e in experts:
                    row = eng.value_load(tail_rows[0:1, wave, e:e + 1], min_val=0, max_val=E * REGION - P)
                    eng.dma_start(rows_dram[wave][bass.ds(row, P), :], zeros[:]).then_inc(s_zero, 16)

            def each_group(eng, group):
                pairs = GROUPS // 2
                for wave in range(WAVES):
                    first, end = wave * pairs // WAVES, (wave + 1) * pairs // WAVES - 1
                    if wave == 0 and end > 0:
                        for half in range(2):
                            group(half, half, None)
                        first = 1
                    if end > first:
                        with eng.Fori(first, end) as gg:
                            for half in range(2):
                                group(gg * 2 + half, half, None)
                    group(2 * end, 0, None)
                    group(2 * end + 1, 1, wave)

            block = ctx.enter_context(nc.Block(name="route"))

            @block.sync
            def _(sp):
                def load(g, half):
                    sp.dma_start(x1[:, half], x1_rows[:, bass.ds(g * GT, GT)]).then_inc(s_x1[half], 16)

                def load_residual(g):
                    sp.dma_start(base[:], x1_rows[:, bass.ds(g * GT, GT)]).then_inc(s_residual, 16)

                def store(g):
                    sp.wait_ge(s_base, (g + 1) * GT)
                    sp.dma_start(base_rows[:, bass.ds(g * GT, GT)], base[:]).then_inc(s_stored, 16)

                def group(g, half, more):
                    store(g)
                    sp.wait_ge(s_stored, g * 16 + 16)
                    load_residual(g + 1)
                    if more:
                        sp.wait_ge(s_xn, g + 2)
                        load(g + 3, 1 - half)

                load(0, 0)
                load(1, 1)
                load_residual(0)
                sp.wait_ge(s_const, 1)
                for k in range(SPARE):
                    r = E * REGION + k * P
                    for wave in range(WAVES):
                        sp.dma_start(rows_dram[wave][r:r + P, :], zeros[:]).then_inc(s_zero, 16)
                sp.wait_ge(s_xn, 1)
                load(2, 0)
                MIDDLE = GROUPS // WAVES
                if MIDDLE > 2:
                    with sp.Fori(0, MIDDLE // 2 - 1) as gg:
                        for half in range(2):
                            group(gg * 2 + half, half, True)
                group(MIDDLE - 2, 0, True)
                zeros_behind(sp, 0, range(E))
                group(MIDDLE - 1, 1, MIDDLE + 2 < GROUPS)
                if GROUPS - 4 > MIDDLE:
                    with sp.Fori(MIDDLE // 2, GROUPS // 2 - 2) as gg:
                        for half in range(2):
                            group(gg * 2 + half, half, True)
                for g in range(max(GROUPS - 4, MIDDLE), GROUPS - 1):
                    group(g, g % 2, g + 3 < GROUPS)
                zeros_behind(sp, 1, range(E // 2))
                store(GROUPS - 1)
                sp.wait_ge(s_stored, 16 * GROUPS)
                sp.wait_ge(s_zero, 16 * WAVES * (SPARE + E))

            @block.gpsimd
            def _(pool):
                pool.memset(zeros[:], 0.0).then_inc(s_const, 1)
                pool.memset(strict[:], 1.0).then_inc(s_const, 1)
                pool.memset(ones[:], 1.0).then_inc(s_const, 1)
                pool.memset(eps[:], EPS).then_inc(s_const, 1)
                pool.memset(chosen[:], 0.0).then_inc(s_const, 1)
                pool.iota(expert_ids[:], pattern=[[0, TOPK], [1, E]], base=0, channel_multiplier=0,
                          allow_small_or_imprecise_dtypes=True).then_inc(s_const, 1)
                pool.iota(regions[:], pattern=[[REGION, E]], base=0, channel_multiplier=0,
                          allow_small_or_imprecise_dtypes=True).then_inc(s_const, 1)
                pool.iota(tail[:], pattern=[[0, WAVES], [REGION, E]], base=0, channel_multiplier=0,
                          allow_small_or_imprecise_dtypes=True).then_inc(s_const, 1)
                pool.wait_ge(s_const, 8)
                pool.affine_select(out=strict[:], in_=strict[:], compare_op=ALU.is_gt, fill=0.0, base=0,
                                   pattern=[[1, P]], channel_multiplier=-1).then_inc(s_const, 1)

                def scatter(g, half, wave):
                    pool.wait_ge(s_place, g + 1)
                    pool.sem_inc(s_pool_passed, 1)
                    for t in range(GT):
                        for k in range(TOPK):
                            i = t * TOPK + k
                            pool.indirect_dma_start(
                                rows_dram[wave], bass.IndirectOffsetOnAxis(ap=placeu[:, half, i:i + 1], axis=0),
                                rows[:, half, t].rearrange("p s d -> p (s d)"), None).then_inc(s_scattered[half], 16)

                pairs = GROUPS // 2 // WAVES
                for wave in range(WAVES):
                    with pool.Fori(wave * pairs, (wave + 1) * pairs) as gg:
                        for half in range(2):
                            scatter(gg * 2 + half, half, wave)
                for half in range(2):
                    pool.wait_ge(s_scattered[half], 16 * TILES * TOPK // 2)

            @block.scalar
            def _(act):
                act.wait_ge(s_const, 9)

                def high_rows(g, half):
                    act.wait_ge(s_xn, g + 1)
                    if not (isinstance(g, int) and g < 2):
                        act.wait_ge(s_scattered[half], passes(g, half) * (16 * GT * TOPK))
                    act.activation(rows[:, half, :, 0], xn[:], ACT.Copy, scale=X_SCALE).then_inc(s_rows_hi, 1)

                def router(g, half):
                    act.wait_ge(s_negmax, g + 1)
                    for t in range(GT):
                        act.activation(probs[:, t], logits[:, t, 0:E], ACT.Exp, bias=negmax[:, t:t + 1],
                                       accum_out=sums[:, t:t + 1])
                    act.activation(sigmoid[:, half], logits[:, :, E], ACT.Exp, scale=-1.0).then_inc(s_probs, 1)

                def shared(g, k):
                    n = block_rows(k)
                    act.wait_ge(s_gu, per_group(g, SB, k + 1))
                    act.activation(silu[0:n, k % 2], gates[k % 2][0:n, :], ACT.Silu, scale=UP_SCALE).then_inc(s_silu, 1)
                    act.wait_ge(s_h, per_group(g, SB, k + 1))
                    act.activation(h_hi[0:n, k], h[0:n, k % 2], ACT.Copy).then_inc(s_h_hi, 1)

                def group(g, half, ends):
                    last = ends == WAVES - 1
                    for k in range(SB):
                        shared(g, k)
                        if k == 0 and not last:
                            high_rows(g + 1, 1 - half)
                    if not last:
                        router(g + 1, 1 - half)

                act.activation(log_var[:], moments[:, :, 1], ACT.Ln, bias=eps[:]).then_inc(s_rough, 1)
                act.wait_ge(s_rough, 1)
                act.activation(rough[:], log_var[:], ACT.Exp, scale=-0.5).then_inc(s_rough, 1)
                high_rows(0, 0)
                router(0, 0)
                each_group(act, group)
                zeros_behind(act, 1, range(E // 2, E))

            @block.vector
            def _(dve):
                dve.wait_ge(s_const, 9)

                def all_rstd():
                    dve.wait_ge(s_rough, 2)
                    dve.tensor_tensor(correction[:], rough[:], rough[:], ALU.mult).then_inc(s_rstd, 1)
                    dve.wait_ge(s_rstd, 1)
                    dve.scalar_tensor_tensor(correction[:], moments[:, :, 1], EPS, correction[:], ALU.add,
                                             ALU.mult).then_inc(s_rstd, 1)
                    dve.wait_ge(s_rstd, 2)
                    dve.tensor_scalar(correction[:], correction[:], -0.5, 1.5, ALU.mult, ALU.add).then_inc(s_rstd, 1)
                    dve.wait_ge(s_rstd, 3)
                    dve.tensor_tensor(rstd[:], rough[:], correction[:], ALU.mult).then_inc(s_rstd, 1)
                    dve.wait_ge(s_rstd, 4)

                def norm(g, half):
                    dve.wait_ge(s_x1[half], passes(g, half) * 16 + 16)
                    for t in range(GT):
                        i = bass.ds(g * GT + t, 1)
                        last = dve.tensor_scalar(xn[:, t], x1[:, half, t],
                                                 moments[:, i, 0:1].rearrange("p a b -> p (a b)"), rstd[:, i],
                                                 ALU.subtract, ALU.mult)
                    last.then_inc(s_xn, 1)

                def low_rows(g, half):
                    dve.wait_ge(s_rows_hi, g + 1)
                    dve.scalar_tensor_tensor(rows[:, half, :, 1], xn[:], X_SCALE, rows[:, half, :, 0],
                                             ALU.mult, ALU.subtract).then_inc(s_rows, 1)

                def transposed(g, half, s):
                    dve.wait_ge(s_turned, per_group(g, 2, s + 1))
                    dve.tensor_copy(xt[:, half, s].rearrange("p c n -> p (c n)"), turned[:, :].bitcast(fp16)).then_inc(s_xt, 1)

                def router(g, half, part, ends=None):
                    done = [(0, 1, 6, ROUTER_STEPS - 1)[part]]

                    def link(ins, apart=False):
                        done[0] += 1
                        ins.then_inc(s_dve, 1)
                        dve.wait_ge(s_dve, g * ROUTER_STEPS + done[0])
                        if apart:
                            dve.sem_inc(s_passed, 1)

                    if part == 0:
                        dve.wait_ge(s_logits_mm, g + 1)
                        link(dve.tensor_scalar(logits[:], small[:, 0:GT * (E + 1)].rearrange("p (t e) -> p t e", t=GT),
                                               UP_SCALE, None, ALU.mult))
                        dve.tensor_reduce(negmax[:], logits[:, :, 0:E], AX.X, ALU.max, negate=True).then_inc(s_negmax, 1)
                    if part == 1:
                        dve.wait_ge(s_probs, g + 1)
                        link(dve.reciprocal(sums[:], sums[:]))
                        link(dve.tensor_tensor(probs[:], probs[:], sums[:].unsqueeze(2).broadcast_to([P, GT, E]), ALU.mult), apart=True)
                        for t in range(GT):
                            ins = dve.max(top[:, t], probs[:, t])
                        link(ins, apart=True)
                        for t in range(GT):
                            ins = dve.max_index(index[:, t], top[:, t], probs[:, t])
                        link(ins)
                        link(dve.tensor_copy(indexf[:], index[:]))
                    if part == 2:
                        for t in range(GT):
                            ins = dve.tensor_tensor(hot[:, t], expert_ids[:], indexf[:, t, 0:TOPK].unsqueeze(2)
                                                    .broadcast_to([P, TOPK, E]), ALU.is_equal)
                        link(ins)
                        for t in range(GT):
                            with nc.allow_low_precision(reason="a sum of at most one 1 and zeros"):
                                ins = dve.tensor_reduce(chosen_now[:, t], hot[:, t].rearrange("p k e -> p e k"), AX.X, ALU.add)
                        link(ins)
                        for t in range(GT):
                            ins = dve.tensor_tensor(chosen[:, t + 1], chosen[:, t], chosen_now[:, t], ALU.add)
                            if t < GT - 1:
                                ins.then_inc(s_chosen, 1)
                                dve.wait_ge(s_chosen, g * (GT + 1) + t + 1)
                        ins.then_inc(s_chosen, 1)
                        link(dve.tensor_reduce(share_sum[:], top[:, :, 0:TOPK], AX.X, ALU.add))
                        link(dve.reciprocal(share_sum[:], share_sum[:]))
                        dve.tensor_tensor(shares[:, bass.ds(g * (GT * TOPK), GT * TOPK)].rearrange("p (t k) -> p t k", k=TOPK),
                                          top[:, :, 0:TOPK], share_sum[:].unsqueeze(2).broadcast_to([P, GT, TOPK]), ALU.mult)
                        link(dve.tensor_scalar(sigmoid[:, half], sigmoid[:, half], 1.0, None, ALU.add))
                        link(dve.reciprocal(sigmoid[:, half], sigmoid[:, half]))
                        link(dve.tensor_scalar(sigmoid[:, half], sigmoid[:, half], DOWN_SCALE, None, ALU.mult))
                        assert done[0] == ROUTER_STEPS - 1
                    if part == 3:
                        dve.wait_ge(s_rank, g + 1)
                        if ends is not None:
                            dve.tensor_tensor(tail[:, ends], tail[:, ends], small[0:1, 256:256 + E], ALU.add).then_inc(s_tail, 1)
                            dve.tensor_copy(counts[ends][:], small[:, 256:256 + E])
                            dve.wait_ge(s_tail, 2 * ends + 1)
                            dve.tensor_copy(tail_rows[:, ends], tail[:, ends]).then_inc(s_tail, 1)
                        if ends is None:
                            dve.tensor_copy(chosen[:, 0], chosen[:, GT]).then_inc(s_chosen, 1)
                        else:
                            dve.memset(chosen[:, 0], 0.0).then_inc(s_chosen, 1)
                        link(dve.tensor_tensor(row_of[:], small[:, 128:128 + GT * E].rearrange("p (t e) -> p t e", t=GT),
                                               regions[:].unsqueeze(1).broadcast_to([P, GT, E]), ALU.add))

                def place_rows(g, half):
                    dve.wait_ge(s_chosen, (g + 1) * (GT + 1))
                    for t in range(GT):
                        ins = dve.tensor_tensor(at[:, t], hot[:, t], row_of[:, t].unsqueeze(1)
                                                .broadcast_to([P, TOPK, E]), ALU.mult)
                    ins.then_inc(s_at, 1)
                    dve.wait_ge(s_at, 2 * g + 1)
                    dve.tensor_reduce(place[:], at[:].rearrange("p t k e -> p (t k) e"), AX.X, ALU.add).then_inc(s_at, 1)
                    dve.wait_ge(s_at, 2 * g + 2)
                    dve.tensor_copy(placeu[:, half], place[:]).then_inc(s_place, 1)
                    dve.tensor_copy(choices[:, bass.ds(g * (GT * TOPK), GT * TOPK)].rearrange("p (t k) -> p t k", k=TOPK),
                                    indexf[:, :, 0:TOPK])
                    dve.tensor_copy(places[:, bass.ds(g * (GT * TOPK), GT * TOPK)], place[:])

                def shared(g, half, k):
                    n = block_rows(k)
                    dve.wait_ge(s_silu, per_group(g, SB, k + 1))
                    dve.scalar_tensor_tensor(h[0:n, k % 2], ups[k % 2][0:n, :], UP_SCALE * H_SCALE, silu[0:n, k % 2],
                                             ALU.mult, ALU.mult).then_inc(s_h, 1)
                    dve.wait_ge(s_h_hi, per_group(g, SB, k + 1))
                    dve.tensor_tensor(h_lo[0:n, k], h[0:n, k % 2], h_hi[0:n, k], ALU.subtract).then_inc(s_h_lo, 1)

                def add_base(g, half):
                    dve.wait_ge(s_residual, g * 16 + 16)
                    dve.wait_ge(s_down, g + 1)
                    for t in range(GT):
                        dve.scalar_tensor_tensor(base[:, t], downs[t // 2][:, (t % 2) * D:(t % 2 + 1) * D],
                                                 sigmoid[:, half, t:t + 1], base[:, t], ALU.mult, ALU.add).then_inc(s_base, 1)

                def group(g, half, ends):
                    last = ends == WAVES - 1
                    router(g, half, 1)
                    for k in range(SB):
                        shared(g, half, k)
                        if k == 0:
                            if not last:
                                norm(g + 1, 1 - half)
                            router(g, half, 2)
                        if k == 1:
                            router(g, half, 3, ends)
                            place_rows(g, half)
                            if not last:
                                low_rows(g + 1, 1 - half)
                        if k in (3, 4) and not last:
                            transposed(g + 1, 1 - half, k - 3)
                    if not last:
                        router(g + 1, 1 - half, 0)
                    add_base(g, half)

                all_rstd()
                norm(0, 0)
                low_rows(0, 0)
                for s in range(2):
                    transposed(0, 0, s)
                router(0, 0, 0)
                each_group(dve, group)

            @block.tensor
            def _(pe):
                pe.wait_ge(s_const, 9)

                def transposes(g, half, s):
                    if s == 0:
                        pe.wait_ge(s_rows, g + 1)
                    if s or not (isinstance(g, int) and g == 0):
                        pe.wait_ge(s_xt, per_group(g, 2, s))
                    bank = turned[:, :].bitcast(fp16)
                    for c in range(DB):
                        for t in range(GT):
                            i = c * GT + t
                            last = pe.transpose(bank[:, i * P:(i + 1) * P],
                                                rows[:, half, t, s, c * P:(c + 1) * P], ident16[:])
                    last.then_inc(s_turned, 1)

                def route(g, half):
                    pe.wait_ge(s_xt, per_group(g, 2, 2))
                    if not (isinstance(g, int) and g == 0):
                        pe.wait_ge(s_dve, g * ROUTER_STEPS)
                    for t in range(GT):
                        n = 0
                        for c in range(DB):
                            for a, w in SPLIT:
                                last = pe.matmul(small[:, t * (E + 1):(t + 1) * (E + 1)], xt[:, half, a, c, t * P:(t + 1) * P],
                                                 router_t[w][:, c], start=n == 0, stop=n == 3 * DB - 1)
                                n += 1
                    last.then_inc(s_logits_mm, 1)

                def ranks(g, ends):
                    pe.wait_ge(s_chosen, g * (GT + 1) + GT)
                    for t in range(GT):
                        out_ = small[:, 128 + t * E:128 + (t + 1) * E]
                        pe.matmul(out_, strict[:], chosen_now[:, t], start=True, stop=False)
                        ins = pe.matmul(out_, ones[:], chosen[:, t], start=False, stop=True)
                    if ends is not None:
                        ins = pe.matmul(small[:, 256:256 + E], ones[:], chosen[:, GT], start=True, stop=True)
                    ins.then_inc(s_rank, 1)

                def shared_up(g, half, k):
                    n = block_rows(k)
                    if k >= 2 or not (isinstance(g, int) and g == 0):
                        pe.wait_ge(s_h, per_group(g, SB, k - 1))
                    for bank, first in ((gates[k % 2], 0), (ups[k % 2], SI)):
                        i = 0
                        for c in range(DB):
                            for w, a in SPLIT:
                                last = pe.matmul(bank[0:n, :], sgu_t[w][:, c, first + k * P:first + k * P + n],
                                                 xt[:, half, a, c], start=i == 0, stop=i == 3 * DB - 1)
                                i += 1
                    last.then_inc(s_gu, 1)

                def shared_down(g, k):
                    n = block_rows(k)
                    pe.wait_ge(s_h_lo, per_group(g, SB, k + 1))
                    if k == 0 and not (isinstance(g, int) and g == 0):
                        pe.wait_ge(s_base, g * GT)
                    for t in range(GT):
                        for i, (a, w) in enumerate(SPLIT):
                            hh = (h_hi, h_lo)[a]
                            last = pe.matmul(downs[t // 2][:, (t % 2) * D:(t % 2 + 1) * D], hh[0:n, k, t * P:(t + 1) * P],
                                             sdn_t[w][0:n, k], start=k == 0 and i == 0 and t % 2 == 0, stop=k == SB - 1 and i == 2,
                                             skip_group_check=True)
                    if k == SB - 1:
                        last.then_inc(s_down, 1)

                def group(g, half, ends):
                    last = ends == WAVES - 1
                    for k in range(SB):
                        shared_up(g, half, k)
                        if k == 2:
                            ranks(g, ends)
                        if k in (3, 4) and not last:
                            transposes(g + 1, 1 - half, k - 3)
                        if k == 5 and not last:
                            route(g + 1, 1 - half)
                        if k >= 2:
                            shared_down(g, k - 2)
                    for k in (SB - 2, SB - 1):
                        shared_down(g, k)

                for s in range(2):
                    transposes(0, 0, s)
                route(0, 0)
                each_group(pe, group)

        def of_wave(w):
            tiles, cols = slice(w * WAVE_TILES, (w + 1) * WAVE_TILES), slice(w * WAVE_TILES * TOPK, (w + 1) * WAVE_TILES * TOPK)
            rows = lambda a: a.rearrange("b (t p) d -> p (b t) d", p=P)[:, tiles]
            return rows(base_dram), hidden_dram[w], places[:, cols], shares[:, cols], rows(out)

        for w in range(WAVES):
            cols = slice(w * WAVE_TILES * TOPK, (w + 1) * WAVE_TILES * TOPK)
            experts_block(nc, w, rows_dram[w], hidden_dram[w], counts[w], places[:, cols], choices[:, cols], gu_t, dn_t,
                          ident32, ident16, SLOT_TILES, U, REGION, UP_SCALE, H_SCALE, DOWN_SCALE,
                          of_wave(w - 1) if w else None)
        combine_block(nc, *of_wave(WAVES - 1))


def prepare_weights(nc, gate_w, gate_up, down, shared_gate_up, shared_down, shared_gate,
                    gu_t, dn_t, sgu_t, sdn_t, router_t, ident32, ident16, W_SCALE):
    fp32, fp16 = mybir.dt.float32, mybir.dt.float16
    ALU, ACT = mybir.AluOpType, mybir.ActivationFunctionType
    P = 128
    E, D = gate_w.shape
    DB = D // P
    I = down.shape[2]
    SI = shared_down.shape[1]
    HB = dn_t[0].shape[0]
    NHB = I // HB
    FB = 2 * NHB
    SLOTS = 4
    BANKS, EACH = 6, 1 + DB
    assert BANKS == 2 * EACH and E % SLOTS == 0

    ctx = ExitStack()
    with ctx:
        def sb(name, shape, dt):
            return ctx.enter_context(nc.sbuf_tensor(name, shape, dt))

        def sem(name):
            return ctx.enter_context(nc.semaphore(name))

        gu = sb("gu", [HB, SLOTS, FB, D], fp32)
        dn = sb("dn", [P, SLOTS, DB, I], fp32)
        sgu = sb("sgu", [HB, 2 * SI // HB, D], fp32)
        sdn = sb("sdn", [P, DB, SI], fp32)
        router = sb("router", [E + 1, D], fp32)
        banks = [ctx.enter_context(nc.psum_tensor(f"w_bank{i}", [P, 512], fp32)) for i in range(BANKS)]
        s_const, s_turned, s_high, s_low = sem("w_const"), sem("w_turned"), sem("w_high"), sem("w_low")
        s_expert, s_rest = [sem(f"w_expert{i}") for i in range(SLOTS)], sem("w_rest")

        block = ctx.enter_context(nc.Block(name="weights"))

        rest = [("sgu", c, q) for c in range(DB) for q in range(2 * SI // (FB * HB))]
        rest += [("sdn", k, n) for k, n in ((0, 2), (2, 2), (4, 1), (5, 1))] + [("router", 0, 0)]

        def rest_parts(kind, a, n, bank, dst):
            if kind == "sgu":
                return bank[:, 0:FB * HB], dst["sgu"][:, a, n * FB * HB:(n + 1) * FB * HB]
            if kind == "sdn":
                r = min(P, SI - a * P)
                return bank[0:r, 0:n * D], dst["sdn"][0:r, a:a + n].rearrange("p k d -> p (k d)")
            return bank[:, 0:DB * (E + 1)], dst["router"][:].rearrange("p c e -> p (c e)")

        @block.sync
        def _(sp):
            def load(e, slot):
                sp.dma_start(gu[:, slot], gate_up[e].rearrange("(b r) d -> r b d", r=HB)).then_inc(s_expert[slot], 16)
                sp.dma_start(dn[:, slot], down[e].rearrange("(t p) i -> p t i", p=P)).then_inc(s_expert[slot], 16)

            for slot in range(SLOTS):
                load(slot, slot)
            with sp.Fori(0, E // SLOTS - 1) as ee:
                for slot in range(SLOTS):
                    sp.wait_ge(s_turned, ee * (SLOTS * EACH) + (slot + 1) * EACH)
                    load(ee * SLOTS + (SLOTS + slot), slot)
            sp.dma_start(sgu[:], shared_gate_up.rearrange("(b r) d -> r b d", r=HB)).then_inc(s_rest, 16)
            sp.dma_start(sdn[:], shared_down.rearrange("(t p) i -> p t i", p=P)).then_inc(s_rest, 16)
            sp.dma_start(router[0:E, :], gate_w).then_inc(s_rest, 16)
            sp.dma_start(router[E:E + 1, :], shared_gate).then_inc(s_rest, 16)

        @block.gpsimd
        def _(pool):
            for m in (ident32, ident16):
                pool.memset(m[:], 0.0).then_inc(s_const, 1)
            pool.wait_ge(s_const, 2)
            for m in (ident32, ident16):
                pool.affine_select(out=m[:], in_=m[:], compare_op=ALU.not_equal, fill=1.0, base=0,
                                   pattern=[[-1, P]], channel_multiplier=1).then_inc(s_const, 1)

        @block.tensor
        def _(pe):
            pe.wait_ge(s_const, 4)

            def free(fill):
                if not isinstance(fill, int) or fill >= BANKS:
                    pe.wait_ge(s_low, fill - BANKS + 1)

            def expert(e, slot, turn):
                half = slot % 2
                pe.wait_ge(s_expert[slot], turn * 32 + 32)
                for c in range(DB):
                    free(e * EACH + c)
                    for b in range(FB):
                        last = pe.transpose(banks[half * EACH + c][:, b * HB:(b + 1) * HB],
                                            gu[:, slot, b, c * P:(c + 1) * P], ident32[0:HB, 0:HB])
                    last.then_inc(s_turned, 1)
                free(e * EACH + DB)
                for b in range(NHB):
                    for t in range(DB):
                        last = pe.transpose(banks[half * EACH + DB][0:HB, b * D + t * P:b * D + (t + 1) * P],
                                            dn[:, slot, t, b * HB:(b + 1) * HB], ident32[:])
                last.then_inc(s_turned, 1)

            for slot in range(SLOTS):
                expert(slot, slot, 0)
            with pe.Fori(1, E // SLOTS) as ee:
                for slot in range(SLOTS):
                    expert(ee * SLOTS + slot, slot, ee)
            pe.wait_ge(s_rest, 64)
            for i, (kind, a, n) in enumerate(rest):
                fill = E * EACH + i
                free(fill)
                bank = banks[fill % BANKS]
                if kind == "sgu":
                    for b in range(FB):
                        last = pe.transpose(bank[:, b * HB:(b + 1) * HB], sgu[:, n * FB + b, a * P:(a + 1) * P],
                                            ident32[0:HB, 0:HB])
                elif kind == "sdn":
                    for k in range(n):
                        r = min(P, SI - (a + k) * P)
                        for t in range(DB):
                            last = pe.transpose(bank[0:r, k * D + t * P:k * D + (t + 1) * P],
                                                sdn[:, t, (a + k) * P:(a + k) * P + r], ident32[:])
                else:
                    for c in range(DB):
                        last = pe.transpose(bank[:, c * (E + 1):(c + 1) * (E + 1)], router[:, c * P:(c + 1) * P],
                                            ident32[0:E + 1, 0:E + 1])
                last.then_inc(s_turned, 1)

        def split(eng, part, fill, bank, dst):
            if part == 0:
                eng.wait_ge(s_turned, fill + 1)
                eng.activation(dst[0], bank, ACT.Copy, scale=W_SCALE).then_inc(s_high, 1)
            else:
                eng.wait_ge(s_high, fill + 1)
                eng.scalar_tensor_tensor(dst[1], bank, W_SCALE, dst[0], ALU.mult, ALU.subtract).then_inc(s_low, 1)

        def split_all(eng, part):
            def expert(e, half):
                for c in range(DB):
                    split(eng, part, e * EACH + c, banks[half * EACH + c][:, 0:2 * I],
                          [w[:, c, bass.ds(e * (2 * I), 2 * I)] for w in gu_t])
                split(eng, part, e * EACH + DB, banks[half * EACH + DB][0:HB, 0:NHB * D],
                      [w[:, bass.ds(e, 1)].rearrange("p e n -> p (e n)") for w in dn_t])

            with eng.Fori(0, E // 2) as ee:
                for half in range(2):
                    expert(ee * 2 + half, half)
            for i, (kind, a, n) in enumerate(rest):
                fill = E * EACH + i
                dst = [dict(sgu=sgu_t[s], sdn=sdn_t[s], router=router_t[s]) for s in range(2)]
                parts = [rest_parts(kind, a, n, banks[fill % BANKS], d) for d in dst]
                split(eng, part, fill, parts[0][0], [x[1] for x in parts])

        @block.scalar
        def _(act):
            split_all(act, 0)

        @block.vector
        def _(dve):
            split_all(dve, 1)


def experts_block(nc, wave, rows_dram, hidden_dram, counts, places, choices, gu_t, dn_t, ident32, ident16,
                  SLOT_TILES, U, REGION, UP_SCALE, H_SCALE, DOWN_SCALE, earlier):
    fp32, fp16, i32 = mybir.dt.float32, mybir.dt.float16, mybir.dt.int32
    ALU, ACT, AX = mybir.AluOpType, mybir.ActivationFunctionType, mybir.AxisListType
    P = 128
    DB = gu_t[0].shape[1]
    D = DB * P
    E = counts.shape[1]
    I2 = gu_t[0].shape[2] // E
    HB = dn_t[0].shape[0]
    I = I2 // 2
    NHB = I // HB
    MOST = (REGION - P) // P
    PASSES = SLOT_TILES // U
    SPLIT = ((0, 0), (0, 1), (1, 0))

    ctx = ExitStack()
    with ctx:
        def sb(name, shape, dt):
            return ctx.enter_context(nc.sbuf_tensor(f"{name}_{wave}", shape, dt))

        def pb(name):
            return ctx.enter_context(nc.psum_tensor(f"{name}_{wave}", [P, 512], fp32))

        def sem(name):
            return ctx.enter_context(nc.semaphore(f"{name}_{wave}"))

        thresholds = sb("thresholds", [P, E, MOST], fp32)
        fuller = sb("fuller", [P, E, MOST], fp32)
        not_after = sb("not_after", [P, E, E], fp32)
        ahead = sb("ahead", [P, E, E], fp32)
        tiles, ends = sb("tiles", [P, E], fp32), sb("ends", [P, E], fp32)
        shift = sb("shift", [P, E], fp32)
        expert_ids = sb("e_expert_ids", [P, E], fp32)
        is_choice = sb("is_choice", [P, places.shape[1], E], fp32)
        moved = sb("moved", [P, places.shape[1]], fp32)
        C = -(-SLOT_TILES // P)
        slot_ids = sb("slot_ids", [P, C], fp32)
        past = sb("past", [P, C, E], fp32)
        expert_of, first_of = sb("expert_of", [P, C], fp32), sb("first_of", [P, C], fp32)
        experts = sb("experts", [1, C * P], i32)
        slot_rows = sb("slot_rows", [1, C * P], i32)

        x_in = sb("e_x_in", [P, U, 2 * D], fp16)
        xt = sb("e_xt", [P, 2, 2, DB, P], fp16)
        silu, h = sb("e_silu", [P, 2, I], fp32), sb("e_h", [P, 2, I], fp32)
        h_parts = sb("e_h_parts", [P, 2, 2, I], fp16)
        ht = sb("e_ht", [HB, 2, 2, NHB, P], fp16)
        y = sb("e_y", [P, U, D], fp32)
        turned, h_turned = [pb("e_turned0"), pb("e_turned1")], [pb("e_h_turned0"), pb("e_h_turned1")]
        gu, yb = [pb("e_gu0"), pb("e_gu1")], [pb("e_y0"), pb("e_y1")]

        s_const, s_plan, s_planned = sem("e_const"), sem("e_plan"), sem("e_planned")
        s_slots, s_slots_turned = sem("e_slots"), sem("e_slots_turned")
        s_in, s_out = [sem(f"e_in{u}") for u in range(U)], [sem(f"e_out{u}") for u in range(U)]
        s_turned, s_xt, s_gu, s_silu = sem("e_turned"), sem("e_xt"), sem("e_gu"), sem("e_silu")
        s_h, s_h_hi, s_h_lo, s_down, s_y = sem("e_h"), sem("e_h_hi"), sem("e_h_lo"), sem("e_down"), sem("e_y")
        s_h_turned, s_ht = sem("e_h_turned_s"), sem("e_ht_s")

        block = ctx.enter_context(nc.Block(name=f"experts{wave}"))

        @block.gpsimd
        def _(pool):
            iota = dict(channel_multiplier=0, allow_small_or_imprecise_dtypes=True)
            pool.iota(thresholds[:], pattern=[[0, E], [P, MOST]], base=0, **iota).then_inc(s_const, 1)
            pool.iota(expert_ids[:], pattern=[[1, E]], base=0, **iota).then_inc(s_const, 1)
            pool.iota(slot_ids[:], pattern=[[P, C]], base=0, channel_multiplier=1,
                      allow_small_or_imprecise_dtypes=True).then_inc(s_const, 1)
            pool.memset(not_after[:], 1.0).then_inc(s_const, 1)
            pool.wait_ge(s_const, 4)
            pool.affine_select(out=not_after[:], in_=not_after[:], compare_op=ALU.is_ge, fill=0.0, base=0,
                               pattern=[[1, E], [-1, E]], channel_multiplier=0).then_inc(s_const, 1)
            if earlier:
                combine_on_gpsimd(nc, ctx, pool, *earlier)

        @block.vector
        def _(dve):
            done = [0]

            def link(ins):
                done[0] += 1
                ins.then_inc(s_plan, 1)
                dve.wait_ge(s_plan, done[0])

            dve.wait_ge(s_const, 5)
            link(dve.tensor_tensor(fuller[:], counts[:].unsqueeze(2).broadcast_to([P, E, MOST]), thresholds[:], ALU.is_gt))
            link(dve.tensor_reduce(tiles[:], fuller[:], AX.X, ALU.add))
            link(dve.tensor_tensor(ahead[:], tiles[:].unsqueeze(1).broadcast_to([P, E, E]), not_after[:], ALU.mult))
            link(dve.tensor_reduce(ends[:], ahead[:], AX.X, ALU.add))
            link(dve.tensor_tensor(past[:], ends[:].unsqueeze(1).broadcast_to([P, C, E]),
                                   slot_ids[:].unsqueeze(2).broadcast_to([P, C, E]), ALU.is_le))
            link(dve.tensor_reduce(expert_of[:], past[:], AX.X, ALU.add))
            link(dve.tensor_tensor(past[:], past[:], tiles[:].unsqueeze(1).broadcast_to([P, C, E]), ALU.mult))
            link(dve.tensor_reduce(first_of[:], past[:], AX.X, ALU.add))
            link(dve.tensor_tensor(first_of[:], slot_ids[:], first_of[:], ALU.subtract))
            link(dve.tensor_scalar(first_of[:], first_of[:], float(P), None, ALU.mult))
            dve.scalar_tensor_tensor(first_of[:], expert_of[:], float(REGION), first_of[:], ALU.mult, ALU.add)\
                .then_inc(s_slots, 1)
            dve.wait_ge(s_slots, 1)
            dve.tensor_scalar(expert_of[:], expert_of[:], float(E - 1), None, ALU.min).then_inc(s_slots, 1)
            dve.wait_ge(s_slots_turned, 1)
            dve.tensor_copy(experts[:], turned[0][0:1, 0:C * P])
            dve.tensor_copy(slot_rows[:], turned[0][0:1, C * P:2 * C * P]).then_inc(s_planned, 1)

            def move_places():
                link(dve.tensor_tensor(shift[:], ends[:], tiles[:], ALU.subtract))
                link(dve.tensor_scalar(shift[:], shift[:], float(P), None, ALU.mult))
                link(dve.scalar_tensor_tensor(shift[:], expert_ids[:], -float(REGION), shift[:], ALU.mult, ALU.add))
                T = places.shape[1]
                link(dve.tensor_tensor(is_choice[:], choices.unsqueeze(2).broadcast_to([P, T, E]),
                                       expert_ids[:].unsqueeze(1).broadcast_to([P, T, E]), ALU.is_equal))
                link(dve.tensor_tensor(is_choice[:], is_choice[:], shift[:].unsqueeze(1).broadcast_to([P, T, E]), ALU.mult))
                link(dve.tensor_reduce(moved[:], is_choice[:], AX.X, ALU.add))
                link(dve.tensor_tensor(places, places, moved[:], ALU.add))

            move_places()

            def copy_xt(n, u):
                dve.wait_ge(s_turned, n + 1)
                dve.tensor_copy(xt[:, u % 2].rearrange("p s c n -> p (s c n)"),
                                turned[u % 2][:, :].bitcast(fp16)[:, 0:2 * D]).then_inc(s_xt, 1)

            def hidden(n, u):
                dve.wait_ge(s_silu, n + 1)
                dve.scalar_tensor_tensor(h[:, u % 2], gu[u % 2][:, I:2 * I], UP_SCALE * H_SCALE,
                                         silu[:, u % 2], ALU.mult, ALU.mult).then_inc(s_h, 1)
                dve.wait_ge(s_h_hi, n + 1)
                dve.tensor_tensor(h_parts[:, u % 2, 1], h[:, u % 2], h_parts[:, u % 2, 0],
                                  ALU.subtract).then_inc(s_h_lo, 1)

            def copy_ht(n, u):
                dve.wait_ge(s_h_turned, n + 1)
                dve.tensor_copy(ht[:, u % 2].rearrange("p s b n -> p (s b n)"),
                                h_turned[u % 2][0:HB, :].bitcast(fp16)[:, 0:2 * NHB * P]).then_inc(s_ht, 1)

            for n in range(3):
                copy_xt(n, n)
            hidden(0, 0)
            copy_ht(0, 0)
            hidden(1, 1)

            def tile(n, u, i=None):
                if i is None or i + 3 < SLOT_TILES:
                    copy_xt(n + 3, (u + 3) % U)
                if i is None or i + 1 < SLOT_TILES:
                    copy_ht(n + 1, (u + 1) % U)
                if i is None or i + 2 < SLOT_TILES:
                    hidden(n + 2, (u + 2) % U)

            with dve.Fori(0, PASSES - 1) as q:
                for u in range(U):
                    tile(q * U + u, u)
            for u in range(U):
                tile((PASSES - 1) * U + u, u, (PASSES - 1) * U + u)

        @block.sync
        def _(sp):
            sp.wait_ge(s_planned, 1)

            def rows_at(i):
                return sp.value_load(slot_rows[0:1, i], min_val=0, max_val=rows_dram.shape[0] - P)

            def load_next(n, u):
                row = rows_at(bass.ds(n + U, 1))
                sp.wait_ge(s_turned, n + 1)
                load(n + U, u, row)

            def load(n, u, row):
                sp.dma_start(x_in[:, u], rows_dram[bass.ds(row, P), :]).then_inc(s_in[u], 16)

            def store(n, u):
                sp.wait_ge(s_y, n + 1)
                sp.dma_start(hidden_dram[bass.ds(n * P, P), :], y[:, u]).then_inc(s_out[u], 16)

            for u in range(U):
                load(u, u, rows_at(bass.ds(u, 1)))
            for u in range(U):
                load_next(u, u)
                if u >= 2:
                    store(u - 2, u - 2)
            with sp.Fori(1, PASSES - 1) as q:
                for u in range(U):
                    load_next(q * U + u, u)
                    store(q * U + (u - 2), (u - 2) % U)
            for n in range((PASSES - 1) * U - 2, SLOT_TILES):
                store(n, n % U)
            for u in range(U):
                sp.wait_ge(s_out[u], 16 * PASSES)

        @block.scalar
        def _(act):
            def gate(n, u):
                act.wait_ge(s_gu, n + 1)
                act.activation(silu[:, u % 2], gu[u % 2][:, 0:I], ACT.Silu, scale=UP_SCALE).then_inc(s_silu, 1)
                act.wait_ge(s_h, n + 1)
                act.activation(h_parts[:, u % 2, 0], h[:, u % 2], ACT.Copy).then_inc(s_h_hi, 1)

            for n in range(2):
                gate(n, n)

            def tile(n, u, q, i=None):
                if i is None or i + 2 < SLOT_TILES:
                    gate(n + 2, (u + 2) % U)
                act.wait_ge(s_down, n + 1)
                if not (isinstance(q, int) and q == 0):
                    act.wait_ge(s_out[u], q * 16)
                act.activation(y[:, u], yb[u % 2][:, 0:D], ACT.Copy, scale=DOWN_SCALE).then_inc(s_y, 1)

            for u in range(U):
                tile(u, u, 0)
            with act.Fori(1, PASSES - 1) as q:
                for u in range(U):
                    tile(q * U + u, u, q)
            for u in range(U):
                n = (PASSES - 1) * U + u
                tile(n, u, PASSES - 1, n)

        @block.tensor
        def _(pe):
            pe.wait_ge(s_slots, 2)
            for i in range(2 * C):
                last = pe.transpose(turned[0][0:1, i * P:(i + 1) * P], (expert_of, first_of)[i // C][:, i % C:i % C + 1],
                                    ident32[:])
            last.then_inc(s_slots_turned, 1)
            pe.wait_ge(s_planned, 1)

            def experts_at(n, count):
                return nc.values_load_multi_w_load_instructions(
                    experts[0:1, bass.ds(n, count)], [pe.engine], min_val=0, max_val=E - 1,
                    skip_runtime_bounds_check_because="the plan bounds it by E - 1")[1]

            def transposes(n, u, p):
                pe.wait_ge(s_in[u], p * 16 + 16)
                if not isinstance(n, int) or n >= 2:
                    pe.wait_ge(s_xt, n - 1)
                for i in range(2 * DB):
                    last = pe.transpose(turned[u % 2][:, :].bitcast(fp16)[:, i * P:(i + 1) * P],
                                        x_in[:, u, i * P:(i + 1) * P], ident16[:])
                last.then_inc(s_turned, 1)

            def up(n, u, e):
                pe.wait_ge(s_xt, n + 1)
                if not isinstance(n, int) or n >= 2:
                    pe.wait_ge(s_h, n - 1)
                k = 0
                for c in range(DB):
                    for a, w in SPLIT:
                        last = pe.matmul(gu[u % 2][:, 0:I2], xt[:, u % 2, a, c], gu_t[w][:, c, bass.ds(e * I2, I2)],
                                         start=k == 0, stop=k == 3 * DB - 1)
                        k += 1
                last.then_inc(s_gu, 1)

            def h_transposes(n, u):
                pe.wait_ge(s_h_lo, n + 1)
                if not isinstance(n, int) or n >= 2:
                    pe.wait_ge(s_ht, n - 1)
                for a in range(2):
                    for b in range(NHB):
                        i = a * NHB + b
                        last = pe.transpose(h_turned[u % 2][0:HB, :].bitcast(fp16)[:, i * P:(i + 1) * P],
                                            h_parts[:, u % 2, a, b * HB:(b + 1) * HB], ident16[:])
                last.then_inc(s_h_turned, 1)

            def down(n, u, e):
                pe.wait_ge(s_ht, n + 1)
                if not isinstance(n, int) or n >= 2:
                    pe.wait_ge(s_y, n - 1)
                k = 0
                for b in range(NHB):
                    for a, w in SPLIT:
                        last = pe.matmul(yb[u % 2][:, 0:D], ht[:, u % 2, a, b],
                                         dn_t[w][:, bass.ds(e, 1), b * D:(b + 1) * D].rearrange("p e n -> p (e n)"),
                                         start=k == 0, stop=k == 3 * NHB - 1)
                        k += 1
                last.then_inc(s_down, 1)

            def tile(n, u, q, es, i=None):
                if i is None or i + 3 < SLOT_TILES:
                    transposes(n + 3, (u + 3) % U, q + (u + 3) // U)
                if i is None or i + 2 < SLOT_TILES:
                    up(n + 2, (u + 2) % U, es[u + 2])
                if i is None or i + 1 < SLOT_TILES:
                    h_transposes(n + 1, (u + 1) % U)
                down(n, u, es[u])

            es = experts_at(0, U + 2)
            for n in range(3):
                transposes(n, n, 0)
                if n < 2:
                    up(n, n, es[n])
            h_transposes(0, 0)
            for u in range(U):
                tile(u, u, 0, es)
            with pe.Fori(1, PASSES - 1) as q:
                es = experts_at(q * U, U + 2)
                for u in range(U):
                    tile(q * U + u, u, q, es)
            es = experts_at((PASSES - 1) * U, U)
            for u in range(U):
                n = (PASSES - 1) * U + u
                tile(n, u, PASSES - 1, es, n)


def combine_on_gpsimd(nc, ctx, pool, base_rows, hidden_dram, places, shares, out_rows):
    fp32, u32 = mybir.dt.float32, mybir.dt.uint32
    ALU = mybir.AluOpType
    P, GT = 128, 4
    D = out_rows.shape[2]
    TILES = out_rows.shape[1]
    TOPK = places.shape[1] // TILES
    W = GT * TOPK

    def sb(name, shape, dt):
        return ctx.enter_context(nc.sbuf_tensor(name, shape, dt))

    def sem(name):
        return ctx.enter_context(nc.semaphore(name))

    place, share = sb("g_place", [P, W], u32), sb("g_share", [P, W], fp32)
    got, acc = sb("g_got", [P, GT, TOPK, D], fp32), sb("g_acc", [P, GT, D], fp32)
    s_place, s_base, s_sum, s_out = sem("g_place_s"), sem("g_base"), sem("g_sum"), sem("g_out")
    s_got, s_weighted, s_passed = sem("g_got"), sem("g_weighted"), sem("g_passed")

    def group(g):
        cols = bass.ds(g * W, W)
        pool.tensor_copy(place[:], places[:, cols]).then_inc(s_place, 1)
        pool.tensor_copy(share[:], shares[:, cols]).then_inc(s_place, 1)
        if not isinstance(g, int):
            pool.wait_ge(s_out, g * 16)
            pool.sem_inc(s_passed, 1)
        pool.dma_start(acc[:], base_rows[:, bass.ds(g * GT, GT)]).then_inc(s_base, 16)
        pool.wait_ge(s_place, g * 2 + 2)
        pool.sem_inc(s_passed, 1)
        for t in range(GT):
            for k in range(TOPK):
                i = t * TOPK + k
                pool.indirect_dma_start(got[:, t, k], None, hidden_dram,
                                        bass.IndirectOffsetOnAxis(ap=place[:, i:i + 1], axis=0)).then_inc(s_got, 16)
        pool.wait_ge(s_got, g * (16 * W) + 16 * W)
        for t in range(GT):
            pool.tensor_tensor(got[:, t], got[:, t], share[:, t * TOPK:(t + 1) * TOPK].unsqueeze(2).broadcast_to(
                [P, TOPK, D]), ALU.mult).then_inc(s_weighted, 1)
        pool.wait_ge(s_base, g * 16 + 16)
        pool.wait_ge(s_weighted, g * GT + GT)
        for k in range(TOPK):
            if k:
                pool.wait_ge(s_sum, g * TOPK + k)
            pool.tensor_tensor(acc[:], acc[:], got[:, :, k], ALU.add).then_inc(s_sum, 1)
        pool.wait_ge(s_sum, g * TOPK + TOPK)
        pool.sem_inc(s_passed, 1)
        pool.dma_start(out_rows[:, bass.ds(g * GT, GT)], acc[:]).then_inc(s_out, 16)

    group(0)
    if TILES > GT:
        with pool.Fori(1, TILES // GT) as g:
            group(g)
    pool.wait_ge(s_out, 16 * (TILES // GT))


def combine_block(nc, base_rows, hidden_dram, places, shares, out_rows):
    fp32, u32 = mybir.dt.float32, mybir.dt.uint32
    ALU = mybir.AluOpType
    P, GT = 128, 4
    D = out_rows.shape[2]
    TILES = out_rows.shape[1]
    TOPK = places.shape[1] // TILES
    GROUPS = TILES // GT
    W = GT * TOPK

    ctx = ExitStack()
    with ctx:
        def sb(name, shape, dt):
            return ctx.enter_context(nc.sbuf_tensor(name, shape, dt))

        def sem(name):
            return ctx.enter_context(nc.semaphore(name))

        place, share = sb("c_place", [P, 2, W], u32), sb("c_share", [P, 2, W], fp32)
        got = sb("c_got", [P, 2, GT, TOPK, D], fp32)
        acc = sb("c_acc", [P, 2, GT, D], fp32)
        s_place, s_share = sem("c_place_s"), sem("c_share_s")
        s_got = [[sem(f"c_got{half}{two}") for two in range(2)] for half in range(2)]
        s_base, s_sum, s_out = [sem("c_base0"), sem("c_base1")], sem("c_sum"), [sem("c_out0"), sem("c_out1")]
        s_link, s_passed = sem("c_link"), sem("c_passed")

        block = ctx.enter_context(nc.Block(name="combine"))

        @block.sync
        def _(sp):
            def load(g, half):
                sp.dma_start(acc[:, half], base_rows[:, bass.ds(g * GT, GT)]).then_inc(s_base[half], 16)

            def store(g, half):
                sp.wait_ge(s_sum, (g + 1) * GT)
                sp.dma_start(out_rows[:, bass.ds(g * GT, GT)], acc[:, half]).then_inc(s_out[half], 16)

            for half in range(2):
                load(half, half)
            if GROUPS > 2:
                with sp.Fori(0, GROUPS // 2 - 1) as gg:
                    for half in range(2):
                        store(gg * 2 + half, half)
                        sp.wait_ge(s_out[half], gg * 16 + 16)
                        load(gg * 2 + (half + 2), half)
            for half in range(2):
                store(GROUPS - 2 + half, half)
            for half in range(2):
                sp.wait_ge(s_out[half], 16 * GROUPS // 2)

        def each_group(eng, group):
            for half in range(2):
                group(half, half, 0)
            if GROUPS > 2:
                with eng.Fori(1, GROUPS // 2) as gg:
                    for half in range(2):
                        group(gg * 2 + half, half, gg)

        @block.gpsimd
        def _(pool):
            def group(g, half, gg):
                pool.wait_ge(s_place, g + 1)
                pool.sem_inc(s_passed, 1)
                for t in range(GT):
                    for k in range(TOPK):
                        i = t * TOPK + k
                        pool.indirect_dma_start(got[:, half, t, k], None, hidden_dram,
                                                bass.IndirectOffsetOnAxis(ap=place[:, half, i:i + 1], axis=0))\
                            .then_inc(s_got[half][t // 2], 16)

            each_group(pool, group)

        @block.vector
        def _(dve):
            def places_of(g, half, gg):
                cols = bass.ds(g * W, W)
                dve.tensor_copy(place[:, half], places[:, cols]).then_inc(s_place, 1)
                dve.tensor_copy(share[:, half], shares[:, cols]).then_inc(s_share, 1)

            def group(g, half, gg):
                dve.wait_ge(s_base[half], gg * 16 + 16)
                for two in range(2):
                    dve.wait_ge(s_got[half][two], gg * (32 * TOPK) + 32 * TOPK)
                    for k in range(TOPK):
                        for t in (2 * two, 2 * two + 1):
                            i = t * TOPK + k
                            ins = dve.scalar_tensor_tensor(acc[:, half, t], got[:, half, t, k], share[:, half, i:i + 1],
                                                           acc[:, half, t], ALU.mult, ALU.add)
                            ins.then_inc(s_sum if k == TOPK - 1 else s_link, 1)
                        if k < TOPK - 1:
                            dve.wait_ge(s_link, g * (GT * (TOPK - 1)) + two * (2 * (TOPK - 1)) + (k + 1) * 2)

            for half in range(2):
                places_of(half, half, 0)
            dve.wait_ge(s_share, 2)
            for half in range(2):
                group(half, half, 0)
                if GROUPS > 2:
                    dve.wait_ge(s_sum, (half + 1) * GT)
                    places_of(half + 2, half, 1)
                    dve.wait_ge(s_share, half + 3)
            if GROUPS > 4:
                with dve.Fori(1, GROUPS // 2 - 1) as gg:
                    for half in range(2):
                        g = gg * 2 + half
                        group(g, half, gg)
                        dve.wait_ge(s_sum, (g + 1) * GT)
                        places_of(g + 2, half, gg + 1)
                        dve.wait_ge(s_share, g + 3)
            if GROUPS > 2:
                for half in range(2):
                    group(GROUPS - 2 + half, half, GROUPS // 2 - 1)


_INS = ['L0_attn_x', 'L0_attn_Wq', 'L0_attn_Wkv', 'L0_attn_Wo', 'L0_ffn_gate_w', 'L0_ffn_expert_gate_up',
        'L0_ffn_expert_down', 'L0_ffn_shared_gate_up', 'L0_ffn_shared_down', 'L0_ffn_shared_gate_vec']


def layer(nc, x, w_q, w_kv, w_o, gate_w, gate_up, down, shared_gate_up, shared_down, shared_gate, rope, out):
    P = 128
    n_seq, seq, D = x.shape
    E, K, U = gate_w.shape[0], 4, 4
    waves = 2
    tokens = n_seq * seq // waves
    region = tokens + P
    slot_tiles = -(-(tokens * K // P + E) // U) * U
    spare = slot_tiles - tokens * K // P
    x1 = nc.dram_tensor("x1_scratch", [n_seq, seq, D], mybir.dt.float32).ap()
    base = nc.dram_tensor("base_scratch", [n_seq, seq, D], mybir.dt.float32).ap()
    rows = [nc.dram_tensor(f"rows_scratch{w}", [E * region + spare * P, 2 * D], mybir.dt.float16).ap()
            for w in range(waves)]
    hidden = [nc.dram_tensor(f"hidden_scratch{w}", [slot_tiles * P, D], mybir.dt.float32).ap() for w in range(waves)]
    with nc.sbuf_tensor("x1_moments", [P, waves * tokens // P, 2], mybir.dt.float32) as moments:
        attention_block(nc, x, w_q, w_kv, w_o, rope, x1, moments, n_seq)
        moe_blocks(nc, x1, moments, gate_w, gate_up, down, shared_gate_up, shared_down, shared_gate, rows, hidden, base,
                   out, n_seq)


def _rope_table(seq, width):
    import numpy as np

    one, base = np.float32(1.0), np.float32(10000.0)
    frequencies = one / base ** (np.arange(0, width, 2, dtype=np.float32) / np.float32(width))
    angles = np.arange(seq, dtype=np.float32)[:, None] * frequencies[None, :]
    cos, sin = np.cos(angles), np.sin(angles)
    table = np.stack([np.concatenate([cos, cos], -1), np.concatenate([sin, -sin], -1)], axis=1)
    return (table * np.float32(2.0 ** -8)).astype(np.float32)


def kernel(**inputs):
    import numpy as _np
    import concourse.bacc as _bacc
    from concourse import mybir as _mybir
    from concourse.bass_utils import run_bass_kernel_spmd as _run

    nc = _bacc.Bacc("TRN2", target_bir_lowering=False, num_devices=1)
    arrays, args = {}, []
    for name in _INS:
        a = _np.ascontiguousarray(inputs[name])
        arrays[f"in_{name}_dram"] = a
        args.append(nc.dram_tensor(f"in_{name}_dram", a.shape, _mybir.dt.from_np(a.dtype), kind="ExternalInput").ap())
    shape = tuple(inputs['L0_attn_x'].shape)
    table = _rope_table(shape[1], 64)
    arrays["in_rope_dram"] = table
    args.append(nc.dram_tensor("in_rope_dram", table.shape, _mybir.dt.float32, kind="ExternalInput").ap())
    args.append(nc.dram_tensor("out_0_dram", shape, _mybir.dt.float32, kind="ExternalOutput").ap())
    layer(nc, *args)
    r = _run(nc, [arrays], core_ids=[0])
    return r.results[0]["out_0_dram"]
```
